# Optimizing a Trainium2 kernel written in Bass

```python
import numpy as np
import jax
import jax.numpy as jnp

def _softmax(x, axis=-1):
    return jax.nn.softmax(x, axis=axis)

def _gelu(x):
    return jax.nn.gelu(x, approximate=True)

def _silu(x):
    return jax.nn.silu(x)

def _sigmoid(x):
    return jax.nn.sigmoid(x)

def _layernorm(x, axis=-1, eps=1e-05):
    m = jnp.mean(x, axis=axis, keepdims=True)
    v = jnp.var(x, axis=axis, keepdims=True)
    return (x - m) / jnp.sqrt(v + eps)

def _scatter_add(tgt, idx, src, axis=0):
    return tgt.at[idx].add(src)

def _segment_sum(src, seg, n):
    return jax.ops.segment_sum(src, seg, n)
kernel_name = 'mk_pixart_seq_d1_seqx_r2_af0890'

def setup_inputs(seed: int=0):
    np.random.seed(seed)
    _w = jnp.asarray

    def _rec_inputs():
        import jax
        import jax.numpy as jnp
        _rk = jax.random.key(seed)
        x = -0.0002928 + 1 * jax.random.normal(jax.random.fold_in(_rk, 1), (16, 100, 512), jnp.float32)
        _lenS = 100 - jax.random.randint(jax.random.fold_in(_rk, 7), (16,), 0, max(1, 100 // 4) + 1, jnp.int32)
        _lenS2 = 722 - jax.random.randint(jax.random.fold_in(_rk, 8), (16,), 0, max(1, 722 // 4) + 1, jnp.int32)
        cond_1024 = 0.0061147 + 1.02565 * jax.random.normal(jax.random.fold_in(_rk, 11), (16, 512), jnp.float32)
        _ctx_1024P = jax.random.normal(jax.random.fold_in(_rk, 12), (16, 16, 512), jnp.float32)
        _ctx_1024c = jax.random.dirichlet(jax.random.fold_in(_rk, 512), 0.3 * jnp.ones((16,), jnp.float32), (16, 722))
        _ctx_1024t = jnp.einsum('bsk,bkd->bsd', _ctx_1024c, _ctx_1024P)
        _ctx_1024t = _ctx_1024t * jax.lax.rsqrt(jnp.mean(jnp.square(_ctx_1024t)) + 1e-12) * 0.953939
        ctx_1024 = -0.00265004 + 0.998804 * (_ctx_1024t + 0.3 * jax.random.normal(jax.random.fold_in(_rk, 612), (16, 722, 512), jnp.float32))
        return (x, cond_1024, ctx_1024)
    x, cond_1024, ctx_1024 = _rec_inputs()

    def _L0_xcond_setup():
        import jax, jax.numpy as jnp
        import numpy as np
        LN_EPS = 1e-06

        def _ln(x):
            mu = jnp.mean(x, axis=-1, keepdims=True)
            var = jnp.var(x, axis=-1, keepdims=True)
            return (x - mu) * jax.lax.rsqrt(var + LN_EPS)
        key = jax.random.key(seed)
        H, NH = (512, 16)
        B, N, S = (4, 512, 77)
        MLP = int(H * 4.0)
        ks = jax.random.split(key, 20)
        s = 1.0 / np.sqrt(H)
        return {'x': jax.random.normal(ks[0], (B, N, H), jnp.float32), 'c': jax.random.normal(ks[1], (B, H), jnp.float32), 'context': jax.random.normal(ks[2], (B, S, H), jnp.float32), 'W_mod': jax.random.normal(ks[3], (H, 6 * H), jnp.float32) * s, 'b_mod': jnp.zeros((6 * H,), jnp.float32), 'W_qkv': jax.random.normal(ks[4], (H, 3 * H), jnp.float32) * s, 'b_qkv': jnp.zeros((3 * H,), jnp.float32), 'W_proj': jax.random.normal(ks[5], (H, H), jnp.float32) * s, 'b_proj': jnp.zeros((H,), jnp.float32), 'W_qc': jax.random.normal(ks[6], (H, H), jnp.float32) * s, 'b_qc': jnp.zeros((H,), jnp.float32), 'W_kvc': jax.random.normal(ks[7], (H, 2 * H), jnp.float32) * s, 'b_kvc': jnp.zeros((2 * H,), jnp.float32), 'W_cproj': jax.random.normal(ks[8], (H, H), jnp.float32) * s, 'b_cproj': jnp.zeros((H,), jnp.float32), 'W_mlp1': jax.random.normal(ks[9], (H, MLP), jnp.float32) * s, 'b_mlp1': jnp.zeros((MLP,), jnp.float32), 'W_mlp2': jax.random.normal(ks[10], (MLP, H), jnp.float32) * (1.0 / np.sqrt(MLP)), 'b_mlp2': jnp.zeros((H,), jnp.float32)}
    _L0_xcond_all = _L0_xcond_setup()
    _L0_xcond_in = {k: v for k, v in _L0_xcond_all.items() if k in ('W_mod', 'b_mod', 'W_qkv', 'b_qkv', 'W_proj', 'b_proj', 'W_qc', 'b_qc', 'W_kvc', 'b_kvc', 'W_cproj', 'b_cproj', 'W_mlp1', 'b_mlp1', 'W_mlp2', 'b_mlp2')}
    del _L0_xcond_all
    return {'x': x, 'cond_1024': cond_1024, 'ctx_1024': ctx_1024, 'L0_xcond_W_mod': _L0_xcond_in['W_mod'], 'L0_xcond_b_mod': _L0_xcond_in['b_mod'], 'L0_xcond_W_qkv': _L0_xcond_in['W_qkv'], 'L0_xcond_b_qkv': _L0_xcond_in['b_qkv'], 'L0_xcond_W_proj': _L0_xcond_in['W_proj'], 'L0_xcond_b_proj': _L0_xcond_in['b_proj'], 'L0_xcond_W_qc': _L0_xcond_in['W_qc'], 'L0_xcond_b_qc': _L0_xcond_in['b_qc'], 'L0_xcond_W_kvc': _L0_xcond_in['W_kvc'], 'L0_xcond_b_kvc': _L0_xcond_in['b_kvc'], 'L0_xcond_W_cproj': _L0_xcond_in['W_cproj'], 'L0_xcond_b_cproj': _L0_xcond_in['b_cproj'], 'L0_xcond_W_mlp1': _L0_xcond_in['W_mlp1'], 'L0_xcond_b_mlp1': _L0_xcond_in['b_mlp1'], 'L0_xcond_W_mlp2': _L0_xcond_in['W_mlp2'], 'L0_xcond_b_mlp2': _L0_xcond_in['b_mlp2']}

def reference(x, cond_1024, ctx_1024, L0_xcond_W_mod, L0_xcond_b_mod, L0_xcond_W_qkv, L0_xcond_b_qkv, L0_xcond_W_proj, L0_xcond_b_proj, L0_xcond_W_qc, L0_xcond_b_qc, L0_xcond_W_kvc, L0_xcond_b_kvc, L0_xcond_W_cproj, L0_xcond_b_cproj, L0_xcond_W_mlp1, L0_xcond_b_mlp1, L0_xcond_W_mlp2, L0_xcond_b_mlp2):
    import jax
    import jax.numpy as jnp

    def _L0_xcond_ref(x, c, context, W_mod, b_mod, W_qkv, b_qkv, W_proj, b_proj, W_qc, b_qc, W_kvc, b_kvc, W_cproj, b_cproj, W_mlp1, b_mlp1, W_mlp2, b_mlp2):
        import jax, jax.numpy as jnp
        import numpy as np
        LN_EPS = 1e-06

        def _ln(x):
            mu = jnp.mean(x, axis=-1, keepdims=True)
            var = jnp.var(x, axis=-1, keepdims=True)
            return (x - mu) * jax.lax.rsqrt(var + LN_EPS)
        B, N, H = x.shape
        NH = 16
        hd = H // NH
        scale = hd ** (-0.5)
        c_proj = jax.nn.silu(c) @ W_mod + b_mod
        shift_a, scale_a, gate_a, shift_m, scale_m, gate_m = jnp.split(c_proj, 6, axis=-1)

        def modulate(t, shift, sc):
            return t * (1 + sc[:, None]) + shift[:, None]
        x_norm = modulate(_ln(x), shift_a, scale_a)
        qkv = x_norm @ W_qkv + b_qkv
        q, k, v = jnp.split(qkv, 3, axis=-1)
        q = q.reshape(B, N, NH, hd).transpose(0, 2, 1, 3)
        k = k.reshape(B, N, NH, hd).transpose(0, 2, 1, 3)
        v = v.reshape(B, N, NH, hd).transpose(0, 2, 1, 3)
        attn_w = jax.nn.softmax(jnp.einsum('bhqd,bhkd->bhqk', q, k) * scale, axis=-1)
        attn_out = jnp.einsum('bhqk,bhkd->bhqd', attn_w, v)
        attn_out = attn_out.transpose(0, 2, 1, 3).reshape(B, N, H)
        attn_out = attn_out @ W_proj + b_proj
        x = x + gate_a[:, None] * attn_out
        S = context.shape[1]
        q_c = _ln(x) @ W_qc + b_qc
        kv_c = _ln(context) @ W_kvc + b_kvc
        k_c, v_c = jnp.split(kv_c, 2, axis=-1)
        q_c = q_c.reshape(B, N, NH, hd).transpose(0, 2, 1, 3)
        k_c = k_c.reshape(B, S, NH, hd).transpose(0, 2, 1, 3)
        v_c = v_c.reshape(B, S, NH, hd).transpose(0, 2, 1, 3)
        c_attn_w = jax.nn.softmax(jnp.einsum('bhqd,bhsd->bhqs', q_c, k_c) * scale, axis=-1)
        c_attn_out = jnp.einsum('bhqs,bhsd->bhqd', c_attn_w, v_c)
        c_attn_out = c_attn_out.transpose(0, 2, 1, 3).reshape(B, N, H)
        c_attn_out = c_attn_out @ W_cproj + b_cproj
        x = x + c_attn_out
        x_norm2 = modulate(_ln(x), shift_m, scale_m)
        h = jax.nn.gelu(x_norm2 @ W_mlp1 + b_mlp1)
        h = h @ W_mlp2 + b_mlp2
        x = x + gate_m[:, None] * h
        return x
    x = _L0_xcond_ref(x, cond_1024, ctx_1024, L0_xcond_W_mod, L0_xcond_b_mod, L0_xcond_W_qkv, L0_xcond_b_qkv, L0_xcond_W_proj, L0_xcond_b_proj, L0_xcond_W_qc, L0_xcond_b_qc, L0_xcond_W_kvc, L0_xcond_b_kvc, L0_xcond_W_cproj, L0_xcond_b_cproj, L0_xcond_W_mlp1, L0_xcond_b_mlp1, L0_xcond_W_mlp2, L0_xcond_b_mlp2)
    return x

_drawn_inputs = setup_inputs


def setup_inputs(seed=0):
    import zlib

    import numpy as np

    out = dict(_drawn_inputs(seed))
    spreads = {'L0_xcond_b_mod': (0.0, 0.1),
     'L0_xcond_b_qkv': (0.0, 0.1),
     'L0_xcond_b_proj': (0.0, 0.1),
     'L0_xcond_b_qc': (0.0, 0.572),
     'L0_xcond_b_kvc': (0.0, 0.1),
     'L0_xcond_b_cproj': (0.0, 0.1),
     'L0_xcond_b_mlp1': (0.0, 0.1),
     'L0_xcond_b_mlp2': (0.0, 0.1)}
    factors = {}
    for name, (base, spread) in spreads.items():
        noise = np.random.default_rng([zlib.crc32(name.encode()), seed]).standard_normal(out[name].shape)
        drawn = base * np.exp(spread * noise) if base else spread * noise
        out[name] = jnp.asarray(drawn.astype(out[name].dtype))
    for name, factor in factors.items():
        out[name] = (out[name] * factor).astype(out[name].dtype)
    return out
```

```python
from contextlib import ExitStack

import concourse.bass as bass
from concourse import mybir

F32 = mybir.dt.float32
F32R = mybir.dt.float32r
I32 = mybir.dt.int32
ALU = mybir.AluOpType
ACT = mybir.ActivationFunctionType
AX = mybir.AxisListType

P = 128
B, N, D = 16, 100, 512
S = 722
NH, HD = 16, 32
MLP = 4 * D
FC = D // P
MC = MLP // P
GROUP_BATCHES = 4
GROUPS = B // GROUP_BATCHES
GT = GROUP_BATCHES * N
SCALE = float(HD) ** -0.5

LN_EPS = 1e-6
RSQRT_SEED = 0x5F3759DF
NEWTON_ROUNDS = 3
SEED_STEPS = 3
NEWTON_STEPS = 1 + 4 * NEWTON_ROUNDS

BIAS_OF = {}
_at = 0
for _name, _n in (("mod", 24), ("qk", 8), ("v", 4), ("proj", 4), ("qc", 4), ("kc", 4), ("vc", 4),
                  ("cproj", 4), ("mlp1", 16), ("mlp2", 4)):
    BIAS_OF[_name] = slice(_at, _at + _n)
    _at += _n
BIAS_COLS = _at


def seed_rsqrt(dve, sem, base, mean_var, var_eps, half_bits, guess):
    dve.tensor_scalar(var_eps, mean_var[:, :, 1], LN_EPS, None, ALU.add).then_inc(sem, 1)
    dve.wait_ge(sem, base + 1)
    dve.tensor_scalar(half_bits, var_eps.bitcast(I32), 1, None, ALU.logical_shift_right).then_inc(sem, 1)
    dve.wait_ge(sem, base + 2)
    dve.tensor_scalar(guess.bitcast(I32), half_bits, -1.0, float(RSQRT_SEED), ALU.mult, ALU.add).then_inc(sem, 1)


def newton_rsqrt(pool, consts, sem, base, mean_var, var_eps, guess, work, neg_mean):
    def after(n):
        wait_apart(pool, consts, sem, base + n)

    pool.tensor_scalar(neg_mean, mean_var[:, :, 0], -1.0, None, ALU.mult).then_inc(sem, 1)
    for r in range(NEWTON_ROUNDS):
        after(4 * r + 1)
        pool.tensor_tensor(work, guess, guess, ALU.mult).then_inc(sem, 1)
        after(4 * r + 2)
        pool.tensor_tensor(work, work, var_eps, ALU.mult).then_inc(sem, 1)
        after(4 * r + 3)
        pool.tensor_scalar(work, work, -0.5, 1.5, ALU.mult, ALU.add).then_inc(sem, 1)
        after(4 * r + 4)
        pool.tensor_tensor(guess, guess, work, ALU.mult).then_inc(sem, 1)


def wait_apart(eng, consts, sem, value):
    if not isinstance(value, int):
        value = eng.snap(eng.to_reg(value))
    eng.wait_ge(consts, 48)
    eng.wait_ge(sem, value)


def product3(pe, out, lhs_hi, lhs_lo, rhs_hi, rhs_lo, chunks):
    for c in range(chunks):
        pe.matmul(out, lhs_hi(c), rhs_hi(c), start=(c == 0), stop=False)
        pe.matmul(out, lhs_hi(c), rhs_lo(c), start=False, stop=False)
        last = pe.matmul(out, lhs_lo(c), rhs_hi(c), start=False, stop=(c == chunks - 1))
    return last


class Shared:

    def __init__(self, nc, ctx):
        def sb(name, shape, dt=F32):
            return ctx.enter_context(nc.sbuf_tensor(name, shape, dt))

        self.bias = sb("bias", [P, BIAS_COLS])[:]
        self.ident = sb("identity", [P, P])[:]
        self.cond = sb("cond", [P, FC, B])[:]
        self.silu = sb("silu", [P, FC, B])[:]
        self.mod = sb("mod", [P, 24, B])[:]
        self.gate_bias = sb("gate_bias", [P, 8, B])[:]
        self.b_qc_scaled = sb("b_qc_scaled", [P, FC])[:]
        self.raw = sb("raw_weights", [P, 2, FC, 512])[:]
        self.consts = ctx.enter_context(nc.semaphore("consts"))
        self.kv_landed = [ctx.enter_context(nc.semaphore(f"kv_landed{i}")) for i in range(2)]

    def b(self, name, f):
        at = BIAS_OF[name].start + f
        return self.bias[:, at:at + 1]


def self_attention_stage(nc, sh, dram):
    GJ = GROUP_BATCHES
    UNITS = 2 * GJ
    chunks = [("mod", 0), ("mod", 1), ("qkv", 0), ("qkv", 1), ("qkv", 2), ("mod", 2), ("proj", 0), ("qc", 0)]
    with ExitStack() as ctx:
        def sb(name, shape, dt=F32):
            return ctx.enter_context(nc.sbuf_tensor(name, shape, dt))

        def sem(name):
            return ctx.enter_context(nc.semaphore(name))

        bank = ctx.enter_context(nc.psum_tensor("bank1", [P, 8, 512], F32))
        w_hi = {"qkv": sb("wqkv_hi", [P, FC, 3 * D], F32R), "proj": sb("wproj_hi", [P, FC, D], F32R),
                "qc": sb("wqc_hi", [P, FC, D], F32R)}
        w_lo = {"qkv": sb("wqkv_lo", [P, FC, 3 * D], F32R), "proj": sb("wproj_lo", [P, FC, D], F32R),
                "qc": sb("wqc_lo", [P, FC, D], F32R)}
        x_tok = sb("x_tok", [N, GJ, D])
        stats = sb("stats", [N, GJ, 6])
        mean_var = sb("mean_var", [N, GJ, 2])
        var_eps = sb("var_eps", [N, GJ])
        half_bits = sb("half_bits", [N, GJ], I32)
        rstd = sb("rstd", [N, GJ])
        newton_work = sb("newton_work", [N, GJ])
        neg_mean = sb("neg_mean", [N, GJ])
        gp = sb("gp", [P, 16, GJ])
        xm = sb("xm", [P, FC, GT])
        x_hi = sb("x_hi", [P, FC, GT], F32R)
        x_lo = sb("x_lo", [P, FC, GT], F32R)
        qk = sb("qk", [P, 2 * FC, GT])
        v = sb("v", [N, GJ, NH, HD + 1])
        prob = [sb(f"prob{i}", [N, 8, N]) for i in range(2)]
        prob_t = [sb(f"prob_t{i}", [N, 2, 4 * N]) for i in range(2)]
        top = sb("top", [N, 2, 8])
        recip = sb("recip", [N, 2, 8])
        att = [sb(f"att{i}", [N, D]) for i in range(2)]
        att_t = sb("att_t", [P, FC, N])
        a_hi = sb("a_hi", [P, FC, GT], F32R)
        a_lo = sb("a_lo", [P, FC, GT], F32R)
        xt = sb("xt", [P, FC, GT])
        gated = [sb(f"gated{i}", [P, GT]) for i in range(2)]
        xn = [sb(f"xn{i}", [N, D]) for i in range(2)]
        q32 = [sb(f"q32_{i}", [P, GT]) for i in range(2)]

        raw_landed = [sem(f"raw_landed{i}") for i in range(2)]
        w_hi_done, w_lo_done = sem("w_hi_done"), sem("w_lo_done")
        silu_done, mod_mm, mod_added, mod_one, gate_bias = (
            sem(n) for n in ("silu_done", "mod_mm", "mod_added", "mod_one", "gate_bias"))
        x_landed, xt_landed, x1_stored, q_stored = (sem(n) for n in ("x_landed", "xt_landed", "x1_stored", "q_stored"))
        ones_set, gp_ready = sem("ones_set"), sem("gp_ready")
        st_a, mv_a, seed_a, newton_a, ln_a = (sem(n) for n in ("st_a", "mv_a", "seed_a", "newton_a", "ln_a"))
        st_b, mv_b, seed_b, newton_b, ln_b = (sem(n) for n in ("st_b", "mv_b", "seed_b", "newton_b", "ln_b"))
        x_turned, xm_ready, x_split = sem("x_turned"), sem("xm_ready"), sem("x_split")
        v_mm, v_copied, qk_mm, qk_copied = (sem(n) for n in ("v_mm", "v_copied", "qk_mm", "qk_copied"))
        s_mm, top_done, sub_done, exp_done = (sem(n) for n in ("s_mm", "top_done", "sub_done", "exp_done"))
        p_turned, p_copied, pv_mm, recip_done, att_ready = (
            sem(n) for n in ("p_turned", "p_copied", "pv_mm", "recip_done", "att_ready"))
        att_turned, att_split = sem("att_turned"), sem("att_split")
        proj_mm, gated_done, x1_ready = sem("proj_mm"), sem("gated_done"), sem("x1_ready")
        x1_turned, xn_back, xn_hi, xn_lo = (sem(n) for n in ("x1_turned", "xn_back", "xn_hi", "xn_lo"))
        q_mm, q32_done, q_split = sem("q_mm"), sem("q32_done"), sem("q_split")

        def chunk_freed(eng, k):
            kinds = [c[0] == "mod" for c in chunks[:k + 1]]
            if kinds[k]:
                eng.wait_ge(mod_mm, sum(kinds))
            else:
                eng.wait_ge(w_lo_done, k + 1 - sum(kinds))

        def unit_bank(u):
            return 2 * (u % 2)

        block = ctx.enter_context(nc.Block())

        @block.sync
        def _(sp):
            sp.dma_start(sh.bias, dram["bias_cols"]).then_inc(sh.consts, 16)
            sp.dma_start(sh.ident, dram["ident"]).then_inc(sh.consts, 16)
            sp.dma_start(sh.cond, dram["cond_t"]).then_inc(sh.consts, 16)
            for k, (kind, q) in enumerate(chunks):
                if k >= 2:
                    chunk_freed(sp, k - 2)
                sp.dma_start(sh.raw[:, k % 2], dram["w_" + kind][:, :, q * 512:(q + 1) * 512]).then_inc(raw_landed[k % 2], 16)
            for q in range(2):
                chunk_freed(sp, len(chunks) - 2 + q)
                sp.dma_start(sh.raw[:, q], dram["w_kvc"][:, :, q * 512:(q + 1) * 512]).then_inc(sh.kv_landed[q], 16)
            with sp.Fori(0, GROUPS) as g:
                wait_apart(sp, sh.consts, x1_stored, 16 * g)
                sp.wait_ge(x1_turned, GJ * g)
                sp.dma_start(xt[:], dram["x_t"][:, :, bass.ds(g * GT, GT)]).then_inc(xt_landed, 16)
                sp.wait_ge(x1_ready, FC * g + FC)
                sp.dma_start(dram["x1"][:, :, bass.ds(g * GT, GT)], xt[:]).then_inc(x1_stored, 16)
                sp.wait_ge(q_split, 2 * FC * g + 2 * FC)
                sp.dma_start(dram["q_hi"].rearrange("(f p) t -> p f t", p=P)[:, :, bass.ds(g * GT, GT)],
                             x_hi[:].bitcast(F32)).then_inc(q_stored, 16)
                sp.dma_start(dram["q_lo"].rearrange("(f p) t -> p f t", p=P)[:, :, bass.ds(g * GT, GT)],
                             x_lo[:].bitcast(F32)).then_inc(q_stored, 16)
            sp.wait_ge(x1_stored, 16 * GROUPS)
            sp.wait_ge(q_stored, 32 * GROUPS)

        @block.tensor
        def _(pe):
            pe.wait_ge(silu_done, 1)
            m = 0
            for k, (kind, q) in enumerate(chunks):
                if kind != "mod":
                    continue
                pe.wait_ge(raw_landed[k % 2], 16 * (k // 2 + 1))
                if m >= 2:
                    pe.wait_ge(mod_added, m - 1)
                for f in range(4):
                    for c in range(FC):
                        last = pe.matmul(bank[:, m % 2, f * B:(f + 1) * B], sh.raw[:, k % 2, c, f * P:(f + 1) * P],
                                         sh.silu[:, c, :], start=(c == 0), stop=(c == FC - 1))
                last.then_inc(mod_mm, 1)
                m += 1
            pe.wait_ge(w_lo_done, 5)
            pe.wait_ge(mod_added, m)

            with pe.Fori(0, GROUPS) as g:
                for j in range(GJ):
                    pe.wait_ge(ln_a, GJ * g + j + 1)
                    if j < 2:
                        pe.wait_ge(xn_lo, GJ * g)
                    else:
                        pe.wait_ge(xm_ready, GJ * g + j - 1)
                    for f in range(FC):
                        last = pe.transpose(bank[:, 4 + j % 2, f * N:(f + 1) * N], x_tok[:, j, f * P:(f + 1) * P],
                                            sh.ident[0:N, 0:N])
                    last.then_inc(x_turned, 1)
                for j in range(GJ):
                    if j == 0:
                        pe.wait_ge(q32_done, FC * g)
                    pe.wait_ge(x_split, 2 * GJ * g + 2 * j + 2)
                    product3(pe, bank[0:N, j, :],
                             lambda c: x_hi[:, c, j * N:(j + 1) * N], lambda c: x_lo[:, c, j * N:(j + 1) * N],
                             lambda c: w_hi["qkv"][:, c, 2 * D:3 * D], lambda c: w_lo["qkv"][:, c, 2 * D:3 * D],
                             FC).then_inc(v_mm, 1)
                for f in range(2 * FC):
                    if f < FC:
                        pe.wait_ge(v_copied, GJ * g + f + 1)
                    else:
                        pe.wait_ge(qk_copied, 2 * FC * g + f - 3)
                    product3(pe, bank[:, f % 4, 0:GT],
                             lambda c: w_hi["qkv"][:, c, f * P:(f + 1) * P], lambda c: w_lo["qkv"][:, c, f * P:(f + 1) * P],
                             lambda c: x_hi[:, c, :], lambda c: x_lo[:, c, :], FC).then_inc(qk_mm, 1)

                def scores(u):
                    if u < 2:
                        pe.wait_ge(qk_copied, 2 * FC * g + 2 * FC)
                    else:
                        pe.wait_ge(sub_done, UNITS * g + u - 1)
                    j = u // 2
                    for h in range(8):
                        f, r = h % 4, 32 * (unit_bank(u) + h // 4)
                        last = pe.matmul(bank[0:N, unit_bank(u) + h // 4, f * N:(f + 1) * N],
                                         qk[r:r + 32, f, j * N:(j + 1) * N], qk[r:r + 32, FC + f, j * N:(j + 1) * N],
                                         start=True, stop=True)
                    last.then_inc(s_mm, 1)

                def turn_probs(u):
                    pe.wait_ge(exp_done, UNITS * g + u + 1)
                    if u == 0:
                        pe.wait_ge(xm_ready, GJ * g + GJ)
                    else:
                        pe.wait_ge(p_copied, UNITS * g + u)
                    for h in range(8):
                        last = pe.transpose(bank[0:N, 4 + h // 4, (h % 4) * N:(h % 4 + 1) * N], prob[u % 2][:, h, :],
                                            sh.ident[0:N, 0:N])
                    last.then_inc(p_turned, 1)

                def weigh(u):
                    pe.wait_ge(p_copied, UNITS * g + u + 1)
                    pe.wait_ge(att_ready, UNITS * g + u)
                    j = u // 2
                    for h in range(8):
                        last = pe.matmul(bank[0:N, 6, h * (HD + 1):(h + 1) * (HD + 1)],
                                         prob_t[u % 2][:, h // 4, (h % 4) * N:(h % 4 + 1) * N],
                                         v[:, j, 4 * (h % 4) + unit_bank(u) + h // 4, :], start=True, stop=True)
                    last.then_inc(pv_mm, 1)

                def turn_att(j):
                    pe.wait_ge(att_ready, UNITS * g + 2 * j + 2)
                    pe.wait_ge(att_split, 3 * GJ * g + 3 * j)
                    for f in range(FC):
                        last = pe.transpose(bank[:, 7, f * N:(f + 1) * N], att[j % 2][:, f * P:(f + 1) * P],
                                            sh.ident[0:N, 0:N])
                    last.then_inc(att_turned, 1)

                scores(0)
                pe.wait_ge(ones_set, 1)
                for u in range(UNITS):
                    if u + 1 < UNITS:
                        scores(u + 1)
                    if u >= 1:
                        weigh(u - 1)
                    turn_probs(u)
                    if u >= 3 and u % 2:
                        turn_att((u - 3) // 2)
                weigh(UNITS - 1)
                turn_att(GJ - 1)
                for f in range(FC):
                    if f == 0:
                        pe.wait_ge(att_split, 3 * GJ * g + 3 * GJ)
                        pe.wait_ge(sub_done, UNITS * g + UNITS)
                    product3(pe, bank[:, f, 0:GT],
                             lambda c: w_hi["proj"][:, c, f * P:(f + 1) * P], lambda c: w_lo["proj"][:, c, f * P:(f + 1) * P],
                             lambda c: a_hi[:, c, :], lambda c: a_lo[:, c, :], FC).then_inc(proj_mm, 1)
                for j in range(GJ):
                    if j == 0:
                        pe.wait_ge(x1_ready, FC * g + FC)
                        pe.wait_ge(gated_done, FC * g + FC)
                    for f in range(FC):
                        last = pe.transpose(bank[0:N, j, f * P:(f + 1) * P], xt[:, f, j * N:(j + 1) * N], sh.ident[:])
                    last.then_inc(x1_turned, 1)
                for j in range(GJ):
                    pe.wait_ge(ln_b, GJ * g + j + 1)
                    if j < 2:
                        pe.wait_ge(p_copied, UNITS * g + UNITS)
                    else:
                        pe.wait_ge(xn_lo, GJ * g + j - 1)
                    for f in range(FC):
                        last = pe.transpose(bank[:, 4 + j % 2, f * N:(f + 1) * N], xn[j % 2][:, f * P:(f + 1) * P],
                                            sh.ident[0:N, 0:N])
                    last.then_inc(xn_back, 1)
                for f in range(FC):
                    if f == 0:
                        pe.wait_ge(xn_lo, GJ * g + GJ)
                    product3(pe, bank[:, f, 0:GT],
                             lambda c: w_hi["qc"][:, c, f * P:(f + 1) * P], lambda c: w_lo["qc"][:, c, f * P:(f + 1) * P],
                             lambda c: a_hi[:, c, :], lambda c: a_lo[:, c, :], FC).then_inc(q_mm, 1)

        @block.scalar
        def _(act):
            act.wait_ge(sh.consts, 48)
            act.activation(sh.silu, sh.cond, ACT.Silu).then_inc(silu_done, 1)
            w = 0
            for k, (kind, q) in enumerate(chunks):
                if kind == "mod":
                    continue
                act.wait_ge(raw_landed[k % 2], 16 * (k // 2 + 1))
                act.activation(w_hi[kind][:, :, q * 512:(q + 1) * 512], sh.raw[:, k % 2], ACT.Copy).then_inc(w_hi_done, 1)
            act.wait_ge(gate_bias, 2)
            with act.Fori(0, GROUPS) as g:
                for j in range(GJ):
                    act.wait_ge(x_turned, GJ * g + j + 1)
                    if j == 0:
                        act.wait_ge(gp_ready, 2 * g + 2)
                        act.wait_ge(x_split, 2 * GJ * g)
                    for f in range(FC):
                        last = act.activation(xm[:, f, j * N:(j + 1) * N], bank[:, 4 + j % 2, f * N:(f + 1) * N],
                                              ACT.Identity, bias=gp[:, f, j:j + 1], scale=gp[:, 4 + f, j:j + 1])
                    last.then_inc(xm_ready, 1)
                for f in range(2 * FC):
                    act.wait_ge(qk_mm, 2 * FC * g + f + 1)
                    if f == 0:
                        act.wait_ge(s_mm, UNITS * g)
                    act.activation(qk[:, f, :], bank[:, f % 4, 0:GT], ACT.Identity,
                                   bias=sh.b("qk", f)).then_inc(qk_copied, 1)

                def copy_probs(u):
                    act.wait_ge(p_turned, UNITS * g + u + 1)
                    act.wait_ge(pv_mm, UNITS * g + (u - 1 if u >= 2 else 0))
                    act.activation(prob_t[u % 2][:], bank[0:N, 4:6, 0:4 * N], ACT.Copy).then_inc(p_copied, 1)

                for u in range(UNITS):
                    act.wait_ge(sub_done, UNITS * g + u + 1)
                    act.activation(prob[u % 2][:], prob[u % 2][:], ACT.Exp, scale=SCALE).then_inc(exp_done, 1)
                    if u >= 1:
                        copy_probs(u - 1)
                copy_probs(UNITS - 1)
                for f in range(FC):
                    act.wait_ge(proj_mm, FC * g + f + 1)
                    act.wait_ge(x1_ready, FC * g + (f - 1 if f >= 2 else 0))
                    for j in range(GJ):
                        last = act.activation(gated[f % 2][:, j * N:(j + 1) * N], bank[:, f, j * N:(j + 1) * N],
                                              ACT.Identity, bias=gp[:, 12 + f, j:j + 1], scale=gp[:, 8 + f, j:j + 1])
                    last.then_inc(gated_done, 1)
                for j in range(GJ):
                    act.wait_ge(xn_back, GJ * g + j + 1)
                    act.activation(a_hi[:, :, j * N:(j + 1) * N],
                                   bank[:, 4 + j % 2, 0:GT].rearrange("p (f t) -> p f t", f=FC), ACT.Copy).then_inc(xn_hi, 1)
                for f in range(FC):
                    act.wait_ge(q_mm, FC * g + f + 1)
                    act.wait_ge(q_split, 2 * FC * g + (2 * f - 2 if f >= 2 else 0))
                    act.activation(q32[f % 2][:], bank[:, f, 0:GT], ACT.Identity, bias=sh.b_qc_scaled[:, f:f + 1],
                                   scale=SCALE).then_inc(q32_done, 1)

        @block.vector
        def _(dve):
            dve.wait_ge(sh.consts, 48)
            dve.tensor_scalar(sh.b_qc_scaled, sh.bias[:, BIAS_OF["qc"]], SCALE, None, ALU.mult).then_inc(gate_bias, 1)
            m = w = 0
            for k, (kind, q) in enumerate(chunks):
                if kind == "mod":
                    dve.wait_ge(mod_mm, m + 1)
                    dve.tensor_tensor(sh.mod[:, 4 * q:4 * q + 4, :], bank[:, m % 2, 0:4 * B].rearrange("p (f b) -> p f b", f=4),
                                      sh.bias[:, 4 * q:4 * q + 4].unsqueeze(2).to_broadcast([P, 4, B]),
                                      ALU.add).then_inc(mod_added, 1)
                    m += 1
                else:
                    dve.wait_ge(w_hi_done, w + 1)
                    sl = slice(q * 512, (q + 1) * 512)
                    dve.tensor_tensor(w_lo[kind][:, :, sl], sh.raw[:, k % 2], w_hi[kind][:, :, sl].bitcast(F32),
                                      ALU.subtract).then_inc(w_lo_done, 1)
                    w += 1
            dve.wait_ge(mod_added, 3)
            dve.tensor_scalar(sh.mod[:, 4:8, :], sh.mod[:, 4:8, :], 1.0, None, ALU.add).then_inc(mod_one, 1)
            dve.tensor_tensor(sh.gate_bias[:, 0:4, :], sh.mod[:, 8:12, :],
                              sh.bias[:, BIAS_OF["proj"]].unsqueeze(2).to_broadcast([P, 4, B]),
                              ALU.mult).then_inc(gate_bias, 1)

            with dve.Fori(0, GROUPS) as g:
                for j in range(GJ):
                    dve.wait_ge(x_landed, 16 * g + 16)
                    dve.bn_stats(stats[:, j, :], x_tok[:, j, :]).then_inc(st_a, 1)
                wait_apart(dve, sh.consts, st_a, GJ * g + GJ)
                for j in range(GJ):
                    dve.bn_aggr(mean_var[:, j, :], stats[:, j, :]).then_inc(mv_a, 1)
                dve.wait_ge(mv_a, GJ * g + GJ)
                seed_rsqrt(dve, seed_a, SEED_STEPS * g, mean_var[:], var_eps[:], half_bits[:], rstd[:])
                dve.wait_ge(newton_a, NEWTON_STEPS * g + NEWTON_STEPS)
                for j in range(GJ):
                    dve.tensor_scalar(x_tok[:, j, :], x_tok[:, j, :], mean_var[:, j, 0:1], rstd[:, j:j + 1],
                                      ALU.subtract, ALU.mult).then_inc(ln_a, 1)
                for j in range(GJ):
                    sl = slice(j * N, (j + 1) * N)
                    dve.wait_ge(xm_ready, GJ * g + j + 1)
                    if j == 0:
                        dve.wait_ge(q_stored, 32 * g)
                    dve.tensor_copy(x_hi[:, :, sl], xm[:, :, sl]).then_inc(x_split, 1)
                    dve.wait_ge(x_split, 2 * GJ * g + 2 * j + 1)
                    dve.tensor_tensor(x_lo[:, :, sl], xm[:, :, sl], x_hi[:, :, sl].bitcast(F32),
                                      ALU.subtract).then_inc(x_split, 1)
                for j in range(GJ):
                    dve.wait_ge(v_mm, GJ * g + j + 1)
                    dve.tensor_copy(v[:, j, :, 0:HD], bank[0:N, j, :].rearrange("p (h d) -> p h d", h=NH)).then_inc(v_copied, 1)

                def soften(u):
                    s = bank[0:N, unit_bank(u):unit_bank(u) + 2, 0:4 * N].rearrange("p b (h k) -> p b h k", h=4)
                    dve.wait_ge(s_mm, UNITS * g + u + 1)
                    dve.tensor_reduce(top[:, u % 2, :].rearrange("p (b h) -> p b h", b=2), s, AX.X, ALU.max).then_inc(top_done, 1)
                    dve.wait_ge(top_done, UNITS * g + u + 1)
                    dve.wait_ge(p_turned, UNITS * g + (u - 1 if u >= 2 else 0))
                    dve.tensor_tensor(prob[u % 2][:].rearrange("p (b h) k -> p b h k", b=2), s,
                                      top[:, u % 2, :].rearrange("p (b h) -> p b h", b=2).unsqueeze(3).to_broadcast([N, 2, 4, N]),
                                      ALU.subtract).then_inc(sub_done, 1)

                def normalise(u):
                    o = bank[0:N, 6, 0:8 * (HD + 1)].rearrange("p (h d) -> p h d", h=8)
                    heads = att[(u // 2) % 2][:].rearrange("p (f q r d) -> p q r f d", f=4, q=2, r=2)[:, u % 2]
                    j = u // 2
                    dve.wait_ge(pv_mm, UNITS * g + u + 1)
                    dve.reciprocal(recip[:, u % 2, :], o[:, :, HD]).then_inc(recip_done, 1)
                    dve.wait_ge(recip_done, UNITS * g + u + 1)
                    dve.wait_ge(att_turned, GJ * g + (j - 1 if j >= 2 else 0))
                    dve.tensor_tensor(heads, o[:, :, 0:HD].rearrange("p (r f) d -> p r f d", r=2),
                                      recip[:, u % 2, :].rearrange("p (r f) -> p r f", r=2).unsqueeze(3).to_broadcast([N, 2, 4, HD]),
                                      ALU.mult).then_inc(att_ready, 1)

                def split_att(j):
                    sl = slice(j * N, (j + 1) * N)
                    dve.wait_ge(att_turned, GJ * g + j + 1)
                    dve.tensor_tensor(att_t[:], bank[:, 7, 0:GT].rearrange("p (f t) -> p f t", f=FC),
                                      sh.bias[:, BIAS_OF["v"]].unsqueeze(2).to_broadcast([P, FC, N]), ALU.add).then_inc(att_split, 1)
                    dve.wait_ge(att_split, 3 * GJ * g + 3 * j + 1)
                    if j == 0:
                        dve.wait_ge(q_mm, FC * g)
                    dve.tensor_copy(a_hi[:, :, sl], att_t[:]).then_inc(att_split, 1)
                    dve.wait_ge(att_split, 3 * GJ * g + 3 * j + 2)
                    dve.tensor_tensor(a_lo[:, :, sl], att_t[:], a_hi[:, :, sl].bitcast(F32), ALU.subtract).then_inc(att_split, 1)

                for u in range(UNITS):
                    soften(u)
                    if u >= 2:
                        normalise(u - 2)
                    if u >= 4 and u % 2 == 0:
                        split_att((u - 4) // 2)
                normalise(UNITS - 2)
                split_att(GJ - 2)
                normalise(UNITS - 1)
                split_att(GJ - 1)
                for f in range(FC):
                    dve.wait_ge(gated_done, FC * g + f + 1)
                    if f == 0:
                        dve.wait_ge(xt_landed, 16 * g + 16)
                    dve.tensor_tensor(xt[:, f, :], xt[:, f, :], gated[f % 2][:], ALU.add).then_inc(x1_ready, 1)
                for j in range(GJ):
                    dve.wait_ge(x1_turned, GJ * g + j + 1)
                    dve.bn_stats(stats[:, j, :], bank[0:N, j, :]).then_inc(st_b, 1)
                wait_apart(dve, sh.consts, st_b, GJ * g + GJ)
                for j in range(GJ):
                    dve.bn_aggr(mean_var[:, j, :], stats[:, j, :]).then_inc(mv_b, 1)
                dve.wait_ge(mv_b, GJ * g + GJ)
                seed_rsqrt(dve, seed_b, SEED_STEPS * g, mean_var[:], var_eps[:], half_bits[:], rstd[:])
                dve.wait_ge(newton_b, NEWTON_STEPS * g + NEWTON_STEPS)

                def lo_back(j):
                    sl = slice(j * N, (j + 1) * N)
                    dve.wait_ge(xn_hi, GJ * g + j + 1)
                    dve.tensor_tensor(a_lo[:, :, sl], bank[:, 4 + j % 2, 0:GT].rearrange("p (f t) -> p f t", f=FC),
                                      a_hi[:, :, sl].bitcast(F32), ALU.subtract).then_inc(xn_lo, 1)

                for j in range(GJ):
                    if j >= 2:
                        dve.wait_ge(xn_back, GJ * g + j - 1)
                    dve.tensor_scalar(xn[j % 2][:], bank[0:N, j, :], mean_var[:, j, 0:1], rstd[:, j:j + 1],
                                      ALU.subtract, ALU.mult).then_inc(ln_b, 1)
                    if j >= 1:
                        lo_back(j - 1)
                lo_back(GJ - 1)
                for f in range(FC):
                    dve.wait_ge(q32_done, FC * g + f + 1)
                    dve.tensor_copy(x_hi[:, f, :], q32[f % 2][:]).then_inc(q_split, 1)
                    dve.wait_ge(q_split, 2 * FC * g + 2 * f + 1)
                    dve.tensor_tensor(x_lo[:, f, :], q32[f % 2][:], x_hi[:, f, :].bitcast(F32), ALU.subtract).then_inc(q_split, 1)

        @block.gpsimd
        def _(pool):
            pool.memset(v[:, :, :, HD:HD + 1], 1.0).then_inc(ones_set, 1)
            pool.wait_ge(sh.consts, 48)
            pool.wait_ge(mod_one, 1)
            pool.wait_ge(gate_bias, 2)
            with pool.Fori(0, GROUPS) as g:
                pool.wait_ge(ln_a, GJ * g)
                pool.dma_start(x_tok[:], dram["x_tok"][:, bass.ds(g * GJ, GJ), :]).then_inc(x_landed, 16)
                wait_apart(pool, sh.consts, gated_done, FC * g)
                pool.tensor_copy(gp[:, 0:12, :], sh.mod[:, 0:12, bass.ds(g * GJ, GJ)]).then_inc(gp_ready, 1)
                pool.tensor_copy(gp[:, 12:16, :], sh.gate_bias[:, 0:4, bass.ds(g * GJ, GJ)]).then_inc(gp_ready, 1)
                wait_apart(pool, sh.consts, seed_a, SEED_STEPS * g + SEED_STEPS)
                newton_rsqrt(pool, sh.consts, newton_a, NEWTON_STEPS * g, mean_var[:], var_eps[:], rstd[:], newton_work[:], neg_mean[:])
                wait_apart(pool, sh.consts, seed_b, SEED_STEPS * g + SEED_STEPS)
                newton_rsqrt(pool, sh.consts, newton_b, NEWTON_STEPS * g, mean_var[:], var_eps[:], rstd[:], newton_work[:], neg_mean[:])


def cross_attention_stage(nc, sh, dram):
    TILES = [(t * P, min(P, S - t * P)) for t in range((S + P - 1) // P)]
    CT = len(TILES)
    HALF = S // 2
    LN_SLOT = 7
    WIDE = HALF + 1
    V_UNITS = [(t, c) for t in range(CT) for c in range(FC)]
    V_SLOTS = [4, 5, 6, 7, 12, 13, 14, 15]
    V_SHARE = len(V_UNITS) // len(V_SLOTS)
    SLOTS = {0: ["K2a"], 1: ["K2b"], 2: ["K3a"], 3: ["T0", "K3b"], 8: ["T5", "K0a"], 9: ["K0b"], 10: ["K1a"], 11: ["K1b"]}
    for _i, _s in enumerate(V_SLOTS):
        SLOTS[_s] = [f"T{_s - 3}"] if _s < 8 else []
        SLOTS[_s] += [f"V{t}{c}" for t, c in V_UNITS[_i * V_SHARE:(_i + 1) * V_SHARE]]
    ENDS = {s: [x[:2] if x[0] == "V" else x for x in work if x[0] != "V" or int(x[2]) == FC - 1]
            for s, work in SLOTS.items()}
    ORDER = [x for s in range(NH) for x in ENDS[s]]
    OWN = ["K2a", "K2b", "K3a", "K3b"]
    SPLIT = [x for x in ORDER if x[0] != "V"]
    VS = [x for x in ORDER if x[0] == "V"]
    BIG = [x for x in ORDER if x[0] != "T"]

    def done(seq, b, x):
        at = seq.index(x)
        if isinstance(b, int) and b < 0:
            return len([y for y in seq[:at + 1] if y not in OWN])
        if isinstance(b, int) and b == B - 1:
            return len(seq) * B - len(OWN) + len([y for y in seq[:at + 1] if y in OWN])
        return len(seq) * (b + 1) - len(OWN) + at + 1

    def pieces_done(b, x):
        return done(ORDER, b, x)

    def splits_done(b, x):
        return done(SPLIT, b, x)

    def vs_done(b, x):
        return len(VS) * (b + 1) + VS.index(x) + 1

    with ExitStack() as ctx:
        def sb(name, shape, dt=F32):
            return ctx.enter_context(nc.sbuf_tensor(name, shape, dt))

        def sem(name):
            return ctx.enter_context(nc.semaphore(name))

        bank = ctx.enter_context(nc.psum_tensor("bank2", [P, 8, 512], F32))
        PROBS_T, PIECES, OUT, TURNED = 2, 4, 6, 7
        wkv_hi = sb("wkv_hi", [P, FC, 2 * D], F32R)
        wkv_lo = sb("wkv_lo", [P, FC, 2 * D], F32R)
        c_raw = sb("c_raw", [P, CT, D])
        c_norm = sb("c_norm", [P, CT, D])
        c_hi = sb("c_hi", [P, FC, S], F32R)
        c_lo = sb("c_lo", [P, FC, S], F32R)
        stats = sb("stats2", [P, CT, 6])
        mean_var = sb("mean_var2", [P, CT, 2])
        var_eps = sb("var_eps2", [P, CT])
        half_bits = sb("half_bits2", [P, CT], I32)
        rstd = sb("rstd2", [P, CT])
        newton_work = sb("newton_work2", [P, CT])
        neg_mean = sb("neg_mean2", [P, CT])
        k_hi = sb("k_hi", [P, 2, S], F32R)
        k_lo = sb("k_lo", [P, 2, S], F32R)
        k_stack = sb("k_stack", [3 * HD, NH, S + 1], F32R)
        q_stack = sb("q_stack", [3 * HD, NH, N], F32R)
        v_next = sb("v_next", [P, CT, D])
        v_now = sb("v_now", [P, CT, D])
        neg_top = sb("neg_top", [N, NH])
        total = sb("total", [N, NH])
        recip = sb("recip2", [N, NH])
        prob = [sb(f"prob2_{i}", [N, S]) for i in range(2)]
        prob_t = [sb(f"prob_t2_{i}", [P, CT, N]) for i in range(4)]
        out_t = sb("out_t", [P, FC, N])
        att = sb("att2", [N, D])

        w_hi_done, w_lo_done, cleared = sem("w_hi_done2"), sem("w_lo_done2"), sem("cleared")
        ctx_landed = [sem(f"ctx_landed{t}") for t in range(CT)]
        k_landed = [sem(f"k_landed{f}") for f in range(FC)]
        q_landed = [sem(f"q_landed{i}") for i in range(2)]
        att_stored = sem("att_stored")
        st_done, mv_done, seed_done, newton_done, ctx_normed = (
            sem(n) for n in ("st_done", "mv_done", "seed_done", "newton_done", "ctx_normed"))
        piece_mm, hi_done, lo_done, v_copied = (sem(n) for n in ("piece_mm", "hi_done", "lo_done", "v_copied2"))
        v_moved = [sem(f"v_moved{i}") for i in range(2)]
        s_mm, top_done, exp_done, p_turned, p_copied_dve, p_copied_act, pv_mm = (
            sem(n) for n in ("s_mm2", "top_done2", "exp_done2", "p_turned2", "p_copied_dve", "p_copied_act", "pv_mm2"))
        recip_done, out_taken, out_turned, att_ready = (
            sem(n) for n in ("recip_done2", "out_taken", "out_turned", "att_ready2"))
        mod_landed = [sem(f"mod_landed{i}") for i in range(2)]
        mod_mm, mod_added = sem("mod_mm2"), sem("mod_added2")

        def steps(eng, step, modulation=None):
            step(-1)
            if modulation:
                modulation()
            step(0)
            with eng.Fori(1, B - 2) as b:
                step(b)
            step(B - 2, last_ln=True)
            step(B - 1, last_ln=True, last=True)

        def own(b, last, x):
            if x in OWN:
                return not is_first(b)
            return not last

        def big_before(b, s, last):
            if s > 0:
                return [(b, x) for x in ENDS[s - 1] if x[0] != "T" and own(b, last, x)]
            return [] if is_first(b) else [(b - 1, x) for x in ENDS[NH - 1]]

        def turned_now(b, s, last):
            return [x for x in ENDS[s] if x[0] == "T" and own(b, last, x)]

        def is_first(b):
            return isinstance(b, int) and b < 0

        def is_int(b, n):
            return isinstance(b, int) and b == n

        def piece_bank(x):
            return TURNED if x[0] == "T" else PIECES + BIG.index(x) % 2

        block = ctx.enter_context(nc.Block())

        @block.sync
        def _(sp):
            def load_ctx(m, t):
                at, n = TILES[t]
                sp.dma_start(c_raw[0:n, t, :], dram["ctx"][bass.ds(m, 1), at:at + n, :].rearrange("b s d -> (b s) d")
                             ).then_inc(ctx_landed[t], 16)

            def load_q(b, half):
                hs = slice(8 * half, 8 * half + 8)
                for i, name in enumerate(("q_hi", "q_hi", "q_lo")):
                    sp.dma_start(q_stack[i * HD:(i + 1) * HD, hs, :].bitcast(F32),
                                 dram[name].rearrange("(h d) t -> d h t", d=HD)[:, hs, bass.ds(b * N, N)]
                                 ).then_inc(q_landed[half], 16)

            def stack_k(f):
                for r in range(4):
                    rows = slice(r * HD, (r + 1) * HD)
                    for i, part in enumerate((k_hi, k_lo, k_hi)):
                        sp.dma_start(k_stack[i * HD:(i + 1) * HD, 4 * f + r, 1:S + 1].bitcast(F32),
                                     part[rows, f % 2, :].bitcast(F32)).then_inc(k_landed[f], 16)

            def step(b, last_ln=False, last=False):
                first = is_first(b)
                if not first:
                    sp.wait_ge(s_mm, NH * b)
                    load_q(b, 1)
                if not last_ln:
                    for t in range(CT):
                        sp.wait_ge(ctx_normed, CT * (b + 2))
                        load_ctx(b + 2, t)
                if not first:
                    wait_apart(sp, sh.consts, lo_done, splits_done(b, "K2b"))
                    if not is_int(b, 0):
                        sp.wait_ge(s_mm, NH * b - 4)
                    stack_k(2)
                    sp.wait_ge(lo_done, splits_done(b, "K3b"))
                    stack_k(3)
                    if not is_int(b, 0):
                        sp.wait_ge(att_ready, b)
                        sp.dma_start(dram["att"][:, bass.ds(b - 1, 1), :].rearrange("p b d -> p (b d)"), att[:]
                                     ).then_inc(att_stored, 16)
                if not last:
                    if not first:
                        sp.wait_ge(s_mm, NH * b + 8)
                    load_q(b + 1, 0)
                    for f in range(2):
                        sp.wait_ge(lo_done, splits_done(b, f"K{f}b"))
                        stack_k(f)

            def load_modulation():
                sp.wait_ge(mod_mm, 1)
                sp.dma_start(sh.raw[:, 0], dram["w_mod"][:, :, 5 * 512:6 * 512]).then_inc(mod_landed[0], 16)
                sp.wait_ge(mod_mm, 2)
                sp.dma_start(sh.raw[:, 1], dram["w_cproj"]).then_inc(mod_landed[1], 16)

            for t in range(CT):
                load_ctx(0, t)
            for q in range(2):
                sp.wait_ge(w_lo_done, q + 1)
                sp.dma_start(sh.raw[:, q], dram["w_mod"][:, :, (3 + q) * 512:(4 + q) * 512]).then_inc(mod_landed[q], 16)
            steps(sp, step, load_modulation)
            sp.wait_ge(att_ready, B)
            sp.dma_start(dram["att"][:, B - 1, :], att[:]).then_inc(att_stored, 16)
            sp.wait_ge(att_stored, 16 * B)
            sp.wait_ge(mod_landed[1], 32)

        @block.tensor
        def _(pe):
            pe.wait_ge(w_lo_done, 2)
            pe.wait_ge(cleared, 3)

            def bank_freed(b, x):
                if x[0] == "T":
                    if x != "T0":
                        pe.wait_ge(lo_done, splits_done(b, f"T{int(x[1]) - 1}"))
                    elif not is_first(b) and not is_int(b, 0):
                        pe.wait_ge(att_ready, b)
                    return
                at = BIG.index(x)
                if is_first(b) and at < len(OWN) + 2:
                    return
                before, its_step = BIG[at - 2], (b if at >= 2 else b - 1)
                if before[0] == "V":
                    pe.wait_ge(v_copied, vs_done(its_step, before))
                else:
                    pe.wait_ge(lo_done, splits_done(its_step, before))

            def piece(b, x):
                if x[0] == "T":
                    t = int(x[1])
                    n = TILES[t][1]
                    bank_freed(b, x)
                    pe.wait_ge(ctx_normed, CT * (b + 1) + t + 1)
                    for c in range(FC):
                        mm = pe.transpose(bank[:, TURNED, c * P:c * P + n], c_norm[0:n, t, c * P:(c + 1) * P], sh.ident[0:n, 0:n])
                elif x[0] == "V":
                    t, c = int(x[1]), int(x[2])
                    at_t, n = TILES[t]
                    out = bank[0:n, piece_bank(x[:2]), :]
                    if c == 0:
                        bank_freed(b, x[:2])
                        pe.wait_ge(lo_done, splits_done(b, f"T{t}"))
                    pe.matmul(out, c_hi[:, c, at_t:at_t + n], wkv_hi[:, c, D:], start=(c == 0), stop=False)
                    pe.matmul(out, c_hi[:, c, at_t:at_t + n], wkv_lo[:, c, D:], start=False, stop=False)
                    mm = pe.matmul(out, c_lo[:, c, at_t:at_t + n], wkv_hi[:, c, D:], start=False, stop=(c == FC - 1))
                    if c < FC - 1:
                        return
                else:
                    f, half = int(x[1]), "ab".index(x[2])
                    at_k = half * (S - WIDE)
                    bank_freed(b, x)
                    if x[1] == "0":
                        pe.wait_ge(lo_done, splits_done(b, f"T{(at_k + WIDE - 1) // P}"))
                    mm = product3(pe, bank[:, piece_bank(x), 0:WIDE],
                                  lambda c: wkv_hi[:, c, f * P:(f + 1) * P], lambda c: wkv_lo[:, c, f * P:(f + 1) * P],
                                  lambda c: c_hi[:, c, at_k:at_k + WIDE], lambda c: c_lo[:, c, at_k:at_k + WIDE], FC)
                mm.then_inc(piece_mm, 1)

            def scores(b, h):
                if h % 8 == 0:
                    pe.wait_ge(q_landed[h // 8], 48 * (b + 1))
                if h % 4 == 0:
                    pe.wait_ge(k_landed[h // 4], 192 * (b + 1))
                if not (is_int(b, 0) and h == 0):
                    pe.wait_ge(exp_done, NH * b + h)
                for half in range(2):
                    mm = pe.matmul(bank[0:N, half, 0:WIDE], q_stack[:, h, :], k_stack[:, h, half * HALF:half * HALF + WIDE],
                                   start=True, stop=True)
                mm.then_inc(s_mm, 1)

            def turn_probs(n, h):
                pe.wait_ge(exp_done, n + 1)
                if not is_int(n, 0):
                    pe.wait_ge(p_copied_dve, n)
                    pe.wait_ge(p_copied_act, n)
                for t, (at, rows) in enumerate(TILES):
                    mm = pe.transpose(bank[0:rows, PROBS_T + t // 3, (t % 3) * N:(t % 3 + 1) * N],
                                      prob[h % 2][:, at:at + rows], sh.ident[0:N, 0:N])
                mm.then_inc(p_turned, 1)

            def weigh(b, g):
                pe.wait_ge(p_copied_dve, NH * b + 4 * g + 4)
                pe.wait_ge(p_copied_act, NH * b + 4 * g + 4)
                if g % 2 == 0:
                    pe.wait_ge(v_moved[g // 2], b + 1)
                if g == 0 and not is_int(b, 0):
                    pe.wait_ge(out_taken, b)
                for t, (at, rows) in enumerate(TILES):
                    for j in range(4):
                        h = 4 * g + j
                        mm = pe.matmul(bank[j * HD:(j + 1) * HD, OUT, g * N:(g + 1) * N], v_now[0:rows, t, h * HD:(h + 1) * HD],
                                       prob_t[j][0:rows, t, :], start=(t == 0), stop=(t == CT - 1), tile_position=(0, j * HD))
                mm.then_inc(pv_mm, 1)

            def turn_out(b, t5_step):
                pe.wait_ge(out_taken, b + 1)
                pe.wait_ge(lo_done, splits_done(t5_step, "T5"))
                for f in range(FC):
                    mm = pe.transpose(bank[0:N, TURNED, f * P:(f + 1) * P], out_t[:, f, :], sh.ident)
                mm.then_inc(out_turned, 1)

            def step(b, last_ln=False, last=False):
                for s in range(NH):
                    if not is_first(b):
                        scores(b, s)
                        if s >= 1:
                            turn_probs(NH * b + s - 1, s - 1)
                        elif not is_int(b, 0):
                            turn_probs(NH * b - 1, NH - 1)
                        if s == 2 and not is_int(b, 0):
                            turn_out(b - 1, b - 1)
                    for x in SLOTS[s]:
                        if own(b, last, x):
                            piece(b, x)
                    if is_first(b):
                        continue
                    if s % 4 == 0 and s > 0:
                        weigh(b, s // 4 - 1)
                    elif s == 0 and not is_int(b, 0):
                        weigh(b - 1, 3)

            def modulation():
                for m in range(3):
                    pe.wait_ge(mod_landed[m % 2], 16 * (m // 2 + 1))
                    if m == 2:
                        pe.wait_ge(mod_added, 1)
                    for f in range(4):
                        for c in range(FC):
                            mm = pe.matmul(bank[:, OUT + m % 2, f * B:(f + 1) * B], sh.raw[:, m % 2, c, f * P:(f + 1) * P],
                                           sh.silu[:, c, :], start=(c == 0), stop=(c == FC - 1))
                    mm.then_inc(mod_mm, 1)
                pe.wait_ge(mod_added, 3)

            steps(pe, step, modulation)
            turn_probs(NH * B - 1, NH - 1)
            weigh(B - 1, 3)
            turn_out(B - 1, B - 2)

        @block.scalar
        def _(act):
            for q in range(2):
                act.wait_ge(sh.kv_landed[q], 16)
                act.activation(wkv_hi[:, :, q * 512:(q + 1) * 512], sh.raw[:, q], ACT.Copy).then_inc(w_hi_done, 1)

            def take(b, x):
                src = bank[:, piece_bank(x), :]
                act.wait_ge(piece_mm, pieces_done(b, x))
                if x[0] == "T":
                    at, n = TILES[int(x[1])]
                    act.activation(c_hi[:, :, at:at + n], src.rearrange("p (c s) -> p c s", c=FC)[:, :, 0:n],
                                   ACT.Copy).then_inc(hi_done, 1)
                elif x[0] == "V":
                    n = TILES[int(x[1])][1]
                    if x == "V0":
                        act.wait_ge(v_moved[1], b + 1)
                        act.wait_ge(v_moved[0], b + 1)
                    act.activation(v_next[0:n, int(x[1]), :], src[0:n, :], ACT.Copy).then_inc(v_copied, 1)
                else:
                    f, half = int(x[1]), "ab".index(x[2])
                    if half == 0 and not (is_first(b)) and f < 2:
                        act.wait_ge(k_landed[f + 2], 192 * (b + 1))
                    if half == 0 and f >= 2:
                        act.wait_ge(k_landed[f - 2], 192 * (b + 1))
                    act.activation(k_hi[:, f % 2, half * HALF:(half + 1) * HALF], src[:, half:half + HALF],
                                   ACT.Identity, bias=sh.b("kc", f)).then_inc(hi_done, 1)

            def soften(b, h):
                act.wait_ge(top_done, NH * b + h + 1)
                if not (is_int(b, 0) and h < 2):
                    act.wait_ge(p_turned, NH * b + h - 1)
                if h % 8 == 0 and not is_int(b, 0):
                    act.wait_ge(recip_done, 2 * b - 1 + h // 8)
                act.activation(prob[h % 2][:].rearrange("p (a k) -> p a k", a=2), bank[0:N, 0:2, 1:1 + HALF], ACT.Exp,
                               bias=neg_top[:, h:h + 1], accum_out=total[:, h:h + 1]).then_inc(exp_done, 1)

            def copy_probs(b, h):
                act.wait_ge(p_turned, NH * b + h + 1)
                if not (is_int(b, 0) and h < 4):
                    act.wait_ge(pv_mm, 4 * b + h // 4)
                act.activation(prob_t[h % 4][:, 3:6, :], bank[:, PROBS_T + 1, 0:3 * N].rearrange("p (t q) -> p t q", t=3),
                               ACT.Copy).then_inc(p_copied_act, 1)

            def step(b, last_ln=False, last=False):
                for s in range(NH):
                    for its_step, x in big_before(b, s, last):
                        take(its_step, x)
                    if not is_first(b):
                        if s >= 1:
                            copy_probs(b, s - 1)
                        elif not is_int(b, 0):
                            copy_probs(b - 1, NH - 1)
                    for x in turned_now(b, s, last):
                        take(b, x)
                    if not is_first(b):
                        soften(b, s)

            act.wait_ge(cleared, 3)
            steps(act, step)
            copy_probs(B - 1, NH - 1)

        @block.vector
        def _(dve):
            for q in range(2):
                sl = slice(q * 512, (q + 1) * 512)
                dve.wait_ge(w_hi_done, q + 1)
                dve.tensor_tensor(wkv_lo[:, :, sl], sh.raw[:, q], wkv_hi[:, :, sl].bitcast(F32), ALU.subtract).then_inc(w_lo_done, 1)
            dve.memset(bank[:, PROBS_T + 1, :], 0.0).then_inc(cleared, 1)

            def ln_stats(m, t):
                n = TILES[t][1]
                dve.wait_ge(ctx_landed[t], 16 * (m + 1))
                dve.bn_stats(stats[0:n, t, :], c_raw[0:n, t, :]).then_inc(st_done, 1)

            def ln_seed(m):
                dve.wait_ge(st_done, CT * (m + 1))
                if not is_int(m, 0):
                    wait_apart(dve, sh.consts, ctx_normed, CT * m)
                for t in range(CT):
                    n = TILES[t][1]
                    dve.bn_aggr(mean_var[0:n, t, :], stats[0:n, t, :]).then_inc(mv_done, 1)
                dve.wait_ge(mv_done, CT * (m + 1))
                seed_rsqrt(dve, seed_done, SEED_STEPS * m, mean_var[:], var_eps[:], half_bits[:], rstd[:])

            def take(b, x):
                if x[0] == "V":
                    return
                src = bank[:, piece_bank(x), :]
                dve.wait_ge(hi_done, splits_done(b, x))
                if x[0] == "T":
                    at, n = TILES[int(x[1])]
                    dve.tensor_tensor(c_lo[:, :, at:at + n], src.rearrange("p (c s) -> p c s", c=FC)[:, :, 0:n],
                                      c_hi[:, :, at:at + n].bitcast(F32), ALU.subtract).then_inc(lo_done, 1)
                else:
                    f, half = int(x[1]), "ab".index(x[2])
                    sl = slice(half * HALF, (half + 1) * HALF)
                    dve.scalar_tensor_tensor(out=k_lo[:, f % 2, sl], in0=src[:, half:half + HALF], scalar=sh.b("kc", f),
                                             in1=k_hi[:, f % 2, sl].bitcast(F32), op0=ALU.add, op1=ALU.subtract
                                             ).then_inc(lo_done, 1)

            def top(b, h):
                dve.wait_ge(s_mm, NH * b + h + 1)
                dve.tensor_reduce(neg_top[:, h:h + 1], bank[0:N, 0:2, 1:1 + HALF], AX.XY, ALU.max, negate=True).then_inc(top_done, 1)

            def copy_probs(b, h):
                dve.wait_ge(p_turned, NH * b + h + 1)
                if not (is_int(b, 0) and h < 4):
                    dve.wait_ge(pv_mm, 4 * b + h // 4)
                dve.tensor_copy(prob_t[h % 4][:, 0:3, :], bank[:, PROBS_T, 0:3 * N].rearrange("p (t q) -> p t q", t=3)
                                ).then_inc(p_copied_dve, 1)

            def invert_totals(b, half):
                hs = slice(8 * half, 8 * half + 8)
                dve.wait_ge(exp_done, NH * b + 8 * half + 8)
                dve.reciprocal(recip[:, hs], total[:, hs]).then_inc(recip_done, 1)

            def take_out(b):
                dve.wait_ge(pv_mm, 4 * b + 4)
                dve.tensor_copy(out_t[:], bank[:, OUT, 0:FC * N].rearrange("p (f t) -> p f t", f=FC)).then_inc(out_taken, 1)

            def normalise(b):
                dve.wait_ge(out_turned, b + 1)
                dve.wait_ge(recip_done, 2 * b + 2)
                if not is_int(b, 0):
                    dve.wait_ge(att_stored, 16 * b)
                dve.tensor_tensor(att[:].rearrange("p (h d) -> p h d", h=NH),
                                  bank[0:N, TURNED, :].rearrange("p (h d) -> p h d", h=NH),
                                  recip[:].unsqueeze(2).to_broadcast([N, NH, HD]), ALU.mult).then_inc(att_ready, 1)

            def step(b, last_ln=False, last=False):
                for s in range(NH):
                    again = not is_first(b) and not is_int(b, 0)
                    if not is_first(b):
                        top(b, s)
                    if s == 1 and again:
                        take_out(b - 1)
                    for its_step, x in big_before(b, s, last):
                        take(its_step, x)
                    if not is_first(b):
                        if s >= 1:
                            copy_probs(b, s - 1)
                        elif again:
                            copy_probs(b - 1, NH - 1)
                    if s == 1 and again:
                        invert_totals(b - 1, 1)
                    if s == 2 and again:
                        normalise(b - 1)
                    for x in turned_now(b, s, last):
                        take(b, x)
                    if s == 9 and not is_first(b):
                        invert_totals(b, 0)
                    if not last_ln:
                        if LN_SLOT <= s < LN_SLOT + CT:
                            ln_stats(b + 2, s - LN_SLOT)
                        if s == LN_SLOT + CT:
                            ln_seed(b + 2)

            dve.wait_ge(cleared, 3)
            for t in range(CT):
                ln_stats(0, t)
            ln_seed(0)
            def modulation():
                for m in range(3):
                    dve.wait_ge(mod_mm, m + 1)
                    dve.tensor_tensor(sh.mod[:, 12 + 4 * m:16 + 4 * m, :],
                                      bank[:, OUT + m % 2, 0:4 * B].rearrange("p (f b) -> p f b", f=4),
                                      sh.bias[:, 12 + 4 * m:16 + 4 * m].unsqueeze(2).to_broadcast([P, 4, B]),
                                      ALU.add).then_inc(mod_added, 1)
                dve.wait_ge(mod_added, 3)
                dve.tensor_scalar(sh.mod[:, 16:20, :], sh.mod[:, 16:20, :], 1.0, None, ALU.add)
                dve.tensor_tensor(sh.gate_bias[:, 4:8, :], sh.mod[:, 20:24, :],
                                  sh.bias[:, BIAS_OF["mlp2"]].unsqueeze(2).to_broadcast([P, 4, B]), ALU.mult)

            steps(dve, step, modulation)
            copy_probs(B - 1, NH - 1)
            invert_totals(B - 1, 1)
            take_out(B - 1)
            normalise(B - 1)

        @block.gpsimd
        def _(pool):
            pool.memset(k_stack[:, :, 0:1].bitcast(F32), 0.0)
            pool.memset(mean_var[:, CT - 1, :], 1.0).then_inc(cleared, 1)
            pool.memset(v_next[:, CT - 1, :], 0.0).then_inc(cleared, 1)

            def normalise_ctx(m):
                wait_apart(pool, sh.consts, seed_done, SEED_STEPS * (m + 1))
                newton_rsqrt(pool, sh.consts, newton_done, NEWTON_STEPS * m, mean_var[:], var_eps[:], rstd[:],
                             newton_work[:], neg_mean[:])
                pool.wait_ge(newton_done, NEWTON_STEPS * (m + 1))
                for t, (at, n) in enumerate(TILES):
                    if not is_int(m, 0):
                        wait_apart(pool, sh.consts, piece_mm, pieces_done(m - 2, f"T{t}"))
                    pool.tensor_scalar(c_norm[0:n, t, :], c_raw[0:n, t, :], neg_mean[0:n, t:t + 1], rstd[0:n, t:t + 1],
                                       ALU.add, ALU.mult).then_inc(ctx_normed, 1)

            def move_v(b, half):
                pool.wait_ge(v_copied, CT * (b + 1))
                if not is_int(b, 0):
                    wait_apart(pool, sh.consts, pv_mm, 4 * (b - 1) + 2 * half + 2)
                pool.tensor_copy(v_now[:, :, 256 * half:256 * half + 256], v_next[:, :, 256 * half:256 * half + 256]
                                 ).then_inc(v_moved[half], 1)

            def step(b, last_ln=False, last=False):
                if not is_first(b):
                    move_v(b, 1)
                if not last_ln:
                    normalise_ctx(b + 2)
                if not last:
                    move_v(b + 1, 0)

            normalise_ctx(0)
            steps(pool, step)


def mlp_stage(nc, sh, dram):
    GJ = GROUP_BATCHES
    HB = 2
    with ExitStack() as ctx:
        def sb(name, shape, dt=F32):
            return ctx.enter_context(nc.sbuf_tensor(name, shape, dt))

        def sem(name):
            return ctx.enter_context(nc.semaphore(name))

        bank = ctx.enter_context(nc.psum_tensor("bank3", [P, 8, 512], F32))
        wc_hi, wc_lo = sb("wc_hi", [P, FC, D], F32R), sb("wc_lo", [P, FC, D], F32R)
        w1_hi, w1_lo = sb("w1_hi", [P, FC, MLP], F32R), sb("w1_lo", [P, FC, MLP], F32R)
        w2_hi, w2_lo = sb("w2_hi", [P, MC, D], F32R), sb("w2_lo", [P, MC, D], F32R)
        a_tok = sb("a_tok", [N, GJ, D])
        att_t = sb("att_t3", [P, FC, N])
        a_hi, a_lo = sb("a_hi3", [P, FC, GT], F32R), sb("a_lo3", [P, FC, GT], F32R)
        xt = sb("xt3", [P, FC, GT])
        xm = sb("xm3", [P, FC, GT])
        h_hi = [sb(f"h_hi{i}", [P, GT], F32R) for i in range(HB)]
        h_lo = [sb(f"h_lo{i}", [P, GT], F32R) for i in range(HB)]
        gp = sb("gp3", [P, 16, GJ])
        stats, mean_var = sb("stats3", [N, GJ, 6]), sb("mean_var3", [N, GJ, 2])
        var_eps, half_bits = sb("var_eps3", [N, GJ]), sb("half_bits3", [N, GJ], I32)
        rstd, newton_work, neg_mean = sb("rstd3", [N, GJ]), sb("newton_work3", [N, GJ]), sb("neg_mean3", [N, GJ])

        raw_landed = [sem(f"raw_landed3_{i}") for i in range(2)]
        w_hi_done, w_lo_done, c_split, gp_ready = sem("w_hi_done3"), sem("w_lo_done3"), sem("c_split"), sem("gp_ready3")
        a_landed, x1_landed, x2_stored, xm_stored = (sem(n) for n in ("a_landed", "x1_landed", "x2_stored", "xm_stored"))
        a_turned, a_split, c_mm, x2_ready, x2_turned = (sem(n) for n in ("a_turned", "a_split", "c_mm", "x2_ready", "x2_turned"))
        st_done, mv_done, seed_done, newton_done, normed = (
            sem(n) for n in ("st_done3", "mv_done3", "seed_done3", "newton_done3", "normed3"))
        xn_back, xm_ready, xm_split = sem("xn_back3"), sem("xm_ready3"), sem("xm_split3")
        xm_landed, x2_landed, out_stored = sem("xm_landed"), sem("x2_landed"), sem("out_stored")
        h_mm, gelu_done, h_split, y_mm, gated_done, y_ready = (
            sem(n) for n in ("h_mm", "gelu_done", "h_split", "y_mm", "gated_done3", "y_ready"))
        gp2_ready = sem("gp2_ready")

        block = ctx.enter_context(nc.Block())

        @block.sync
        def _(sp):
            with sp.Fori(0, GROUPS) as g:
                gs = bass.ds(g * GT, GT)
                sp.wait_ge(w_lo_done, 2 * g)
                sp.dma_start(sh.raw[:, 0], dram["w_mlp1"][:, :, bass.ds(g * 512, 512)]).then_inc(raw_landed[0], 16)
                sp.wait_ge(normed, GJ * g)
                sp.wait_ge(xn_back, GJ * g)
                sp.dma_start(a_tok[:], dram["att"][:, bass.ds(g * GJ, GJ), :]).then_inc(a_landed, 16)
                sp.wait_ge(x2_stored, 16 * g)
                sp.wait_ge(x2_turned, GJ * g)
                sp.dma_start(xt[:], dram["x1"][:, :, gs]).then_inc(x1_landed, 16)
                sp.wait_ge(c_split, 1)
                sp.dma_start(sh.raw[:, 1], dram["w_mlp2"][:, bass.ds(g * 4, 4), :]).then_inc(raw_landed[1], 16)
                sp.wait_ge(x2_ready, FC * g + FC)
                sp.dma_start(dram["x2"][:, :, gs], xt[:]).then_inc(x2_stored, 16)
                sp.wait_ge(xm_split, 2 * GJ * g + 2 * GJ)
                sp.dma_start(dram["xm_hi"][:, :, gs], a_hi[:].bitcast(F32)).then_inc(xm_stored, 16)
                sp.dma_start(dram["xm_lo"][:, :, gs], a_lo[:].bitcast(F32)).then_inc(xm_stored, 16)
            sp.wait_ge(x2_stored, 16 * GROUPS)
            sp.wait_ge(xm_stored, 32 * GROUPS)
            with sp.Fori(0, GROUPS) as g:
                gs = bass.ds(g * GT, GT)
                sp.wait_ge(h_mm, MC * g)
                sp.dma_start(a_hi[:].bitcast(F32), dram["xm_hi"][:, :, gs]).then_inc(xm_landed, 16)
                sp.dma_start(a_lo[:].bitcast(F32), dram["xm_lo"][:, :, gs]).then_inc(xm_landed, 16)
                sp.wait_ge(out_stored, 16 * g)
                sp.dma_start(xt[:], dram["x2"][:, :, gs]).then_inc(x2_landed, 16)
                sp.wait_ge(y_ready, FC * g + FC)
                sp.dma_start(dram["out"][:, :, gs], xt[:]).then_inc(out_stored, 16)
            sp.wait_ge(out_stored, 16 * GROUPS)

        @block.tensor
        def _(pe):
            pe.wait_ge(c_split, 1)
            with pe.Fori(0, GROUPS) as g:
                for j in range(GJ):
                    if j == 0:
                        pe.wait_ge(a_landed, 16 * g + 16)
                        pe.wait_ge(xm_ready, GJ * g)
                    if j >= 2:
                        pe.wait_ge(a_split, 3 * GJ * g + 3 * j - 5)
                    for f in range(FC):
                        mm = pe.transpose(bank[:, 4 + j % 2, f * N:(f + 1) * N], a_tok[:, j, f * P:(f + 1) * P], sh.ident[0:N, 0:N])
                    mm.then_inc(a_turned, 1)
                for f in range(FC):
                    if f == 0:
                        pe.wait_ge(a_split, 3 * GJ * g + 3 * GJ)
                        pe.wait_ge(normed, GJ * g)
                    product3(pe, bank[:, f, 0:GT],
                             lambda c: wc_hi[:, c, f * P:(f + 1) * P], lambda c: wc_lo[:, c, f * P:(f + 1) * P],
                             lambda c: a_hi[:, c, :], lambda c: a_lo[:, c, :], FC).then_inc(c_mm, 1)
                for j in range(GJ):
                    if j == 0:
                        pe.wait_ge(x2_ready, FC * g + FC)
                    for f in range(FC):
                        mm = pe.transpose(bank[0:N, j, f * P:(f + 1) * P], xt[:, f, j * N:(j + 1) * N], sh.ident)
                    mm.then_inc(x2_turned, 1)
                for j in range(GJ):
                    pe.wait_ge(normed, GJ * g + j + 1)
                    if j >= 2:
                        pe.wait_ge(xm_ready, GJ * g + j - 1)
                    for f in range(FC):
                        mm = pe.transpose(bank[:, 4 + j % 2, f * N:(f + 1) * N], a_tok[:, j, f * P:(f + 1) * P], sh.ident[0:N, 0:N])
                    mm.then_inc(xn_back, 1)
            pe.wait_ge(w_lo_done, 2 * GROUPS)
            pe.wait_ge(xm_ready, GJ * GROUPS)
            pe.wait_ge(normed, GJ * GROUPS)
            with pe.Fori(0, GROUPS) as g:
                def hidden(c):
                    if c == 0:
                        pe.wait_ge(xm_landed, 32 * g + 32)
                        pe.wait_ge(gelu_done, MC * g)
                    if c >= 4:
                        pe.wait_ge(gelu_done, MC * g + c - 3)
                    product3(pe, bank[:, 4 + c % 4, 0:GT],
                             lambda k: w1_hi[:, k, c * P:(c + 1) * P], lambda k: w1_lo[:, k, c * P:(c + 1) * P],
                             lambda k: a_hi[:, k, :], lambda k: a_lo[:, k, :], FC).then_inc(h_mm, 1)

                def output(c):
                    pe.wait_ge(h_split, 2 * MC * g + 2 * c + 2)
                    if c == 0:
                        pe.wait_ge(gated_done, FC * g)
                    for f in range(FC):
                        out = bank[:, f, 0:GT]
                        fs = slice(f * P, (f + 1) * P)
                        pe.matmul(out, w2_hi[:, c, fs], h_hi[c % HB][:], start=(c == 0), stop=False)
                        pe.matmul(out, w2_lo[:, c, fs], h_hi[c % HB][:], start=False, stop=False)
                        mm = pe.matmul(out, w2_hi[:, c, fs], h_lo[c % HB][:], start=False, stop=(c == MC - 1))
                    mm.then_inc(y_mm, 1)

                hidden(0)
                for c in range(MC):
                    if c + 1 < MC:
                        hidden(c + 1)
                    output(c)

        @block.scalar
        def _(act):
            act.activation(wc_hi[:], sh.raw[:, 1], ACT.Copy).then_inc(w_hi_done, 1)
            with act.Fori(0, GROUPS) as g:
                act.wait_ge(raw_landed[0], 16 * g + 16)
                act.activation(w1_hi[:, :, bass.ds(g * 512, 512)], sh.raw[:, 0], ACT.Copy).then_inc(w_hi_done, 1)
                act.wait_ge(raw_landed[1], 16 * g + 16)
                act.activation(w2_hi[:, bass.ds(g * 4, 4), :], sh.raw[:, 1], ACT.Copy).then_inc(w_hi_done, 1)
                for j in range(GJ):
                    act.wait_ge(xn_back, GJ * g + j + 1)
                    if j == 0:
                        act.wait_ge(gp_ready, 2 * g + 2)
                        act.wait_ge(xm_split, 2 * GJ * g)
                    for f in range(FC):
                        last = act.activation(xm[:, f, j * N:(j + 1) * N], bank[:, 4 + j % 2, f * N:(f + 1) * N],
                                              ACT.Identity, bias=gp[:, f, j:j + 1], scale=gp[:, 4 + f, j:j + 1])
                    last.then_inc(xm_ready, 1)
            act.wait_ge(xm_split, 2 * GJ * GROUPS)
            with act.Fori(0, GROUPS) as g:
                for c in range(MC):
                    act.wait_ge(h_mm, MC * g + c + 1)
                    if c >= HB:
                        act.wait_ge(h_split, 2 * MC * g + 2 * (c - HB) + 2)
                    elif c == 0:
                        act.wait_ge(h_split, 2 * MC * g)
                    act.activation(xm[:, c % HB, :], bank[:, 4 + c % 4, 0:GT], ACT.Gelu_apprx_tanh,
                                   bias=sh.b("mlp1", c)).then_inc(gelu_done, 1)
                act.wait_ge(y_mm, MC * g + MC)
                act.wait_ge(gp2_ready, 2 * g + 2)
                for f in range(FC):
                    act.wait_ge(y_ready, FC * g + (f - 1 if f >= 2 else 0))
                    for j in range(GJ):
                        last = act.activation(xm[:, 2 + f % 2, j * N:(j + 1) * N], bank[:, f, j * N:(j + 1) * N],
                                              ACT.Identity, bias=gp[:, 12 + f, j:j + 1], scale=gp[:, 8 + f, j:j + 1])
                    last.then_inc(gated_done, 1)

        @block.vector
        def _(dve):
            dve.wait_ge(w_hi_done, 1)
            dve.tensor_tensor(wc_lo[:], sh.raw[:, 1], wc_hi[:].bitcast(F32), ALU.subtract).then_inc(c_split, 1)
            with dve.Fori(0, GROUPS) as g:
                dve.wait_ge(w_hi_done, 2 * g + 2)
                s1, s2 = bass.ds(g * 512, 512), bass.ds(g * 4, 4)
                dve.tensor_tensor(w1_lo[:, :, s1], sh.raw[:, 0], w1_hi[:, :, s1].bitcast(F32), ALU.subtract).then_inc(w_lo_done, 1)
                for j in range(GJ):
                    sl = slice(j * N, (j + 1) * N)
                    dve.wait_ge(a_turned, GJ * g + j + 1)
                    dve.wait_ge(a_split, 3 * GJ * g + 3 * j)
                    dve.tensor_tensor(att_t[:], bank[:, 4 + j % 2, 0:GT].rearrange("p (f t) -> p f t", f=FC),
                                      sh.bias[:, BIAS_OF["vc"]].unsqueeze(2).to_broadcast([P, FC, N]), ALU.add).then_inc(a_split, 1)
                    dve.wait_ge(a_split, 3 * GJ * g + 3 * j + 1)
                    if j == 0:
                        dve.wait_ge(xm_stored, 32 * g)
                    dve.tensor_copy(a_hi[:, :, sl], att_t[:]).then_inc(a_split, 1)
                    dve.wait_ge(a_split, 3 * GJ * g + 3 * j + 2)
                    dve.tensor_tensor(a_lo[:, :, sl], att_t[:], a_hi[:, :, sl].bitcast(F32), ALU.subtract).then_inc(a_split, 1)
                for f in range(FC):
                    dve.wait_ge(c_mm, FC * g + f + 1)
                    if f == 0:
                        dve.wait_ge(x1_landed, 16 * g + 16)
                    dve.scalar_tensor_tensor(out=xt[:, f, :], in0=bank[:, f, 0:GT], scalar=sh.b("cproj", f), in1=xt[:, f, :],
                                             op0=ALU.add, op1=ALU.add).then_inc(x2_ready, 1)
                for j in range(GJ):
                    dve.wait_ge(x2_turned, GJ * g + j + 1)
                    dve.bn_stats(stats[:, j, :], bank[0:N, j, :]).then_inc(st_done, 1)
                wait_apart(dve, sh.consts, st_done, GJ * g + GJ)
                for j in range(GJ):
                    dve.bn_aggr(mean_var[:, j, :], stats[:, j, :]).then_inc(mv_done, 1)
                dve.wait_ge(mv_done, GJ * g + GJ)
                seed_rsqrt(dve, seed_done, SEED_STEPS * g, mean_var[:], var_eps[:], half_bits[:], rstd[:])
                dve.wait_ge(w_hi_done, 2 * g + 3)
                dve.tensor_tensor(w2_lo[:, s2, :], sh.raw[:, 1], w2_hi[:, s2, :].bitcast(F32), ALU.subtract).then_inc(w_lo_done, 1)
                dve.wait_ge(newton_done, NEWTON_STEPS * g + NEWTON_STEPS)
                for j in range(GJ):
                    dve.wait_ge(a_turned, GJ * g + GJ)
                    dve.tensor_scalar(a_tok[:, j, :], bank[0:N, j, :], mean_var[:, j, 0:1], rstd[:, j:j + 1],
                                      ALU.subtract, ALU.mult).then_inc(normed, 1)
                for j in range(GJ):
                    sl = slice(j * N, (j + 1) * N)
                    dve.wait_ge(xm_ready, GJ * g + j + 1)
                    dve.wait_ge(c_mm, FC * g + FC)
                    dve.tensor_copy(a_hi[:, :, sl], xm[:, :, sl]).then_inc(xm_split, 1)
                    dve.wait_ge(xm_split, 2 * GJ * g + 2 * j + 1)
                    dve.tensor_tensor(a_lo[:, :, sl], xm[:, :, sl], a_hi[:, :, sl].bitcast(F32), ALU.subtract).then_inc(xm_split, 1)
            with dve.Fori(0, GROUPS) as g:
                for c in range(MC):
                    dve.wait_ge(gelu_done, MC * g + c + 1)
                    if c >= HB:
                        dve.wait_ge(y_mm, MC * g + c - HB + 1)
                    elif c == 0:
                        dve.wait_ge(y_mm, MC * g)
                    dve.tensor_copy(h_hi[c % HB][:], xm[:, c % HB, :]).then_inc(h_split, 1)
                    dve.wait_ge(h_split, 2 * MC * g + 2 * c + 1)
                    dve.tensor_tensor(h_lo[c % HB][:], xm[:, c % HB, :], h_hi[c % HB][:].bitcast(F32), ALU.subtract).then_inc(h_split, 1)
                for f in range(FC):
                    if f == 0:
                        dve.wait_ge(x2_landed, 16 * g + 16)
                    dve.wait_ge(gated_done, FC * g + f + 1)
                    dve.tensor_tensor(xt[:, f, :], xt[:, f, :], xm[:, 2 + f % 2, :], ALU.add).then_inc(y_ready, 1)

        @block.gpsimd
        def _(pool):
            with pool.Fori(0, GROUPS) as g:
                wait_apart(pool, sh.consts, xm_ready, GJ * g)
                pool.tensor_copy(gp[:, 0:8, :], sh.mod[:, 12:20, bass.ds(g * GJ, GJ)]).then_inc(gp_ready, 2)
                wait_apart(pool, sh.consts, seed_done, SEED_STEPS * g + SEED_STEPS)
                newton_rsqrt(pool, sh.consts, newton_done, NEWTON_STEPS * g, mean_var[:], var_eps[:], rstd[:], newton_work[:], neg_mean[:])
            with pool.Fori(0, GROUPS) as g:
                wait_apart(pool, sh.consts, gated_done, FC * g)
                pool.tensor_copy(gp[:, 8:12, :], sh.mod[:, 20:24, bass.ds(g * GJ, GJ)]).then_inc(gp2_ready, 1)
                pool.tensor_copy(gp[:, 12:16, :], sh.gate_bias[:, 4:8, bass.ds(g * GJ, GJ)]).then_inc(gp2_ready, 1)


def build(nc, x_tok, x_t, ctx_tok, cond_t, bias_cols, ident, w_mod, w_qkv, w_proj, w_qc, w_kvc, w_cproj, w_mlp1, w_mlp2, out):
    dram = {"x_tok": x_tok, "x_t": x_t, "ctx": ctx_tok, "cond_t": cond_t, "bias_cols": bias_cols, "ident": ident,
            "w_mod": w_mod, "w_qkv": w_qkv, "w_proj": w_proj, "w_qc": w_qc, "w_kvc": w_kvc, "w_cproj": w_cproj,
            "w_mlp1": w_mlp1, "w_mlp2": w_mlp2, "out": out}
    dram["x1"] = nc.dram_tensor("scratch_x1", (P, FC, B * N), F32, kind="Internal").ap()
    dram["q_hi"] = nc.dram_tensor("scratch_q_hi", (D, B * N), F32, kind="Internal").ap()
    dram["q_lo"] = nc.dram_tensor("scratch_q_lo", (D, B * N), F32, kind="Internal").ap()
    dram["att"] = nc.dram_tensor("scratch_att", (N, B, D), F32, kind="Internal").ap()
    for name in ("x2", "xm_hi", "xm_lo"):
        dram[name] = nc.dram_tensor("scratch_" + name, (P, FC, B * N), F32, kind="Internal").ap()
    with ExitStack() as ctx:
        sh = Shared(nc, ctx)
        self_attention_stage(nc, sh, dram)
        cross_attention_stage(nc, sh, dram)
        mlp_stage(nc, sh, dram)


_INS = ["x_tok", "x_t", "ctx_tok", "cond_t", "bias_cols", "ident", "w_mod", "w_qkv", "w_proj", "w_qc", "w_kvc",
        "w_cproj", "w_mlp1", "w_mlp2"]


def kernel(x, cond_1024, ctx_1024, L0_xcond_W_mod, L0_xcond_b_mod, L0_xcond_W_qkv, L0_xcond_b_qkv,
           L0_xcond_W_proj, L0_xcond_b_proj, L0_xcond_W_qc, L0_xcond_b_qc, L0_xcond_W_kvc, L0_xcond_b_kvc,
           L0_xcond_W_cproj, L0_xcond_b_cproj, L0_xcond_W_mlp1, L0_xcond_b_mlp1, L0_xcond_W_mlp2,
           L0_xcond_b_mlp2):
    import numpy as _np
    import concourse.bacc as _bacc
    from concourse import mybir as _mybir
    from concourse.bass_utils import run_bass_kernel_spmd as _run

    def chunked(w):
        return _np.ascontiguousarray(_np.asarray(w).reshape(-1, 128, w.shape[1]).transpose(1, 0, 2))

    x = _np.asarray(x)
    biases = [L0_xcond_b_mod, L0_xcond_b_qkv, L0_xcond_b_proj, L0_xcond_b_qc, L0_xcond_b_kvc,
              L0_xcond_b_cproj, L0_xcond_b_mlp1, L0_xcond_b_mlp2]
    laid = {
        "x_tok": _np.ascontiguousarray(x.transpose(1, 0, 2)),
        "x_t": chunked(x.reshape(-1, x.shape[2]).T),
        "ctx_tok": _np.ascontiguousarray(ctx_1024),
        "cond_t": chunked(_np.asarray(cond_1024).T),
        "bias_cols": _np.ascontiguousarray(_np.concatenate([_np.asarray(b) for b in biases]).reshape(-1, 128).T),
        "ident": _np.eye(128, dtype=_np.float32),
        "w_mod": chunked(L0_xcond_W_mod), "w_qkv": chunked(L0_xcond_W_qkv), "w_proj": chunked(L0_xcond_W_proj),
        "w_qc": chunked(L0_xcond_W_qc), "w_kvc": chunked(L0_xcond_W_kvc), "w_cproj": chunked(L0_xcond_W_cproj),
        "w_mlp1": chunked(L0_xcond_W_mlp1), "w_mlp2": chunked(L0_xcond_W_mlp2),
    }
    nc = _bacc.Bacc("TRN2", target_bir_lowering=False, num_devices=1)
    arrays, args = {}, []
    for name in _INS:
        a = laid[name]
        arrays[f"in_{name}_dram"] = a
        args.append(nc.dram_tensor(f"in_{name}_dram", a.shape, _mybir.dt.from_np(a.dtype), kind="ExternalInput").ap())
    args.append(nc.dram_tensor("out_0_dram", (P, FC, B * N), _mybir.dt.float32, kind="ExternalOutput").ap())
    build(nc, *args)
    r = _run(nc, [arrays], core_ids=[0])
    got = _np.asarray(r.results[0]["out_0_dram"])
    return _np.ascontiguousarray(got.transpose(2, 1, 0).reshape(B, N, D))
```

```python
from contextlib import ExitStack

import concourse.bass as bass
from concourse import mybir

F32 = mybir.dt.float32
F32R = mybir.dt.float32r
I32 = mybir.dt.int32
ALU = mybir.AluOpType
ACT = mybir.ActivationFunctionType
AX = mybir.AxisListType

P = 128
B, N, D = 16, 100, 512
S = 722
NH, HD = 16, 32
MLP = 4 * D
FC = D // P
MC = MLP // P
GROUP_BATCHES = 4
GROUPS = B // GROUP_BATCHES
GT = GROUP_BATCHES * N
SCALE = float(HD) ** -0.5

LN_EPS = 1e-6
RSQRT_SEED = 0x5F3759DF
NEWTON_ROUNDS = 3
SEED_STEPS = 3
NEWTON_STEPS = 1 + 4 * NEWTON_ROUNDS
RSQRT_STEPS = SEED_STEPS + 3 * NEWTON_ROUNDS

BIAS_OF = {}
_at = 0
for _name, _n in (("mod", 24), ("qk", 8), ("v", 4), ("proj", 4), ("qc", 4), ("kc", 4), ("vc", 4),
                  ("cproj", 4), ("mlp1", 16), ("mlp2", 4)):
    BIAS_OF[_name] = slice(_at, _at + _n)
    _at += _n
BIAS_COLS = _at


def seed_rsqrt(dve, sem, base, mean_var, var_eps, half_bits, guess):
    dve.tensor_scalar(var_eps, mean_var[:, :, 1], LN_EPS, None, ALU.add).then_inc(sem, 1)
    dve.wait_ge(sem, base + 1)
    dve.tensor_scalar(half_bits, var_eps.bitcast(I32), 1, None, ALU.logical_shift_right).then_inc(sem, 1)
    dve.wait_ge(sem, base + 2)
    dve.tensor_scalar(guess.bitcast(I32), half_bits, -1.0, float(RSQRT_SEED), ALU.mult, ALU.add).then_inc(sem, 1)


def rsqrt(dve, sem, base, mean_var, var_eps, half_bits, guess, work):
    seed_rsqrt(dve, sem, base, mean_var, var_eps, half_bits, guess)
    for r in range(NEWTON_ROUNDS):
        before = base + SEED_STEPS + 3 * r
        dve.wait_ge(sem, before)
        dve.scalar_tensor_tensor(out=work, in0=guess, scalar=-0.5, in1=guess, op0=ALU.mult, op1=ALU.mult).then_inc(sem, 1)
        dve.wait_ge(sem, before + 1)
        dve.tensor_tensor(work, work, var_eps, ALU.mult).then_inc(sem, 1)
        dve.wait_ge(sem, before + 2)
        dve.scalar_tensor_tensor(out=guess, in0=work, scalar=1.5, in1=guess, op0=ALU.add, op1=ALU.mult).then_inc(sem, 1)


def newton_rsqrt(pool, consts, sem, base, mean_var, var_eps, guess, work, neg_mean):
    def after(n):
        wait_apart(pool, consts, sem, base + n)

    pool.tensor_scalar(neg_mean, mean_var[:, :, 0], -1.0, None, ALU.mult).then_inc(sem, 1)
    for r in range(NEWTON_ROUNDS):
        after(4 * r + 1)
        pool.tensor_tensor(work, guess, guess, ALU.mult).then_inc(sem, 1)
        after(4 * r + 2)
        pool.tensor_tensor(work, work, var_eps, ALU.mult).then_inc(sem, 1)
        after(4 * r + 3)
        pool.tensor_scalar(work, work, -0.5, 1.5, ALU.mult, ALU.add).then_inc(sem, 1)
        after(4 * r + 4)
        pool.tensor_tensor(guess, guess, work, ALU.mult).then_inc(sem, 1)


def wait_apart(eng, consts, sem, value):
    if not isinstance(value, int):
        value = eng.snap(eng.to_reg(value))
    eng.wait_ge(consts, 48)
    eng.wait_ge(sem, value)


def product3(pe, out, lhs_hi, lhs_lo, rhs_hi, rhs_lo, chunks):
    for c in range(chunks):
        pe.matmul(out, lhs_hi(c), rhs_hi(c), start=(c == 0), stop=False)
        pe.matmul(out, lhs_hi(c), rhs_lo(c), start=False, stop=False)
        last = pe.matmul(out, lhs_lo(c), rhs_hi(c), start=False, stop=(c == chunks - 1))
    return last


class Shared:

    def __init__(self, nc, ctx):
        def sb(name, shape, dt=F32):
            return ctx.enter_context(nc.sbuf_tensor(name, shape, dt))

        self.bias = sb("bias", [P, BIAS_COLS])[:]
        self.ident = sb("identity", [P, P])[:]
        self.cond = sb("cond", [P, FC, B])[:]
        self.silu = sb("silu", [P, FC, B])[:]
        self.mod = sb("mod", [P, 24, B])[:]
        self.gate_bias = sb("gate_bias", [P, 8, B])[:]
        self.b_qc_scaled = sb("b_qc_scaled", [P, FC])[:]
        self.raw = sb("raw_weights", [P, 2, FC, 512])[:]
        self.consts = ctx.enter_context(nc.semaphore("consts"))
        self.kv_landed = [ctx.enter_context(nc.semaphore(f"kv_landed{i}")) for i in range(2)]

    def b(self, name, f):
        at = BIAS_OF[name].start + f
        return self.bias[:, at:at + 1]


def self_attention_stage(nc, sh, dram):
    GJ = GROUP_BATCHES
    UNITS = 2 * FC
    AHEAD = 3
    staging = [0, 2, 1, 0, 1, 2, 0, 1]
    chunks = [("mod", 0), ("mod", 1), ("qkv", 0), ("qkv", 1), ("qkv", 2), ("mod", 2), ("proj", 0), ("qc", 0)]
    with ExitStack() as ctx:
        def sb(name, shape, dt=F32):
            return ctx.enter_context(nc.sbuf_tensor(name, shape, dt))

        def sem(name):
            return ctx.enter_context(nc.semaphore(name))

        bank = ctx.enter_context(nc.psum_tensor("bank1", [P, 8, 512], F32))
        w_hi = {"qkv": sb("wqkv_hi", [P, FC, 3 * D], F32R), "proj": sb("wproj_hi", [P, FC, D], F32R),
                "qc": sb("wqc_hi", [P, FC, D], F32R)}
        w_lo = {"qkv": sb("wqkv_lo", [P, FC, 3 * D], F32R), "proj": sb("wproj_lo", [P, FC, D], F32R),
                "qc": sb("wqc_lo", [P, FC, D], F32R)}
        x_tok = sb("x_tok", [N, GJ, D])
        stats_a, stats_b = sb("stats_a", [N, GJ, 6]), sb("stats_b", [N, GJ, 6])
        mean_var_a, mean_var_b = sb("mean_var_a", [N, GJ, 2]), sb("mean_var_b", [N, GJ, 2])
        var_eps_a, var_eps_b = sb("var_eps_a", [N, GJ]), sb("var_eps_b", [N, GJ])
        half_bits = sb("half_bits", [N, GJ], I32)
        rstd_a, rstd_b = sb("rstd_a", [N, GJ]), sb("rstd_b", [N, GJ])
        newton_work = sb("newton_work", [N, GJ])
        gp = sb("gp", [P, 8, GJ])
        gate = sb("gate", [P, 8, GJ])
        xm = sb("xm", [P, FC, GT])
        x_hi = sb("x_hi", [P, FC, GT], F32R)
        x_lo = sb("x_lo", [P, FC, GT], F32R)
        qk = sb("qk", [P, 2 * FC, GT])
        q_hi, q_lo = (qk[:, i * FC:(i + 1) * FC, :].bitcast(F32R) for i in range(2))
        v = sb("v", [N, GJ, NH, HD + 1])
        prob = [sb(f"prob{i}", [N, 8, N]) for i in range(2)]
        prob_t = [sb(f"prob_t{i}", [N, 2, 4 * N]) for i in range(2)]
        top = sb("top", [N, 2, 8])
        recip = sb("recip", [N, 2, 8])
        att = sb("att", [N, GJ, D])
        att_t = sb("att_t", [P, GT])
        a_hi = sb("a_hi", [P, FC, GT], F32R)
        a_lo = sb("a_lo", [P, FC, GT], F32R)
        xt = sb("xt", [P, FC, GT])
        gated = [sb(f"gated{i}", [P, GT]) for i in range(2)]
        xn = [sb(f"xn{i}", [N, D]) for i in range(2)]
        q32 = [sb(f"q32_{i}", [P, GT]) for i in range(2)]

        raw_landed = [sem(f"raw_landed{i}") for i in range(3)]
        raw = [sh.raw[:, 0], sh.raw[:, 1], qk[:].rearrange("p f t -> p (f t)")[:, 0:FC * 512].rearrange("p (c n) -> p c n", c=FC)]

        w_hi_done, w_lo_done = sem("w_hi_done"), sem("w_lo_done")
        silu_done, mod_mm, mod_added, mod_one, gate_bias = (
            sem(n) for n in ("silu_done", "mod_mm", "mod_added", "mod_one", "gate_bias"))
        x_landed, xt_landed, x1_stored, q_stored = (sem(n) for n in ("x_landed", "xt_landed", "x1_stored", "q_stored"))
        ones_set, gp_ready, gate_ready = sem("ones_set"), sem("gp_ready"), sem("gate_ready")
        st_a, mv_a, rstd_done_a, ln_a = (sem(n) for n in ("st_a", "mv_a", "rstd_done_a", "ln_a"))
        st_b, mv_b, rstd_done_b, ln_b = (sem(n) for n in ("st_b", "mv_b", "rstd_done_b", "ln_b"))
        x_turned, xm_ready, x_split = sem("x_turned"), sem("xm_ready"), sem("x_split")
        v_mm, v_copied, qk_mm, qk_copied = (sem(n) for n in ("v_mm", "v_copied", "qk_mm", "qk_copied"))
        s_mm, top_done, sub_done, exp_done = (sem(n) for n in ("s_mm", "top_done", "sub_done", "exp_done"))
        p_turned, p_copied, pv_mm, recip_done, att_ready = (
            sem(n) for n in ("p_turned", "p_copied", "pv_mm", "recip_done", "att_ready"))
        att_turned, att_added, att_split = sem("att_turned"), sem("att_added"), sem("att_split")
        proj_mm, gated_done, x1_ready = sem("proj_mm"), sem("gated_done"), sem("x1_ready")
        x1_turned, xn_back, xn_hi, xn_lo = (sem(n) for n in ("x1_turned", "xn_back", "xn_hi", "xn_lo"))
        q_mm, q32_done, q_split = sem("q_mm"), sem("q32_done"), sem("q_split")

        def landings(k):
            return staging[:k + 1].count(staging[k])

        def chunk_used(eng, k):
            kinds = [c[0] == "mod" for c in chunks[:k + 1]]
            if kinds[k]:
                eng.wait_ge(mod_mm, sum(kinds))
            else:
                eng.wait_ge(w_lo_done, k + 1 - sum(kinds))

        def unit_bank(u):
            return 2 * (u % 2)

        def qk_tile(n):
            return n // 2 + FC * (n % 2)

        def qk_bank(n):
            return 6 if n == 1 else 7

        def groups(eng, front, body):
            front(0)
            with eng.Fori(0, GROUPS - 1) as g:
                body(g)
            body(GROUPS - 1, last=True)

        block = ctx.enter_context(nc.Block())

        @block.sync
        def _(sp):
            sp.dma_start(sh.bias, dram["bias_cols"]).then_inc(sh.consts, 16)
            sp.dma_start(sh.ident, dram["ident"]).then_inc(sh.consts, 16)
            sp.dma_start(sh.cond, dram["cond_t"]).then_inc(sh.consts, 16)
            for k, (kind, q) in enumerate(chunks):
                before = [i for i in range(k) if staging[i] == staging[k]]
                if before:
                    chunk_used(sp, before[-1])
                sp.dma_start(raw[staging[k]], dram["w_" + kind][:, :, q * 512:(q + 1) * 512]).then_inc(raw_landed[staging[k]], 16)
            for q in range(2):
                chunk_used(sp, len(chunks) - 2 + q)
                sp.dma_start(sh.raw[:, q], dram["w_kvc"][:, :, q * 512:(q + 1) * 512]).then_inc(sh.kv_landed[q], 16)
            with sp.Fori(0, GROUPS) as g:
                wait_apart(sp, sh.consts, x1_stored, 16 * g)
                sp.wait_ge(x1_turned, GJ * g)
                sp.dma_start(xt[:], dram["x_t"][:, :, bass.ds(g * GT, GT)]).then_inc(xt_landed, 16)
                sp.wait_ge(x1_ready, FC * g + FC)
                sp.dma_start(dram["x1"][:, :, bass.ds(g * GT, GT)], xt[:]).then_inc(x1_stored, 16)
                sp.wait_ge(q_split, 2 * FC * g + 2 * FC)
                sp.dma_start(dram["q_hi"].rearrange("(f p) t -> p f t", p=P)[:, :, bass.ds(g * GT, GT)],
                             q_hi.bitcast(F32)).then_inc(q_stored, 16)
                sp.dma_start(dram["q_lo"].rearrange("(f p) t -> p f t", p=P)[:, :, bass.ds(g * GT, GT)],
                             q_lo.bitcast(F32)).then_inc(q_stored, 16)
            sp.wait_ge(x1_stored, 16 * GROUPS)
            sp.wait_ge(q_stored, 32 * GROUPS)

        @block.tensor
        def _(pe):
            def modulation(m):
                k = [i for i, c in enumerate(chunks) if c[0] == "mod"][m]
                pe.wait_ge(raw_landed[staging[k]], 16 * landings(k))
                if m >= 2:
                    pe.wait_ge(mod_added, m - 1)
                for f in range(4):
                    for c in range(FC):
                        mm = pe.matmul(bank[:, m % 2, f * B:(f + 1) * B], raw[staging[k]][:, c, f * P:(f + 1) * P],
                                       sh.silu[:, c, :], start=(c == 0), stop=(c == FC - 1))
                mm.then_inc(mod_mm, 1)

            def turn_x(g, first=False):
                for j in range(GJ):
                    pe.wait_ge(ln_a, GJ * g + j + 1)
                    if j == 0 and not first:
                        pe.wait_ge(att_ready, UNITS * g)
                        pe.wait_ge(att_added, FC * g)
                    if j >= 2:
                        pe.wait_ge(xm_ready, GJ * g + j - 1)
                    for f in range(FC):
                        mm = pe.transpose(bank[:, 6 + j % 2, f * N:(f + 1) * N], x_tok[:, j, f * P:(f + 1) * P],
                                          sh.ident[0:N, 0:N])
                    mm.then_inc(x_turned, 1)

            def front(g):
                pe.wait_ge(silu_done, 1)
                modulation(0)
                modulation(1)
                turn_x(g, first=True)
                modulation(2)
                pe.wait_ge(w_lo_done, 3)
                pe.wait_ge(mod_added, 3)

            def body(g, last=False):
                def product_v(j):
                    product3(pe, bank[0:N, j, :],
                             lambda c: x_hi[:, c, j * N:(j + 1) * N], lambda c: x_lo[:, c, j * N:(j + 1) * N],
                             lambda c: w_hi["qkv"][:, c, 2 * D:3 * D], lambda c: w_lo["qkv"][:, c, 2 * D:3 * D],
                             FC).then_inc(v_mm, 1)

                def product_qk(n):
                    if n >= 2:
                        pe.wait_ge(qk_copied, 2 * FC * g + (1 if n == 2 else n))
                    if n == AHEAD + 4:
                        pe.wait_ge(att_added, FC * g + 1)
                    fs = slice(qk_tile(n) * P, (qk_tile(n) + 1) * P)
                    product3(pe, bank[:, qk_bank(n), 0:GT],
                             lambda c: w_hi["qkv"][:, c, fs], lambda c: w_lo["qkv"][:, c, fs],
                             lambda c: x_hi[:, c, :], lambda c: x_lo[:, c, :], FC).then_inc(qk_mm, 1)

                def scores(u):
                    if u % 2 == 0:
                        pe.wait_ge(qk_copied, 2 * FC * g + u + 2)
                    if u < 2:
                        pe.wait_ge(v_copied, GJ * g + GJ)
                    else:
                        pe.wait_ge(sub_done, UNITS * g + u - 1)
                    f = u // 2
                    for h in range(8):
                        j, r = h % 4, 32 * (unit_bank(u) + h // 4)
                        mm = pe.matmul(bank[0:N, unit_bank(u) + h // 4, j * N:(j + 1) * N],
                                       qk[r:r + 32, f, j * N:(j + 1) * N], qk[r:r + 32, FC + f, j * N:(j + 1) * N],
                                       start=True, stop=True)
                    mm.then_inc(s_mm, 1)

                def turn_probs(u):
                    pe.wait_ge(exp_done, UNITS * g + u + 1)
                    if u == 0:
                        pe.wait_ge(xn_lo, GJ * g)
                    else:
                        pe.wait_ge(p_copied, UNITS * g + u)
                    for h in range(8):
                        mm = pe.transpose(bank[0:N, 4 + h // 4, (h % 4) * N:(h % 4 + 1) * N], prob[u % 2][:, h, :],
                                          sh.ident[0:N, 0:N])
                    mm.then_inc(p_turned, 1)

                def weigh(u):
                    pe.wait_ge(p_copied, UNITS * g + u + 1)
                    if u == 0:
                        pe.wait_ge(qk_copied, 2 * FC * g + 2)
                    pe.wait_ge(att_ready, UNITS * g + u)
                    for h in range(8):
                        mm = pe.matmul(bank[0:N, 6, h * (HD + 1):(h + 1) * (HD + 1)],
                                       prob_t[u % 2][:, h // 4, (h % 4) * N:(h % 4 + 1) * N],
                                       v[:, h % 4, 4 * (u // 2) + unit_bank(u) + h // 4, :], start=True, stop=True)
                    mm.then_inc(pv_mm, 1)

                def turn_att(f):
                    pe.wait_ge(att_ready, UNITS * g + 2 * f + 2)
                    pe.wait_ge(qk_copied, 2 * FC * g + (AHEAD + 4 if f == 0 else 2 * FC))
                    if f >= 1:
                        pe.wait_ge(att_added, FC * g + f)
                    for j in range(GJ):
                        mm = pe.transpose(bank[:, 7, j * N:(j + 1) * N], att[:, j, f * P:(f + 1) * P], sh.ident[0:N, 0:N])
                    mm.then_inc(att_turned, 1)

                def project(c):
                    pe.wait_ge(att_split, 2 * FC * g + 2 * c + 2)
                    if c == 0:
                        pe.wait_ge(w_lo_done, 5)
                        pe.wait_ge(sub_done, UNITS * g + UNITS)
                    for f in range(FC):
                        out, fs = bank[:, f, 0:GT], slice(f * P, (f + 1) * P)
                        pe.matmul(out, w_hi["proj"][:, c, fs], a_hi[:, c, :], start=(c == 0), stop=False)
                        pe.matmul(out, w_hi["proj"][:, c, fs], a_lo[:, c, :], start=False, stop=False)
                        mm = pe.matmul(out, w_lo["proj"][:, c, fs], a_hi[:, c, :], start=False, stop=(c == FC - 1))
                        if c == FC - 1:
                            mm.then_inc(proj_mm, 1)

                pe.wait_ge(x_split, 2 * GJ * g + 2 * GJ)
                pe.wait_ge(xm_ready, GJ * g + GJ)
                product_qk(0)
                product_qk(1)
                for j in range(GJ):
                    if j == 0:
                        pe.wait_ge(q32_done, FC * g)
                    product_v(j)
                product_qk(2)
                scores(0)
                pe.wait_ge(ones_set, 1)
                for u in range(UNITS):
                    if u + 1 < UNITS:
                        scores(u + 1)
                    if AHEAD + u < 2 * FC:
                        product_qk(AHEAD + u)
                    if u >= 1:
                        weigh(u - 1)
                    turn_probs(u)
                    if u >= 3 and u % 2:
                        turn_att((u - 3) // 2)
                project(0)
                weigh(UNITS - 1)
                project(1)
                turn_att(FC - 1)
                project(2)
                project(3)
                if not last:
                    turn_x(g + 1)
                for j in range(GJ):
                    if j == 0:
                        pe.wait_ge(x1_ready, FC * g + FC)
                        pe.wait_ge(gated_done, FC * g + FC)
                    for f in range(FC):
                        mm = pe.transpose(bank[0:N, j, f * P:(f + 1) * P], xt[:, f, j * N:(j + 1) * N], sh.ident)
                    mm.then_inc(x1_turned, 1)
                for j in range(GJ):
                    pe.wait_ge(ln_b, GJ * g + j + 1)
                    if j < 2:
                        pe.wait_ge(p_copied, UNITS * g + UNITS)
                    else:
                        pe.wait_ge(xn_lo, GJ * g + j - 1)
                    for f in range(FC):
                        mm = pe.transpose(bank[:, 4 + j % 2, f * N:(f + 1) * N], xn[j % 2][:, f * P:(f + 1) * P],
                                          sh.ident[0:N, 0:N])
                    mm.then_inc(xn_back, 1)
                for f in range(FC):
                    if f == 0:
                        pe.wait_ge(xn_lo, GJ * g + GJ)
                    product3(pe, bank[:, f, 0:GT],
                             lambda c: w_hi["qc"][:, c, f * P:(f + 1) * P], lambda c: w_lo["qc"][:, c, f * P:(f + 1) * P],
                             lambda c: a_hi[:, c, :], lambda c: a_lo[:, c, :], FC).then_inc(q_mm, 1)

            groups(pe, front, body)

        @block.scalar
        def _(act):
            act.wait_ge(sh.consts, 48)
            act.activation(sh.silu, sh.cond, ACT.Silu).then_inc(silu_done, 1)

            def round_weights(kinds):
                for k, (kind, q) in enumerate(chunks):
                    if kind in kinds:
                        act.wait_ge(raw_landed[staging[k]], 16 * landings(k))
                        act.activation(w_hi[kind][:, :, q * 512:(q + 1) * 512], raw[staging[k]], ACT.Copy).then_inc(w_hi_done, 1)

            def front(g):
                round_weights(("qkv",))
                modulate(g)
                round_weights(("proj", "qc"))
                act.wait_ge(gate_bias, 2)

            def modulate(g):
                for j in range(GJ):
                    act.wait_ge(x_turned, GJ * g + j + 1)
                    if j == 0:
                        act.wait_ge(gp_ready, g + 1)
                        act.wait_ge(x_split, 2 * GJ * g)
                    for f in range(FC):
                        last = act.activation(xm[:, f, j * N:(j + 1) * N], bank[:, 6 + j % 2, f * N:(f + 1) * N],
                                              ACT.Identity, bias=gp[:, f, j:j + 1], scale=gp[:, 4 + f, j:j + 1])
                    last.then_inc(xm_ready, 1)

            def body(g, last=False):
                def copy_qk(n):
                    act.wait_ge(qk_mm, 2 * FC * g + n + 1)
                    if n == 0:
                        act.wait_ge(s_mm, UNITS * g)
                        act.wait_ge(q_stored, 32 * g)
                    act.activation(qk[:, qk_tile(n), :], bank[:, qk_bank(n), 0:GT], ACT.Identity,
                                   bias=sh.b("qk", qk_tile(n))).then_inc(qk_copied, 1)

                def exponentiate(u):
                    act.wait_ge(sub_done, UNITS * g + u + 1)
                    act.activation(prob[u % 2][:], prob[u % 2][:], ACT.Exp, scale=SCALE).then_inc(exp_done, 1)

                def copy_probs(u):
                    act.wait_ge(p_turned, UNITS * g + u + 1)
                    act.wait_ge(pv_mm, UNITS * g + (u - 1 if u >= 2 else 0))
                    act.activation(prob_t[u % 2][:], bank[0:N, 4:6, 0:4 * N], ACT.Copy).then_inc(p_copied, 1)

                def add_bias(f):
                    act.wait_ge(att_turned, FC * g + f + 1)
                    act.wait_ge(att_split, 2 * FC * g + 2 * f)
                    act.activation(att_t[:], bank[:, 7, 0:GT], ACT.Identity, bias=sh.b("v", f)).then_inc(att_added, 1)

                for n in range(AHEAD):
                    copy_qk(n)
                exponentiate(0)
                for u in range(UNITS):
                    if u + 1 < UNITS:
                        exponentiate(u + 1)
                    if AHEAD + u < 2 * FC:
                        copy_qk(AHEAD + u)
                    copy_probs(u)
                    if u >= 3 and u % 2:
                        add_bias((u - 3) // 2)
                add_bias(FC - 1)
                act.wait_ge(gate_ready, 2 * g + 2)
                for f in range(FC):
                    act.wait_ge(proj_mm, FC * g + f + 1)
                    act.wait_ge(x1_ready, FC * g + (f - 1 if f >= 2 else 0))
                    for j in range(GJ):
                        mm = act.activation(gated[f % 2][:, j * N:(j + 1) * N], bank[:, f, j * N:(j + 1) * N],
                                            ACT.Identity, bias=gate[:, 4 + f, j:j + 1], scale=gate[:, f, j:j + 1])
                    mm.then_inc(gated_done, 1)
                if not last:
                    modulate(g + 1)
                for j in range(GJ):
                    act.wait_ge(xn_back, GJ * g + j + 1)
                    act.activation(a_hi[:, :, j * N:(j + 1) * N],
                                   bank[:, 4 + j % 2, 0:GT].rearrange("p (f t) -> p f t", f=FC), ACT.Copy).then_inc(xn_hi, 1)
                for f in range(FC):
                    act.wait_ge(q_mm, FC * g + f + 1)
                    act.wait_ge(q_split, 2 * FC * g + (2 * f - 2 if f >= 2 else 0))
                    act.activation(q32[f % 2][:], bank[:, f, 0:GT], ACT.Identity, bias=sh.b_qc_scaled[:, f:f + 1],
                                   scale=SCALE).then_inc(q32_done, 1)

            groups(act, front, body)

        @block.vector
        def _(dve):
            dve.wait_ge(sh.consts, 48)
            dve.tensor_scalar(sh.b_qc_scaled, sh.bias[:, BIAS_OF["qc"]], SCALE, None, ALU.mult).then_inc(gate_bias, 1)
            def add_mod_bias(m):
                dve.wait_ge(mod_mm, m + 1)
                dve.tensor_tensor(sh.mod[:, 4 * m:4 * m + 4, :], bank[:, m % 2, 0:4 * B].rearrange("p (f b) -> p f b", f=4),
                                  sh.bias[:, 4 * m:4 * m + 4].unsqueeze(2).to_broadcast([P, 4, B]),
                                  ALU.add).then_inc(mod_added, 1)

            def split_weights(kinds):
                order = [(k, c) for k, c in enumerate(chunks) if c[0] != "mod"]
                for w, (k, (kind, q)) in enumerate(order):
                    if kind in kinds:
                        dve.wait_ge(w_hi_done, w + 1)
                        sl = slice(q * 512, (q + 1) * 512)
                        dve.tensor_tensor(w_lo[kind][:, :, sl], raw[staging[k]], w_hi[kind][:, :, sl].bitcast(F32),
                                          ALU.subtract).then_inc(w_lo_done, 1)

            def stats_of_x(g, j):
                dve.wait_ge(x_landed, 16 * g + 16)
                dve.bn_stats(stats_a[:, j, :], x_tok[:, j, :]).then_inc(st_a, 1)

            def rstd_of_x(g):
                wait_apart(dve, sh.consts, st_a, GJ * g + GJ)
                for j in range(GJ):
                    dve.bn_aggr(mean_var_a[:, j, :], stats_a[:, j, :]).then_inc(mv_a, 1)
                dve.wait_ge(mv_a, GJ * g + GJ)
                rsqrt(dve, rstd_done_a, RSQRT_STEPS * g, mean_var_a[:], var_eps_a[:], half_bits[:], rstd_a[:], newton_work[:])

            def normalise_x(g, js):
                dve.wait_ge(rstd_done_a, RSQRT_STEPS * g + RSQRT_STEPS)
                for j in js:
                    dve.tensor_scalar(x_tok[:, j, :], x_tok[:, j, :], mean_var_a[:, j, 0:1], rstd_a[:, j:j + 1],
                                      ALU.subtract, ALU.mult).then_inc(ln_a, 1)

            def split_x(g):
                for j in range(GJ):
                    sl = slice(j * N, (j + 1) * N)
                    dve.wait_ge(xm_ready, GJ * g + j + 1)
                    if j == 0:
                        dve.wait_ge(qk_mm, 2 * FC * g)
                    dve.tensor_copy(x_hi[:, :, sl], xm[:, :, sl]).then_inc(x_split, 1)
                    dve.wait_ge(x_split, 2 * GJ * g + 2 * j + 1)
                    dve.tensor_tensor(x_lo[:, :, sl], xm[:, :, sl], x_hi[:, :, sl].bitcast(F32),
                                      ALU.subtract).then_inc(x_split, 1)

            def front(g):
                for j in range(GJ):
                    stats_of_x(g, j)
                rstd_of_x(g)
                normalise_x(g, range(GJ))
                add_mod_bias(0)
                add_mod_bias(1)
                dve.wait_ge(mod_added, 2)
                dve.tensor_scalar(sh.mod[:, 4:8, :], sh.mod[:, 4:8, :], 1.0, None, ALU.add).then_inc(mod_one, 1)
                split_weights(("qkv",))
                split_x(g)
                add_mod_bias(2)
                dve.wait_ge(mod_added, 3)
                dve.tensor_tensor(sh.gate_bias[:, 0:4, :], sh.mod[:, 8:12, :],
                                  sh.bias[:, BIAS_OF["proj"]].unsqueeze(2).to_broadcast([P, 4, B]),
                                  ALU.mult).then_inc(gate_bias, 1)
                split_weights(("proj", "qc"))

            def body(g, last=False):
                for j in range(GJ):
                    dve.wait_ge(v_mm, GJ * g + j + 1)
                    dve.tensor_copy(v[:, j, :, 0:HD], bank[0:N, j, :].rearrange("p (h d) -> p h d", h=NH)).then_inc(v_copied, 1)

                def soften(u):
                    s = bank[0:N, unit_bank(u):unit_bank(u) + 2, 0:4 * N].rearrange("p b (h k) -> p b h k", h=4)
                    dve.wait_ge(s_mm, UNITS * g + u + 1)
                    dve.tensor_reduce(top[:, u % 2, :].rearrange("p (b h) -> p b h", b=2), s, AX.X, ALU.max).then_inc(top_done, 1)
                    dve.wait_ge(top_done, UNITS * g + u + 1)
                    dve.wait_ge(p_turned, UNITS * g + (u - 1 if u >= 2 else 0))
                    dve.tensor_tensor(prob[u % 2][:].rearrange("p (b h) k -> p b h k", b=2), s,
                                      top[:, u % 2, :].rearrange("p (b h) -> p b h", b=2).unsqueeze(3).to_broadcast([N, 2, 4, N]),
                                      ALU.subtract).then_inc(sub_done, 1)

                def normalise(u):
                    o = bank[0:N, 6, 0:8 * (HD + 1)].rearrange("p (h d) -> p h d", h=8)
                    head = 4 * (u // 2) + unit_bank(u)
                    dve.wait_ge(pv_mm, UNITS * g + u + 1)
                    dve.reciprocal(recip[:, u % 2, :], o[:, :, HD]).then_inc(recip_done, 1)
                    dve.wait_ge(recip_done, UNITS * g + u + 1)
                    dve.wait_ge(att_turned, FC * g)
                    dve.tensor_tensor(att[:].rearrange("p j (h d) -> p h j d", h=NH)[:, head:head + 2],
                                      o[:, :, 0:HD].rearrange("p (r j) d -> p r j d", r=2),
                                      recip[:, u % 2, :].rearrange("p (r j) -> p r j", r=2).unsqueeze(3).to_broadcast([N, 2, 4, HD]),
                                      ALU.mult).then_inc(att_ready, 1)

                def split_att(f):
                    dve.wait_ge(att_added, FC * g + f + 1)
                    if f == 0:
                        dve.wait_ge(q_mm, FC * g)
                    dve.tensor_copy(a_hi[:, f, :], att_t[:]).then_inc(att_split, 1)
                    dve.wait_ge(att_split, 2 * FC * g + 2 * f + 1)
                    dve.tensor_tensor(a_lo[:, f, :], att_t[:], a_hi[:, f, :].bitcast(F32), ALU.subtract).then_inc(att_split, 1)

                for u in range(UNITS):
                    soften(u)
                    if u >= 2:
                        normalise(u - 2)
                    if u >= 5 and u % 2:
                        split_att((u - 5) // 2)
                    if not last:
                        if 1 <= u <= GJ:
                            stats_of_x(g + 1, u - 1)
                        if u == GJ + 1:
                            rstd_of_x(g + 1)
                        if u >= GJ + 2:
                            normalise_x(g + 1, (0, 1) if u == GJ + 2 else (2, 3))
                normalise(UNITS - 2)
                split_att(FC - 2)
                normalise(UNITS - 1)
                split_att(FC - 1)
                for f in range(FC):
                    dve.wait_ge(gated_done, FC * g + f + 1)
                    if f == 0:
                        dve.wait_ge(xt_landed, 16 * g + 16)
                    dve.tensor_tensor(xt[:, f, :], xt[:, f, :], gated[f % 2][:], ALU.add).then_inc(x1_ready, 1)
                for j in range(GJ):
                    dve.wait_ge(x1_turned, GJ * g + j + 1)
                    dve.bn_stats(stats_b[:, j, :], bank[0:N, j, :]).then_inc(st_b, 1)
                wait_apart(dve, sh.consts, st_b, GJ * g + GJ)
                for j in range(GJ):
                    dve.bn_aggr(mean_var_b[:, j, :], stats_b[:, j, :]).then_inc(mv_b, 1)
                dve.wait_ge(mv_b, GJ * g + GJ)
                rsqrt(dve, rstd_done_b, RSQRT_STEPS * g, mean_var_b[:], var_eps_b[:], half_bits[:], rstd_b[:], newton_work[:])
                dve.wait_ge(rstd_done_b, RSQRT_STEPS * g + RSQRT_STEPS)

                def lo_back(j):
                    sl = slice(j * N, (j + 1) * N)
                    dve.wait_ge(xn_hi, GJ * g + j + 1)
                    dve.tensor_tensor(a_lo[:, :, sl], bank[:, 4 + j % 2, 0:GT].rearrange("p (f t) -> p f t", f=FC),
                                      a_hi[:, :, sl].bitcast(F32), ALU.subtract).then_inc(xn_lo, 1)

                for j in range(GJ):
                    if j >= 2:
                        dve.wait_ge(xn_back, GJ * g + j - 1)
                    dve.tensor_scalar(xn[j % 2][:], bank[0:N, j, :], mean_var_b[:, j, 0:1], rstd_b[:, j:j + 1],
                                      ALU.subtract, ALU.mult).then_inc(ln_b, 1)
                    if j >= 1:
                        lo_back(j - 1)
                lo_back(GJ - 1)
                if not last:
                    split_x(g + 1)
                for f in range(FC):
                    dve.wait_ge(q32_done, FC * g + f + 1)
                    dve.tensor_copy(q_hi[:, f, :], q32[f % 2][:]).then_inc(q_split, 1)
                    dve.wait_ge(q_split, 2 * FC * g + 2 * f + 1)
                    dve.tensor_tensor(q_lo[:, f, :], q32[f % 2][:], q_hi[:, f, :].bitcast(F32), ALU.subtract).then_inc(q_split, 1)

            groups(dve, front, body)

        @block.gpsimd
        def _(pool):
            pool.memset(v[:, :, :, HD:HD + 1], 1.0).then_inc(ones_set, 1)
            def load_x(g):
                pool.dma_start(x_tok[:], dram["x_tok"][:, bass.ds(g * GJ, GJ), :]).then_inc(x_landed, 16)

            def copy_modulation(g):
                pool.tensor_copy(gp[:], sh.mod[:, 0:8, bass.ds(g * GJ, GJ)]).then_inc(gp_ready, 1)

            def front(g):
                load_x(g)
                pool.wait_ge(mod_one, 1)
                copy_modulation(g)
                pool.wait_ge(gate_bias, 2)

            def body(g, last=False):
                wait_apart(pool, sh.consts, gated_done, FC * g)
                pool.tensor_copy(gate[:, 0:4, :], sh.mod[:, 8:12, bass.ds(g * GJ, GJ)]).then_inc(gate_ready, 1)
                pool.tensor_copy(gate[:, 4:8, :], sh.gate_bias[:, 0:4, bass.ds(g * GJ, GJ)]).then_inc(gate_ready, 1)
                if not last:
                    wait_apart(pool, sh.consts, x_turned, GJ * g + GJ)
                    load_x(g + 1)
                    wait_apart(pool, sh.consts, xm_ready, GJ * g + GJ)
                    copy_modulation(g + 1)

            groups(pool, front, body)


def cross_attention_stage(nc, sh, dram):
    TILES = [(t * P, min(P, S - t * P)) for t in range((S + P - 1) // P)]
    CT = len(TILES)
    HALF = S // 2
    LN_SLOT = 7
    WIDE = HALF + 1
    V_UNITS = [(t, c) for t in range(CT) for c in range(FC)]
    V_SLOTS = [4, 5, 6, 7, 12, 13, 14, 15]
    V_SHARE = len(V_UNITS) // len(V_SLOTS)
    SLOTS = {0: ["K2a"], 1: ["K2b"], 2: ["K3a"], 3: ["T0", "K3b"], 8: ["T5", "K0a"], 9: ["K0b"], 10: ["K1a"], 11: ["K1b"]}
    for _i, _s in enumerate(V_SLOTS):
        SLOTS[_s] = [f"T{_s - 3}"] if _s < 8 else []
        SLOTS[_s] += [f"V{t}{c}" for t, c in V_UNITS[_i * V_SHARE:(_i + 1) * V_SHARE]]
    ENDS = {s: [x[:2] if x[0] == "V" else x for x in work if x[0] != "V" or int(x[2]) == FC - 1]
            for s, work in SLOTS.items()}
    ORDER = [x for s in range(NH) for x in ENDS[s]]
    OWN = ["K2a", "K2b", "K3a", "K3b"]
    SPLIT = [x for x in ORDER if x[0] != "V"]
    VS = [x for x in ORDER if x[0] == "V"]
    BIG = [x for x in ORDER if x[0] != "T"]

    def done(seq, b, x):
        at = seq.index(x)
        if isinstance(b, int) and b < 0:
            return len([y for y in seq[:at + 1] if y not in OWN])
        if isinstance(b, int) and b == B - 1:
            return len(seq) * B - len(OWN) + len([y for y in seq[:at + 1] if y in OWN])
        return len(seq) * (b + 1) - len(OWN) + at + 1

    def pieces_done(b, x):
        return done(ORDER, b, x)

    def splits_done(b, x):
        return done(SPLIT, b, x)

    def vs_done(b, x):
        return len(VS) * (b + 1) + VS.index(x) + 1

    with ExitStack() as ctx:
        def sb(name, shape, dt=F32):
            return ctx.enter_context(nc.sbuf_tensor(name, shape, dt))

        def sem(name):
            return ctx.enter_context(nc.semaphore(name))

        bank = ctx.enter_context(nc.psum_tensor("bank2", [P, 8, 512], F32))
        PROBS_T, PIECES, OUT, TURNED = 2, 4, 6, 7
        wkv_hi = sb("wkv_hi", [P, FC, 2 * D], F32R)
        wkv_lo = sb("wkv_lo", [P, FC, 2 * D], F32R)
        c_raw = sb("c_raw", [P, CT, D])
        c_norm = sb("c_norm", [P, CT, D])
        c_hi = sb("c_hi", [P, FC, S], F32R)
        c_lo = sb("c_lo", [P, FC, S], F32R)
        stats = sb("stats2", [P, CT, 6])
        mean_var = sb("mean_var2", [P, CT, 2])
        var_eps = sb("var_eps2", [P, CT])
        half_bits = sb("half_bits2", [P, CT], I32)
        rstd = sb("rstd2", [P, CT])
        newton_work = sb("newton_work2", [P, CT])
        neg_mean = sb("neg_mean2", [P, CT])
        k_hi = sb("k_hi", [P, 2, S], F32R)
        k_lo = sb("k_lo", [P, 2, S], F32R)
        k_stack = sb("k_stack", [3 * HD, NH, S + 1], F32R)
        q_stack = sb("q_stack", [3 * HD, NH, N], F32R)
        v_next = sb("v_next", [P, CT, D])
        v_now = sb("v_now", [P, CT, D])
        neg_top = sb("neg_top", [N, NH])
        total = sb("total", [N, NH])
        recip = sb("recip2", [N, NH])
        prob = [sb(f"prob2_{i}", [N, S]) for i in range(2)]
        prob_t = [sb(f"prob_t2_{i}", [P, CT, N]) for i in range(4)]
        out_t = sb("out_t", [P, FC, N])
        att = sb("att2", [N, D])

        w_hi_done, w_lo_done, cleared = sem("w_hi_done2"), sem("w_lo_done2"), sem("cleared")
        ctx_landed = [sem(f"ctx_landed{t}") for t in range(CT)]
        k_landed = [sem(f"k_landed{f}") for f in range(FC)]
        q_landed = [sem(f"q_landed{i}") for i in range(2)]
        att_stored = sem("att_stored")
        st_done, mv_done, seed_done, newton_done, ctx_normed = (
            sem(n) for n in ("st_done", "mv_done", "seed_done", "newton_done", "ctx_normed"))
        piece_mm, hi_done, lo_done, v_copied = (sem(n) for n in ("piece_mm", "hi_done", "lo_done", "v_copied2"))
        v_moved = [sem(f"v_moved{i}") for i in range(2)]
        s_mm, top_done, exp_done, p_turned, p_copied_dve, p_copied_act, pv_mm = (
            sem(n) for n in ("s_mm2", "top_done2", "exp_done2", "p_turned2", "p_copied_dve", "p_copied_act", "pv_mm2"))
        recip_done, out_taken, out_turned, att_ready = (
            sem(n) for n in ("recip_done2", "out_taken", "out_turned", "att_ready2"))
        mod_landed = [sem(f"mod_landed{i}") for i in range(2)]
        mod_mm, mod_added = sem("mod_mm2"), sem("mod_added2")

        def steps(eng, step, modulation=None):
            step(-1)
            if modulation:
                modulation()
            step(0)
            with eng.Fori(1, B - 2) as b:
                step(b)
            step(B - 2, last_ln=True)
            step(B - 1, last_ln=True, last=True)

        def own(b, last, x):
            if x in OWN:
                return not is_first(b)
            return not last

        def big_before(b, s, last):
            if s > 0:
                return [(b, x) for x in ENDS[s - 1] if x[0] != "T" and own(b, last, x)]
            return [] if is_first(b) else [(b - 1, x) for x in ENDS[NH - 1]]

        def turned_now(b, s, last):
            return [x for x in ENDS[s] if x[0] == "T" and own(b, last, x)]

        def is_first(b):
            return isinstance(b, int) and b < 0

        def is_int(b, n):
            return isinstance(b, int) and b == n

        def piece_bank(x):
            return TURNED if x[0] == "T" else PIECES + BIG.index(x) % 2

        block = ctx.enter_context(nc.Block())

        @block.sync
        def _(sp):
            def load_ctx(m, t):
                at, n = TILES[t]
                sp.dma_start(c_raw[0:n, t, :], dram["ctx"][bass.ds(m, 1), at:at + n, :].rearrange("b s d -> (b s) d")
                             ).then_inc(ctx_landed[t], 16)

            def load_q(b, half):
                hs = slice(8 * half, 8 * half + 8)
                for i, name in enumerate(("q_hi", "q_hi", "q_lo")):
                    sp.dma_start(q_stack[i * HD:(i + 1) * HD, hs, :].bitcast(F32),
                                 dram[name].rearrange("(h d) t -> d h t", d=HD)[:, hs, bass.ds(b * N, N)]
                                 ).then_inc(q_landed[half], 16)

            def stack_k(f):
                for r in range(4):
                    rows = slice(r * HD, (r + 1) * HD)
                    for i, part in enumerate((k_hi, k_lo, k_hi)):
                        sp.dma_start(k_stack[i * HD:(i + 1) * HD, 4 * f + r, 1:S + 1].bitcast(F32),
                                     part[rows, f % 2, :].bitcast(F32)).then_inc(k_landed[f], 16)

            def step(b, last_ln=False, last=False):
                first = is_first(b)
                if not first:
                    sp.wait_ge(s_mm, NH * b)
                    load_q(b, 1)
                if not last_ln:
                    for t in range(CT):
                        sp.wait_ge(ctx_normed, CT * (b + 2))
                        load_ctx(b + 2, t)
                if not first:
                    wait_apart(sp, sh.consts, lo_done, splits_done(b, "K2b"))
                    if not is_int(b, 0):
                        sp.wait_ge(s_mm, NH * b - 4)
                    stack_k(2)
                    sp.wait_ge(lo_done, splits_done(b, "K3b"))
                    stack_k(3)
                    if not is_int(b, 0):
                        sp.wait_ge(att_ready, b)
                        sp.dma_start(dram["att"][:, bass.ds(b - 1, 1), :].rearrange("p b d -> p (b d)"), att[:]
                                     ).then_inc(att_stored, 16)
                if not last:
                    if not first:
                        sp.wait_ge(s_mm, NH * b + 8)
                    load_q(b + 1, 0)
                    for f in range(2):
                        sp.wait_ge(lo_done, splits_done(b, f"K{f}b"))
                        stack_k(f)

            def load_modulation():
                sp.wait_ge(mod_mm, 1)
                sp.dma_start(sh.raw[:, 0], dram["w_mod"][:, :, 5 * 512:6 * 512]).then_inc(mod_landed[0], 16)
                sp.wait_ge(mod_mm, 2)
                sp.dma_start(sh.raw[:, 1], dram["w_cproj"]).then_inc(mod_landed[1], 16)

            for t in range(CT):
                load_ctx(0, t)
            for q in range(2):
                sp.wait_ge(w_lo_done, q + 1)
                sp.dma_start(sh.raw[:, q], dram["w_mod"][:, :, (3 + q) * 512:(4 + q) * 512]).then_inc(mod_landed[q], 16)
            steps(sp, step, load_modulation)
            sp.wait_ge(att_ready, B)
            sp.dma_start(dram["att"][:, B - 1, :], att[:]).then_inc(att_stored, 16)
            sp.wait_ge(att_stored, 16 * B)
            sp.wait_ge(mod_landed[1], 32)

        @block.tensor
        def _(pe):
            pe.wait_ge(w_lo_done, 2)
            pe.wait_ge(cleared, 3)

            def bank_freed(b, x):
                if x[0] == "T":
                    if x != "T0":
                        pe.wait_ge(lo_done, splits_done(b, f"T{int(x[1]) - 1}"))
                    elif not is_first(b) and not is_int(b, 0):
                        pe.wait_ge(att_ready, b)
                    return
                at = BIG.index(x)
                if is_first(b) and at < len(OWN) + 2:
                    return
                before, its_step = BIG[at - 2], (b if at >= 2 else b - 1)
                if before[0] == "V":
                    pe.wait_ge(v_copied, vs_done(its_step, before))
                else:
                    pe.wait_ge(lo_done, splits_done(its_step, before))

            def piece(b, x):
                if x[0] == "T":
                    t = int(x[1])
                    n = TILES[t][1]
                    bank_freed(b, x)
                    pe.wait_ge(ctx_normed, CT * (b + 1) + t + 1)
                    for c in range(FC):
                        mm = pe.transpose(bank[:, TURNED, c * P:c * P + n], c_norm[0:n, t, c * P:(c + 1) * P], sh.ident[0:n, 0:n])
                elif x[0] == "V":
                    t, c = int(x[1]), int(x[2])
                    at_t, n = TILES[t]
                    out = bank[0:n, piece_bank(x[:2]), :]
                    if c == 0:
                        bank_freed(b, x[:2])
                        pe.wait_ge(lo_done, splits_done(b, f"T{t}"))
                    pe.matmul(out, c_hi[:, c, at_t:at_t + n], wkv_hi[:, c, D:], start=(c == 0), stop=False)
                    pe.matmul(out, c_hi[:, c, at_t:at_t + n], wkv_lo[:, c, D:], start=False, stop=False)
                    mm = pe.matmul(out, c_lo[:, c, at_t:at_t + n], wkv_hi[:, c, D:], start=False, stop=(c == FC - 1))
                    if c < FC - 1:
                        return
                else:
                    f, half = int(x[1]), "ab".index(x[2])
                    at_k = half * (S - WIDE)
                    bank_freed(b, x)
                    if x[1] == "0":
                        pe.wait_ge(lo_done, splits_done(b, f"T{(at_k + WIDE - 1) // P}"))
                    mm = product3(pe, bank[:, piece_bank(x), 0:WIDE],
                                  lambda c: wkv_hi[:, c, f * P:(f + 1) * P], lambda c: wkv_lo[:, c, f * P:(f + 1) * P],
                                  lambda c: c_hi[:, c, at_k:at_k + WIDE], lambda c: c_lo[:, c, at_k:at_k + WIDE], FC)
                mm.then_inc(piece_mm, 1)

            def scores(b, h):
                if h % 8 == 0:
                    pe.wait_ge(q_landed[h // 8], 48 * (b + 1))
                if h % 4 == 0:
                    pe.wait_ge(k_landed[h // 4], 192 * (b + 1))
                if not (is_int(b, 0) and h == 0):
                    pe.wait_ge(exp_done, NH * b + h)
                for half in range(2):
                    mm = pe.matmul(bank[0:N, half, 0:WIDE], q_stack[:, h, :], k_stack[:, h, half * HALF:half * HALF + WIDE],
                                   start=True, stop=True)
                mm.then_inc(s_mm, 1)

            def turn_probs(n, h):
                pe.wait_ge(exp_done, n + 1)
                if not is_int(n, 0):
                    pe.wait_ge(p_copied_dve, n)
                    pe.wait_ge(p_copied_act, n)
                for t, (at, rows) in enumerate(TILES):
                    mm = pe.transpose(bank[0:rows, PROBS_T + t // 3, (t % 3) * N:(t % 3 + 1) * N],
                                      prob[h % 2][:, at:at + rows], sh.ident[0:N, 0:N])
                mm.then_inc(p_turned, 1)

            def weigh(b, g):
                pe.wait_ge(p_copied_dve, NH * b + 4 * g + 4)
                pe.wait_ge(p_copied_act, NH * b + 4 * g + 4)
                if g % 2 == 0:
                    pe.wait_ge(v_moved[g // 2], b + 1)
                if g == 0 and not is_int(b, 0):
                    pe.wait_ge(out_taken, b)
                for t, (at, rows) in enumerate(TILES):
                    for j in range(4):
                        h = 4 * g + j
                        mm = pe.matmul(bank[j * HD:(j + 1) * HD, OUT, g * N:(g + 1) * N], v_now[0:rows, t, h * HD:(h + 1) * HD],
                                       prob_t[j][0:rows, t, :], start=(t == 0), stop=(t == CT - 1), tile_position=(0, j * HD))
                mm.then_inc(pv_mm, 1)

            def turn_out(b, t5_step):
                pe.wait_ge(out_taken, b + 1)
                pe.wait_ge(lo_done, splits_done(t5_step, "T5"))
                for f in range(FC):
                    mm = pe.transpose(bank[0:N, TURNED, f * P:(f + 1) * P], out_t[:, f, :], sh.ident)
                mm.then_inc(out_turned, 1)

            def step(b, last_ln=False, last=False):
                for s in range(NH):
                    if not is_first(b):
                        scores(b, s)
                        if s >= 1:
                            turn_probs(NH * b + s - 1, s - 1)
                        elif not is_int(b, 0):
                            turn_probs(NH * b - 1, NH - 1)
                        if s == 2 and not is_int(b, 0):
                            turn_out(b - 1, b - 1)
                    for x in SLOTS[s]:
                        if own(b, last, x):
                            piece(b, x)
                    if is_first(b):
                        continue
                    if s % 4 == 0 and s > 0:
                        weigh(b, s // 4 - 1)
                    elif s == 0 and not is_int(b, 0):
                        weigh(b - 1, 3)

            def modulation():
                for m in range(3):
                    pe.wait_ge(mod_landed[m % 2], 16 * (m // 2 + 1))
                    if m == 2:
                        pe.wait_ge(mod_added, 1)
                    for f in range(4):
                        for c in range(FC):
                            mm = pe.matmul(bank[:, OUT + m % 2, f * B:(f + 1) * B], sh.raw[:, m % 2, c, f * P:(f + 1) * P],
                                           sh.silu[:, c, :], start=(c == 0), stop=(c == FC - 1))
                    mm.then_inc(mod_mm, 1)
                pe.wait_ge(mod_added, 3)

            steps(pe, step, modulation)
            turn_probs(NH * B - 1, NH - 1)
            weigh(B - 1, 3)
            turn_out(B - 1, B - 2)

        @block.scalar
        def _(act):
            for q in range(2):
                act.wait_ge(sh.kv_landed[q], 16)
                act.activation(wkv_hi[:, :, q * 512:(q + 1) * 512], sh.raw[:, q], ACT.Copy).then_inc(w_hi_done, 1)

            def take(b, x):
                src = bank[:, piece_bank(x), :]
                act.wait_ge(piece_mm, pieces_done(b, x))
                if x[0] == "T":
                    at, n = TILES[int(x[1])]
                    act.activation(c_hi[:, :, at:at + n], src.rearrange("p (c s) -> p c s", c=FC)[:, :, 0:n],
                                   ACT.Copy).then_inc(hi_done, 1)
                elif x[0] == "V":
                    n = TILES[int(x[1])][1]
                    if x == "V0":
                        act.wait_ge(v_moved[1], b + 1)
                        act.wait_ge(v_moved[0], b + 1)
                    act.activation(v_next[0:n, int(x[1]), :], src[0:n, :], ACT.Copy).then_inc(v_copied, 1)
                else:
                    f, half = int(x[1]), "ab".index(x[2])
                    if half == 0 and not (is_first(b)) and f < 2:
                        act.wait_ge(k_landed[f + 2], 192 * (b + 1))
                    if half == 0 and f >= 2:
                        act.wait_ge(k_landed[f - 2], 192 * (b + 1))
                    act.activation(k_hi[:, f % 2, half * HALF:(half + 1) * HALF], src[:, half:half + HALF],
                                   ACT.Identity, bias=sh.b("kc", f)).then_inc(hi_done, 1)

            def soften(b, h):
                act.wait_ge(top_done, NH * b + h + 1)
                if not (is_int(b, 0) and h < 2):
                    act.wait_ge(p_turned, NH * b + h - 1)
                if h % 8 == 0 and not is_int(b, 0):
                    act.wait_ge(recip_done, 2 * b - 1 + h // 8)
                act.activation(prob[h % 2][:].rearrange("p (a k) -> p a k", a=2), bank[0:N, 0:2, 1:1 + HALF], ACT.Exp,
                               bias=neg_top[:, h:h + 1], accum_out=total[:, h:h + 1]).then_inc(exp_done, 1)

            def copy_probs(b, h):
                act.wait_ge(p_turned, NH * b + h + 1)
                if not (is_int(b, 0) and h < 4):
                    act.wait_ge(pv_mm, 4 * b + h // 4)
                act.activation(prob_t[h % 4][:, 3:6, :], bank[:, PROBS_T + 1, 0:3 * N].rearrange("p (t q) -> p t q", t=3),
                               ACT.Copy).then_inc(p_copied_act, 1)

            def step(b, last_ln=False, last=False):
                for s in range(NH):
                    for its_step, x in big_before(b, s, last):
                        take(its_step, x)
                    if not is_first(b):
                        if s >= 1:
                            copy_probs(b, s - 1)
                        elif not is_int(b, 0):
                            copy_probs(b - 1, NH - 1)
                    for x in turned_now(b, s, last):
                        take(b, x)
                    if not is_first(b):
                        soften(b, s)

            act.wait_ge(cleared, 3)
            steps(act, step)
            copy_probs(B - 1, NH - 1)

        @block.vector
        def _(dve):
            for q in range(2):
                sl = slice(q * 512, (q + 1) * 512)
                dve.wait_ge(w_hi_done, q + 1)
                dve.tensor_tensor(wkv_lo[:, :, sl], sh.raw[:, q], wkv_hi[:, :, sl].bitcast(F32), ALU.subtract).then_inc(w_lo_done, 1)
            dve.memset(bank[:, PROBS_T + 1, :], 0.0).then_inc(cleared, 1)

            def ln_stats(m, t):
                n = TILES[t][1]
                dve.wait_ge(ctx_landed[t], 16 * (m + 1))
                dve.bn_stats(stats[0:n, t, :], c_raw[0:n, t, :]).then_inc(st_done, 1)

            def ln_seed(m):
                dve.wait_ge(st_done, CT * (m + 1))
                if not is_int(m, 0):
                    wait_apart(dve, sh.consts, ctx_normed, CT * m)
                for t in range(CT):
                    n = TILES[t][1]
                    dve.bn_aggr(mean_var[0:n, t, :], stats[0:n, t, :]).then_inc(mv_done, 1)
                dve.wait_ge(mv_done, CT * (m + 1))
                seed_rsqrt(dve, seed_done, SEED_STEPS * m, mean_var[:], var_eps[:], half_bits[:], rstd[:])

            def take(b, x):
                if x[0] == "V":
                    return
                src = bank[:, piece_bank(x), :]
                dve.wait_ge(hi_done, splits_done(b, x))
                if x[0] == "T":
                    at, n = TILES[int(x[1])]
                    dve.tensor_tensor(c_lo[:, :, at:at + n], src.rearrange("p (c s) -> p c s", c=FC)[:, :, 0:n],
                                      c_hi[:, :, at:at + n].bitcast(F32), ALU.subtract).then_inc(lo_done, 1)
                else:
                    f, half = int(x[1]), "ab".index(x[2])
                    sl = slice(half * HALF, (half + 1) * HALF)
                    dve.scalar_tensor_tensor(out=k_lo[:, f % 2, sl], in0=src[:, half:half + HALF], scalar=sh.b("kc", f),
                                             in1=k_hi[:, f % 2, sl].bitcast(F32), op0=ALU.add, op1=ALU.subtract
                                             ).then_inc(lo_done, 1)

            def top(b, h):
                dve.wait_ge(s_mm, NH * b + h + 1)
                dve.tensor_reduce(neg_top[:, h:h + 1], bank[0:N, 0:2, 1:1 + HALF], AX.XY, ALU.max, negate=True).then_inc(top_done, 1)

            def copy_probs(b, h):
                dve.wait_ge(p_turned, NH * b + h + 1)
                if not (is_int(b, 0) and h < 4):
                    dve.wait_ge(pv_mm, 4 * b + h // 4)
                dve.tensor_copy(prob_t[h % 4][:, 0:3, :], bank[:, PROBS_T, 0:3 * N].rearrange("p (t q) -> p t q", t=3)
                                ).then_inc(p_copied_dve, 1)

            def invert_totals(b, half):
                hs = slice(8 * half, 8 * half + 8)
                dve.wait_ge(exp_done, NH * b + 8 * half + 8)
                dve.reciprocal(recip[:, hs], total[:, hs]).then_inc(recip_done, 1)

            def take_out(b):
                dve.wait_ge(pv_mm, 4 * b + 4)
                dve.tensor_copy(out_t[:], bank[:, OUT, 0:FC * N].rearrange("p (f t) -> p f t", f=FC)).then_inc(out_taken, 1)

            def normalise(b):
                dve.wait_ge(out_turned, b + 1)
                dve.wait_ge(recip_done, 2 * b + 2)
                if not is_int(b, 0):
                    dve.wait_ge(att_stored, 16 * b)
                dve.tensor_tensor(att[:].rearrange("p (h d) -> p h d", h=NH),
                                  bank[0:N, TURNED, :].rearrange("p (h d) -> p h d", h=NH),
                                  recip[:].unsqueeze(2).to_broadcast([N, NH, HD]), ALU.mult).then_inc(att_ready, 1)

            def step(b, last_ln=False, last=False):
                for s in range(NH):
                    again = not is_first(b) and not is_int(b, 0)
                    if not is_first(b):
                        top(b, s)
                    if s == 1 and again:
                        take_out(b - 1)
                    for its_step, x in big_before(b, s, last):
                        take(its_step, x)
                    if not is_first(b):
                        if s >= 1:
                            copy_probs(b, s - 1)
                        elif again:
                            copy_probs(b - 1, NH - 1)
                    if s == 1 and again:
                        invert_totals(b - 1, 1)
                    if s == 2 and again:
                        normalise(b - 1)
                    for x in turned_now(b, s, last):
                        take(b, x)
                    if s == 9 and not is_first(b):
                        invert_totals(b, 0)
                    if not last_ln:
                        if LN_SLOT <= s < LN_SLOT + CT:
                            ln_stats(b + 2, s - LN_SLOT)
                        if s == LN_SLOT + CT:
                            ln_seed(b + 2)

            dve.wait_ge(cleared, 3)
            for t in range(CT):
                ln_stats(0, t)
            ln_seed(0)
            def modulation():
                for m in range(3):
                    dve.wait_ge(mod_mm, m + 1)
                    dve.tensor_tensor(sh.mod[:, 12 + 4 * m:16 + 4 * m, :],
                                      bank[:, OUT + m % 2, 0:4 * B].rearrange("p (f b) -> p f b", f=4),
                                      sh.bias[:, 12 + 4 * m:16 + 4 * m].unsqueeze(2).to_broadcast([P, 4, B]),
                                      ALU.add).then_inc(mod_added, 1)
                dve.wait_ge(mod_added, 3)
                dve.tensor_scalar(sh.mod[:, 16:20, :], sh.mod[:, 16:20, :], 1.0, None, ALU.add)
                dve.tensor_tensor(sh.gate_bias[:, 4:8, :], sh.mod[:, 20:24, :],
                                  sh.bias[:, BIAS_OF["mlp2"]].unsqueeze(2).to_broadcast([P, 4, B]), ALU.mult)

            steps(dve, step, modulation)
            copy_probs(B - 1, NH - 1)
            invert_totals(B - 1, 1)
            take_out(B - 1)
            normalise(B - 1)

        @block.gpsimd
        def _(pool):
            pool.memset(k_stack[:, :, 0:1].bitcast(F32), 0.0)
            pool.memset(mean_var[:, CT - 1, :], 1.0).then_inc(cleared, 1)
            pool.memset(v_next[:, CT - 1, :], 0.0).then_inc(cleared, 1)

            def normalise_ctx(m):
                wait_apart(pool, sh.consts, seed_done, SEED_STEPS * (m + 1))
                newton_rsqrt(pool, sh.consts, newton_done, NEWTON_STEPS * m, mean_var[:], var_eps[:], rstd[:],
                             newton_work[:], neg_mean[:])
                pool.wait_ge(newton_done, NEWTON_STEPS * (m + 1))
                for t, (at, n) in enumerate(TILES):
                    if not is_int(m, 0):
                        wait_apart(pool, sh.consts, piece_mm, pieces_done(m - 2, f"T{t}"))
                    pool.tensor_scalar(c_norm[0:n, t, :], c_raw[0:n, t, :], neg_mean[0:n, t:t + 1], rstd[0:n, t:t + 1],
                                       ALU.add, ALU.mult).then_inc(ctx_normed, 1)

            def move_v(b, half):
                pool.wait_ge(v_copied, CT * (b + 1))
                if not is_int(b, 0):
                    wait_apart(pool, sh.consts, pv_mm, 4 * (b - 1) + 2 * half + 2)
                pool.tensor_copy(v_now[:, :, 256 * half:256 * half + 256], v_next[:, :, 256 * half:256 * half + 256]
                                 ).then_inc(v_moved[half], 1)

            def step(b, last_ln=False, last=False):
                if not is_first(b):
                    move_v(b, 1)
                if not last_ln:
                    normalise_ctx(b + 2)
                if not last:
                    move_v(b + 1, 0)

            normalise_ctx(0)
            steps(pool, step)


def mlp_stage(nc, sh, dram):
    GJ = GROUP_BATCHES
    PAIRS = GROUPS // 2
    HB = 2
    AHEAD = 4
    quarters = [("w_mlp1", q) for q in range(4)] + [("w_mlp2", q) for q in (3, 2, 1, 0)]
    with ExitStack() as ctx:
        def sb(name, shape, dt=F32):
            return ctx.enter_context(nc.sbuf_tensor(name, shape, dt))

        def sem(name):
            return ctx.enter_context(nc.semaphore(name))

        bank = ctx.enter_context(nc.psum_tensor("bank3", [P, 8, 512], F32))
        wc_hi, wc_lo = sb("wc_hi", [P, FC, D], F32R), sb("wc_lo", [P, FC, D], F32R)
        w1_hi, w1_lo = sb("w1_hi", [P, FC, MLP], F32R), sb("w1_lo", [P, FC, MLP], F32R)
        a_tok, att_t = [sb("a_tok", [N, GJ, D])[:]], [sb("att_t3", [P, FC, N])[:]]
        a_hi, a_lo = [sb("a_hi3", [P, FC, GT], F32R)[:]], [sb("a_lo3", [P, FC, GT], F32R)[:]]
        xt, xm = [sb("xt3", [P, FC, GT])[:]], [sb("xm3", [P, FC, GT])[:]]
        with ExitStack() as place:
            def early(name, shape, dt=F32):
                return place.enter_context(nc.sbuf_tensor(name, shape, dt))[:]

            a_tok.append(early("a_tok_1", [N, GJ, D]))
            xt.append(early("xt3_1", [P, FC, GT]))
            xm.append(early("xm3_1", [P, FC, GT]))
            att_t.append(early("att_t3_1", [P, FC, N]))
            early("gap", [P, MC * D - GJ * D - 2 * FC * GT - FC * N])
            a_hi.append(early("a_hi3_1", [P, FC, GT], F32R))
            a_lo.append(early("a_lo3_1", [P, FC, GT], F32R))
        w2_hi, w2_lo = sb("w2_hi", [P, MC, D], F32R), sb("w2_lo", [P, MC, D], F32R)
        m_hi, m_lo = [wc_hi[:, :, 0:GT], a_hi[0]], [wc_lo[:, :, 0:GT], a_lo[0]]
        hidden_raw, gated = xm[0][:, 0:HB, :], xm[0][:, HB:FC, :]
        h_hi = [sb(f"h_hi{i}", [P, GT], F32R) for i in range(HB)]
        h_lo = [sb(f"h_lo{i}", [P, GT], F32R) for i in range(HB)]
        gp = sb("gp3", [P, 2, 8, GJ])
        gp2 = sb("gp3_gate", [P, 8, GJ])
        stats, mean_var = sb("stats3", [N, 2, GJ, 6]), sb("mean_var3", [N, 2, GJ, 2])
        var_eps, half_bits = sb("var_eps3", [N, 2, GJ]), sb("half_bits3", [N, 2, GJ], I32)
        rstd, newton_work = sb("rstd3", [N, 2, GJ]), sb("newton_work3", [N, GJ])

        raw_landed = [sem(f"raw_landed3_{i}") for i in range(2)]
        w_hi_done, w_lo_done, c_hi_done, c_split, gp_ready = (
            sem(n) for n in ("w_hi_done3", "w_lo_done3", "c_hi_done3", "c_split", "gp_ready3"))
        a_landed, x1_landed = ([sem(f"{n}{i}") for i in range(2)] for n in ("a_landed", "x1_landed"))
        x2_stored, xm_stored = ([sem(f"{n}{i}") for i in range(2)] for n in ("x2_stored", "xm_stored"))
        a_turned, a_split, c_mm, x2_ready, x2_turned = (sem(n) for n in ("a_turned", "a_split", "c_mm", "x2_ready", "x2_turned"))
        st_done, mv_done, rstd_done, normed = (sem(n) for n in ("st_done3", "mv_done3", "rstd_done3", "normed3"))
        xn_back, xm_ready, xm_split = sem("xn_back3"), sem("xm_ready3"), sem("xm_split3")
        m_landed, x2_landed, out_stored = [sem(f"m_landed{i}") for i in range(2)], sem("x2_landed"), sem("out_stored")
        h_mm, gelu_done, h_split, y_mm, gated_done, y_ready = (
            sem(n) for n in ("h_mm", "gelu_done", "h_split", "y_mm", "gated_done3", "y_ready"))
        gp2_ready = sem("gp2_ready")

        block = ctx.enter_context(nc.Block())

        @block.sync
        def _(sp):
            def load_quarter(k):
                name, q = quarters[k]
                src = dram[name][:, :, q * 512:(q + 1) * 512] if name == "w_mlp1" else dram[name][:, 4 * q:4 * q + 4, :]
                if k >= 2:
                    sp.wait_ge(w_lo_done, k - 1)
                elif k == 1:
                    sp.wait_ge(c_split, 1)
                sp.dma_start(sh.raw[:, k % 2], src).then_inc(raw_landed[k % 2], 16)

            def load_mlp_input(g):
                if g >= 2:
                    sp.wait_ge(h_mm, MC * (g - 1))
                elif g == 1:
                    sp.wait_ge(xm_stored[0], 32 * PAIRS)
                    sp.wait_ge(xm_stored[1], 32 * PAIRS)
                else:
                    sp.wait_ge(xm_stored[0], 32)
                    sp.wait_ge(c_mm, FC * GROUPS)
                sp.dma_start(m_hi[g % 2].bitcast(F32), dram["xm_hi"][:, :, g * GT:(g + 1) * GT]).then_inc(m_landed[g % 2], 16)
                sp.dma_start(m_lo[g % 2].bitcast(F32), dram["xm_lo"][:, :, g * GT:(g + 1) * GT]).then_inc(m_landed[g % 2], 16)

            for g in range(GROUPS):
                i = g % 2
                if g >= 2:
                    sp.wait_ge(xn_back, GJ * (g - 1))
                sp.dma_start(a_tok[i], dram["att"][:, g * GJ:(g + 1) * GJ, :]).then_inc(a_landed[i], 16)
                if i == 1:
                    for s in (g - 1, g):
                        if g >= 2:
                            sp.wait_ge(x2_stored[s % 2], 16)
                        sp.dma_start(xt[s % 2], dram["x1"][:, :, s * GT:(s + 1) * GT]).then_inc(x1_landed[s % 2], 16)
                    if g == 3:
                        sp.wait_ge(xm_stored[1], 32)
                    load_quarter(g - 1)
                    load_quarter(g)
            load_quarter(4)
            load_mlp_input(0)
            load_quarter(5)
            for i in range(2):
                sp.wait_ge(x2_stored[i], 16 * PAIRS)
            load_quarter(6)
            load_quarter(7)
            for g in range(GROUPS):
                if g + 1 < GROUPS:
                    load_mlp_input(g + 1)
                if g >= 1:
                    sp.wait_ge(out_stored, 16 * g)
                sp.dma_start(xt[0], dram["x2"][:, :, g * GT:(g + 1) * GT]).then_inc(x2_landed, 16)
                sp.wait_ge(y_ready, FC * g + FC)
                sp.dma_start(dram["out"][:, :, g * GT:(g + 1) * GT], xt[0]).then_inc(out_stored, 16)
            sp.wait_ge(out_stored, 16 * GROUPS)

        @block.tensor
        def _(pe):
            pe.wait_ge(c_split, 1)
            with pe.Fori(0, PAIRS) as p:
                for i in range(2):
                    g = 2 * p + i
                    for j in range(GJ):
                        if j == 0:
                            pe.wait_ge(a_landed[i], 16 * p + 16)
                            pe.wait_ge(normed, 2 * GJ * p)
                            pe.wait_ge(xm_ready, 2 * GJ * p)
                        if j >= 2:
                            pe.wait_ge(a_split, 3 * GJ * g + 3 * j - 5)
                        for f in range(FC):
                            mm = pe.transpose(bank[:, 4 * i + j % 2, f * N:(f + 1) * N], a_tok[i][:, j, f * P:(f + 1) * P],
                                              sh.ident[0:N, 0:N])
                        mm.then_inc(a_turned, 1)
                for i in range(2):
                    g = 2 * p + i
                    for f in range(FC):
                        if f == 0:
                            pe.wait_ge(a_split, 3 * GJ * g + 3 * GJ)
                        product3(pe, bank[:, 4 * i + f, 0:GT],
                                 lambda c: wc_hi[:, c, f * P:(f + 1) * P], lambda c: wc_lo[:, c, f * P:(f + 1) * P],
                                 lambda c: a_hi[i][:, c, :], lambda c: a_lo[i][:, c, :], FC).then_inc(c_mm, 1)
                for i in range(2):
                    g = 2 * p + i
                    for j in range(GJ):
                        if j == 0:
                            pe.wait_ge(x2_ready, FC * g + FC)
                        for f in range(FC):
                            mm = pe.transpose(bank[0:N, 4 * i + j, f * P:(f + 1) * P], xt[i][:, f, j * N:(j + 1) * N], sh.ident)
                        mm.then_inc(x2_turned, 1)
                for i in range(2):
                    g = 2 * p + i
                    for j in range(GJ):
                        pe.wait_ge(normed, GJ * g + max(j + 1, 4))
                        if j >= 2:
                            pe.wait_ge(xm_ready, GJ * g + j - 1)
                        for f in range(FC):
                            mm = pe.transpose(bank[:, 4 * i + 2 + j % 2, f * N:(f + 1) * N], a_tok[i][:, j, f * P:(f + 1) * P],
                                              sh.ident[0:N, 0:N])
                        mm.then_inc(xn_back, 1)
            pe.wait_ge(w_lo_done, 4)
            pe.wait_ge(normed, GJ * GROUPS)
            pe.wait_ge(xm_ready, GJ * GROUPS)
            with pe.Fori(0, PAIRS) as p:
                for i in range(2):
                    g = 2 * p + i

                    def hidden(c):
                        if c == 0:
                            pe.wait_ge(m_landed[i], 32 * p + 32)
                            pe.wait_ge(gelu_done, MC * g)
                        if c >= 4:
                            pe.wait_ge(gelu_done, MC * g + c - 3)
                        product3(pe, bank[:, 4 + c % 4, 0:GT],
                                 lambda k: w1_hi[:, k, c * P:(c + 1) * P], lambda k: w1_lo[:, k, c * P:(c + 1) * P],
                                 lambda k: m_hi[i][:, k, :], lambda k: m_lo[i][:, k, :], FC).then_inc(h_mm, 1)

                    def output(c):
                        pe.wait_ge(h_split, 2 * MC * g + 2 * c + 2)
                        if c == 0:
                            pe.wait_ge(w_lo_done, len(quarters))
                            pe.wait_ge(gated_done, FC * g)
                        for f in range(FC):
                            out = bank[:, f, 0:GT]
                            fs = slice(f * P, (f + 1) * P)
                            pe.matmul(out, w2_hi[:, c, fs], h_hi[c % HB][:], start=(c == 0), stop=False)
                            pe.matmul(out, w2_lo[:, c, fs], h_hi[c % HB][:], start=False, stop=False)
                            mm = pe.matmul(out, w2_hi[:, c, fs], h_lo[c % HB][:], start=False, stop=(c == MC - 1))
                        mm.then_inc(y_mm, 1)

                    for c in range(AHEAD):
                        hidden(c)
                    for c in range(MC):
                        output(c)
                        if c + AHEAD < MC:
                            hidden(c + AHEAD)

        def split_target(k):
            name, q = quarters[k]
            if name == "w_mlp1":
                return w1_hi[:, :, q * 512:(q + 1) * 512], w1_lo[:, :, q * 512:(q + 1) * 512]
            return w2_hi[:, 4 * q:4 * q + 4, :], w2_lo[:, 4 * q:4 * q + 4, :]

        @block.scalar
        def _(act):
            act.activation(wc_hi[:], sh.raw[:, 1], ACT.Copy).then_inc(c_hi_done, 1)
            with act.Fori(0, PAIRS) as p:
                for q in range(2):
                    act.wait_ge(raw_landed[q], 16 * p + 16)
                    act.activation(w1_hi[:, :, bass.ds((2 * p + q) * 512, 512)], sh.raw[:, q], ACT.Copy).then_inc(w_hi_done, 1)
                for i in range(2):
                    g = 2 * p + i
                    for j in range(GJ):
                        act.wait_ge(xn_back, GJ * g + j + 1)
                        if j == 0:
                            act.wait_ge(gp_ready, 2 * p + 2)
                            act.wait_ge(xm_split, 4 * GJ * p)
                        for f in range(FC):
                            last = act.activation(xm[i][:, f, j * N:(j + 1) * N], bank[:, 4 * i + 2 + j % 2, f * N:(f + 1) * N],
                                                  ACT.Identity, bias=gp[:, i, f, j:j + 1], scale=gp[:, i, 4 + f, j:j + 1])
                        last.then_inc(xm_ready, 1)
            for k in range(4, 8):
                act.wait_ge(raw_landed[k % 2], 16 * (k // 2 + 1))
                if k == 5:
                    act.wait_ge(xm_split, 2 * GJ * GROUPS)
                    act.wait_ge(x2_stored[1], 16 * PAIRS)
                act.activation(split_target(k)[0], sh.raw[:, k % 2], ACT.Copy).then_inc(w_hi_done, 1)
            with act.Fori(0, PAIRS) as p:
                for i in range(2):
                    g = 2 * p + i
                    for c in range(MC):
                        act.wait_ge(h_mm, MC * g + c + 1)
                        if c >= HB:
                            act.wait_ge(h_split, 2 * MC * g + 2 * (c - HB) + 2)
                        elif c == 0:
                            act.wait_ge(h_split, 2 * MC * g)
                        act.activation(hidden_raw[:, c % HB, :], bank[:, 4 + c % 4, 0:GT], ACT.Gelu_apprx_tanh,
                                       bias=sh.b("mlp1", c)).then_inc(gelu_done, 1)
                    act.wait_ge(y_mm, MC * g + MC)
                    act.wait_ge(gp2_ready, 2 * g + 2)
                    for f in range(FC):
                        act.wait_ge(y_ready, FC * g + (f - 1 if f >= 2 else 0))
                        for j in range(GJ):
                            last = act.activation(gated[:, f % 2, j * N:(j + 1) * N], bank[:, f, j * N:(j + 1) * N],
                                                  ACT.Identity, bias=gp2[:, 4 + f, j:j + 1], scale=gp2[:, f, j:j + 1])
                        last.then_inc(gated_done, 1)

        @block.vector
        def _(dve):
            dve.wait_ge(c_hi_done, 1)
            dve.tensor_tensor(wc_lo[:], sh.raw[:, 1], wc_hi[:].bitcast(F32), ALU.subtract).then_inc(c_split, 1)
            with dve.Fori(0, PAIRS) as p:
                for i in range(2):
                    g = 2 * p + i
                    for j in range(GJ):
                        sl = slice(j * N, (j + 1) * N)
                        dve.wait_ge(a_turned, GJ * g + j + 1)
                        dve.wait_ge(a_split, 3 * GJ * g + 3 * j)
                        dve.tensor_tensor(att_t[i], bank[:, 4 * i + j % 2, 0:GT].rearrange("p (f t) -> p f t", f=FC),
                                          sh.bias[:, BIAS_OF["vc"]].unsqueeze(2).to_broadcast([P, FC, N]), ALU.add).then_inc(a_split, 1)
                        dve.wait_ge(a_split, 3 * GJ * g + 3 * j + 1)
                        if j == 0:
                            dve.wait_ge(xm_stored[i], 32 * p)
                        dve.tensor_copy(a_hi[i][:, :, sl], att_t[i]).then_inc(a_split, 1)
                        dve.wait_ge(a_split, 3 * GJ * g + 3 * j + 2)
                        dve.tensor_tensor(a_lo[i][:, :, sl], att_t[i], a_hi[i][:, :, sl].bitcast(F32), ALU.subtract).then_inc(a_split, 1)
                for i in range(2):
                    g = 2 * p + i
                    for f in range(FC):
                        dve.wait_ge(c_mm, FC * g + f + 1)
                        if f == 0:
                            dve.wait_ge(x1_landed[i], 16 * p + 16)
                        dve.scalar_tensor_tensor(out=xt[i][:, f, :], in0=bank[:, 4 * i + f, 0:GT], scalar=sh.b("cproj", f),
                                                 in1=xt[i][:, f, :], op0=ALU.add, op1=ALU.add).then_inc(x2_ready, 1)
                for i in range(2):
                    g = 2 * p + i
                    for j in range(GJ):
                        dve.wait_ge(x2_turned, GJ * g + j + 1)
                        dve.bn_stats(stats[:, i, j, :], bank[0:N, 4 * i + j, :]).then_inc(st_done, 1)
                    wait_apart(dve, sh.consts, st_done, GJ * g + GJ)
                    for j in range(GJ):
                        dve.bn_aggr(mean_var[:, i, j, :], stats[:, i, j, :]).then_inc(mv_done, 1)
                    dve.wait_ge(mv_done, GJ * g + GJ)
                    rsqrt(dve, rstd_done, RSQRT_STEPS * g, mean_var[:, i], var_eps[:, i], half_bits[:, i], rstd[:, i],
                          newton_work[:])
                for i in range(2):
                    g = 2 * p + i
                    dve.wait_ge(rstd_done, RSQRT_STEPS * g + RSQRT_STEPS)
                    for j in range(GJ):
                        dve.wait_ge(a_turned, GJ * g + GJ)
                        dve.tensor_scalar(a_tok[i][:, j, :], bank[0:N, 4 * i + j, :], mean_var[:, i, j, 0:1], rstd[:, i, j:j + 1],
                                          ALU.subtract, ALU.mult).then_inc(normed, 1)
                for q in range(2):
                    qs = bass.ds((2 * p + q) * 512, 512)
                    dve.wait_ge(w_hi_done, 2 * p + q + 1)
                    dve.tensor_tensor(w1_lo[:, :, qs], sh.raw[:, q], w1_hi[:, :, qs].bitcast(F32), ALU.subtract).then_inc(w_lo_done, 1)
                for i in range(2):
                    g = 2 * p + i
                    for j in range(GJ):
                        sl = slice(j * N, (j + 1) * N)
                        dve.wait_ge(xm_ready, GJ * g + j + 1)
                        dve.wait_ge(c_mm, FC * g + FC)
                        dve.tensor_copy(a_hi[i][:, :, sl], xm[i][:, :, sl]).then_inc(xm_split, 1)
                        dve.wait_ge(xm_split, 2 * GJ * g + 2 * j + 1)
                        dve.tensor_tensor(a_lo[i][:, :, sl], xm[i][:, :, sl], a_hi[i][:, :, sl].bitcast(F32),
                                          ALU.subtract).then_inc(xm_split, 1)
            for k in range(4, 8):
                hi, lo = split_target(k)
                dve.wait_ge(w_hi_done, k + 1)
                if k == 6:
                    dve.wait_ge(xm_stored[1], 32 * PAIRS)
                dve.tensor_tensor(lo, sh.raw[:, k % 2], hi.bitcast(F32), ALU.subtract).then_inc(w_lo_done, 1)
            with dve.Fori(0, PAIRS) as p:
                for i in range(2):
                    g = 2 * p + i
                    for c in range(MC):
                        dve.wait_ge(gelu_done, MC * g + c + 1)
                        if c >= HB:
                            dve.wait_ge(y_mm, MC * g + c - HB + 1)
                        elif c == 0:
                            dve.wait_ge(y_mm, MC * g)
                        dve.tensor_copy(h_hi[c % HB][:], hidden_raw[:, c % HB, :]).then_inc(h_split, 1)
                        dve.wait_ge(h_split, 2 * MC * g + 2 * c + 1)
                        dve.tensor_tensor(h_lo[c % HB][:], hidden_raw[:, c % HB, :], h_hi[c % HB][:].bitcast(F32),
                                          ALU.subtract).then_inc(h_split, 1)
                    for f in range(FC):
                        if f == 0:
                            dve.wait_ge(x2_landed, 16 * g + 16)
                        dve.wait_ge(gated_done, FC * g + f + 1)
                        dve.tensor_tensor(xt[0][:, f, :], xt[0][:, f, :], gated[:, f % 2, :], ALU.add).then_inc(y_ready, 1)

        @block.gpsimd
        def _(pool):
            with pool.Fori(0, PAIRS) as p:
                wait_apart(pool, sh.consts, xm_ready, 2 * GJ * p)
                for i in range(2):
                    pool.tensor_copy(gp[:, i], sh.mod[:, 12:20, bass.ds((2 * p + i) * GJ, GJ)]).then_inc(gp_ready, 1)
                for i in range(2):
                    g = 2 * p + i
                    wait_apart(pool, sh.consts, x2_ready, FC * g + FC)
                    pool.dma_start(dram["x2"][:, :, bass.ds(g * GT, GT)], xt[i]).then_inc(x2_stored[i], 16)
                for i in range(2):
                    g = 2 * p + i
                    wait_apart(pool, sh.consts, xm_split, 2 * GJ * g + 2 * GJ)
                    pool.dma_start(dram["xm_hi"][:, :, bass.ds(g * GT, GT)], a_hi[i].bitcast(F32)).then_inc(xm_stored[i], 16)
                    pool.dma_start(dram["xm_lo"][:, :, bass.ds(g * GT, GT)], a_lo[i].bitcast(F32)).then_inc(xm_stored[i], 16)
            with pool.Fori(0, GROUPS) as g:
                wait_apart(pool, sh.consts, gated_done, FC * g)
                pool.tensor_copy(gp2[:, 0:4, :], sh.mod[:, 20:24, bass.ds(g * GJ, GJ)]).then_inc(gp2_ready, 1)
                pool.tensor_copy(gp2[:, 4:8, :], sh.gate_bias[:, 4:8, bass.ds(g * GJ, GJ)]).then_inc(gp2_ready, 1)


def build(nc, x_tok, x_t, ctx_tok, cond_t, bias_cols, ident, w_mod, w_qkv, w_proj, w_qc, w_kvc, w_cproj, w_mlp1, w_mlp2, out):
    dram = {"x_tok": x_tok, "x_t": x_t, "ctx": ctx_tok, "cond_t": cond_t, "bias_cols": bias_cols, "ident": ident,
            "w_mod": w_mod, "w_qkv": w_qkv, "w_proj": w_proj, "w_qc": w_qc, "w_kvc": w_kvc, "w_cproj": w_cproj,
            "w_mlp1": w_mlp1, "w_mlp2": w_mlp2, "out": out}
    dram["x1"] = nc.dram_tensor("scratch_x1", (P, FC, B * N), F32, kind="Internal").ap()
    dram["q_hi"] = nc.dram_tensor("scratch_q_hi", (D, B * N), F32, kind="Internal").ap()
    dram["q_lo"] = nc.dram_tensor("scratch_q_lo", (D, B * N), F32, kind="Internal").ap()
    dram["att"] = nc.dram_tensor("scratch_att", (N, B, D), F32, kind="Internal").ap()
    for name in ("x2", "xm_hi", "xm_lo"):
        dram[name] = nc.dram_tensor("scratch_" + name, (P, FC, B * N), F32, kind="Internal").ap()
    with ExitStack() as ctx:
        sh = Shared(nc, ctx)
        self_attention_stage(nc, sh, dram)
        cross_attention_stage(nc, sh, dram)
        mlp_stage(nc, sh, dram)


_INS = ["x_tok", "x_t", "ctx_tok", "cond_t", "bias_cols", "ident", "w_mod", "w_qkv", "w_proj", "w_qc", "w_kvc",
        "w_cproj", "w_mlp1", "w_mlp2"]


def kernel(x, cond_1024, ctx_1024, L0_xcond_W_mod, L0_xcond_b_mod, L0_xcond_W_qkv, L0_xcond_b_qkv,
           L0_xcond_W_proj, L0_xcond_b_proj, L0_xcond_W_qc, L0_xcond_b_qc, L0_xcond_W_kvc, L0_xcond_b_kvc,
           L0_xcond_W_cproj, L0_xcond_b_cproj, L0_xcond_W_mlp1, L0_xcond_b_mlp1, L0_xcond_W_mlp2,
           L0_xcond_b_mlp2):
    import numpy as _np
    import concourse.bacc as _bacc
    from concourse import mybir as _mybir
    from concourse.bass_utils import run_bass_kernel_spmd as _run

    def chunked(w):
        return _np.ascontiguousarray(_np.asarray(w).reshape(-1, 128, w.shape[1]).transpose(1, 0, 2))

    x = _np.asarray(x)
    biases = [L0_xcond_b_mod, L0_xcond_b_qkv, L0_xcond_b_proj, L0_xcond_b_qc, L0_xcond_b_kvc,
              L0_xcond_b_cproj, L0_xcond_b_mlp1, L0_xcond_b_mlp2]
    laid = {
        "x_tok": _np.ascontiguousarray(x.transpose(1, 0, 2)),
        "x_t": chunked(x.reshape(-1, x.shape[2]).T),
        "ctx_tok": _np.ascontiguousarray(ctx_1024),
        "cond_t": chunked(_np.asarray(cond_1024).T),
        "bias_cols": _np.ascontiguousarray(_np.concatenate([_np.asarray(b) for b in biases]).reshape(-1, 128).T),
        "ident": _np.eye(128, dtype=_np.float32),
        "w_mod": chunked(L0_xcond_W_mod), "w_qkv": chunked(L0_xcond_W_qkv), "w_proj": chunked(L0_xcond_W_proj),
        "w_qc": chunked(L0_xcond_W_qc), "w_kvc": chunked(L0_xcond_W_kvc), "w_cproj": chunked(L0_xcond_W_cproj),
        "w_mlp1": chunked(L0_xcond_W_mlp1), "w_mlp2": chunked(L0_xcond_W_mlp2),
    }
    nc = _bacc.Bacc("TRN2", target_bir_lowering=False, num_devices=1)
    arrays, args = {}, []
    for name in _INS:
        a = laid[name]
        arrays[f"in_{name}_dram"] = a
        args.append(nc.dram_tensor(f"in_{name}_dram", a.shape, _mybir.dt.from_np(a.dtype), kind="ExternalInput").ap())
    args.append(nc.dram_tensor("out_0_dram", (P, FC, B * N), _mybir.dt.float32, kind="ExternalOutput").ap())
    build(nc, *args)
    r = _run(nc, [arrays], core_ids=[0])
    got = _np.asarray(r.results[0]["out_0_dram"])
    return _np.ascontiguousarray(got.transpose(2, 1, 0).reshape(B, N, D))
```

```python
from contextlib import ExitStack

import concourse.bass as bass
from concourse import mybir

F32 = mybir.dt.float32
F32R = mybir.dt.float32r
I32 = mybir.dt.int32
ALU = mybir.AluOpType
ACT = mybir.ActivationFunctionType
AX = mybir.AxisListType

P = 128
B, N, D = 16, 100, 512
S = 722
NH, HD = 16, 32
MLP = 4 * D
FC = D // P
MC = MLP // P
GROUP_BATCHES = 4
GROUPS = B // GROUP_BATCHES
GT = GROUP_BATCHES * N
SCALE = float(HD) ** -0.5

LN_EPS = 1e-6
RSQRT_SEED = 0x5F3759DF
NEWTON_ROUNDS = 3
SEED_STEPS = 3
NEWTON_STEPS = 1 + 4 * NEWTON_ROUNDS
RSQRT_STEPS = SEED_STEPS + 3 * NEWTON_ROUNDS

BIAS_OF = {}
_at = 0
for _name, _n in (("mod", 24), ("qk", 8), ("v", 4), ("proj", 4), ("qc", 4), ("kc", 4), ("vc", 4),
                  ("cproj", 4), ("mlp1", 16), ("mlp2", 4)):
    BIAS_OF[_name] = slice(_at, _at + _n)
    _at += _n
BIAS_COLS = _at


def seed_rsqrt(dve, sem, base, mean_var, var_eps, half_bits, guess):
    dve.tensor_scalar(var_eps, mean_var[:, :, 1], LN_EPS, None, ALU.add).then_inc(sem, 1)
    dve.wait_ge(sem, base + 1)
    dve.tensor_scalar(half_bits, var_eps.bitcast(I32), 1, None, ALU.logical_shift_right).then_inc(sem, 1)
    dve.wait_ge(sem, base + 2)
    dve.tensor_scalar(guess.bitcast(I32), half_bits, -1.0, float(RSQRT_SEED), ALU.mult, ALU.add).then_inc(sem, 1)


def rsqrt(dve, sem, base, mean_var, var_eps, half_bits, guess, work):
    seed_rsqrt(dve, sem, base, mean_var, var_eps, half_bits, guess)
    for r in range(NEWTON_ROUNDS):
        before = base + SEED_STEPS + 3 * r
        dve.wait_ge(sem, before)
        dve.scalar_tensor_tensor(out=work, in0=guess, scalar=-0.5, in1=guess, op0=ALU.mult, op1=ALU.mult).then_inc(sem, 1)
        dve.wait_ge(sem, before + 1)
        dve.tensor_tensor(work, work, var_eps, ALU.mult).then_inc(sem, 1)
        dve.wait_ge(sem, before + 2)
        dve.scalar_tensor_tensor(out=guess, in0=work, scalar=1.5, in1=guess, op0=ALU.add, op1=ALU.mult).then_inc(sem, 1)


def newton_rsqrt(pool, consts, sem, base, mean_var, var_eps, guess, work, neg_mean):
    def after(n):
        wait_apart(pool, consts, sem, base + n)

    pool.tensor_scalar(neg_mean, mean_var[:, :, 0], -1.0, None, ALU.mult).then_inc(sem, 1)
    for r in range(NEWTON_ROUNDS):
        after(4 * r + 1)
        pool.tensor_tensor(work, guess, guess, ALU.mult).then_inc(sem, 1)
        after(4 * r + 2)
        pool.tensor_tensor(work, work, var_eps, ALU.mult).then_inc(sem, 1)
        after(4 * r + 3)
        pool.tensor_scalar(work, work, -0.5, 1.5, ALU.mult, ALU.add).then_inc(sem, 1)
        after(4 * r + 4)
        pool.tensor_tensor(guess, guess, work, ALU.mult).then_inc(sem, 1)


def wait_apart(eng, consts, sem, value):
    if not isinstance(value, int):
        value = eng.snap(eng.to_reg(value))
    eng.wait_ge(consts, 48)
    eng.wait_ge(sem, value)


def product3(pe, out, lhs_hi, lhs_lo, rhs_hi, rhs_lo, chunks):
    for c in range(chunks):
        pe.matmul(out, lhs_hi(c), rhs_hi(c), start=(c == 0), stop=False)
        pe.matmul(out, lhs_hi(c), rhs_lo(c), start=False, stop=False)
        last = pe.matmul(out, lhs_lo(c), rhs_hi(c), start=False, stop=(c == chunks - 1))
    return last


class Shared:

    def __init__(self, nc, ctx):
        def sb(name, shape, dt=F32):
            return ctx.enter_context(nc.sbuf_tensor(name, shape, dt))

        self.bias = sb("bias", [P, BIAS_COLS])[:]
        self.ident = sb("identity", [P, P])[:]
        self.cond = sb("cond", [P, FC, B])[:]
        self.silu = sb("silu", [P, FC, B])[:]
        self.mod = sb("mod", [P, 24, B])[:]
        self.gate_bias = sb("gate_bias", [P, 8, B])[:]
        self.b_qc_scaled = sb("b_qc_scaled", [P, FC])[:]
        self.raw = sb("raw_weights", [P, 2, FC, 512])[:]
        self.consts = ctx.enter_context(nc.semaphore("consts"))
        self.mod_landed = [ctx.enter_context(nc.semaphore(f"mod_landed{i}")) for i in range(2)]

    def b(self, name, f):
        at = BIAS_OF[name].start + f
        return self.bias[:, at:at + 1]


def self_attention_stage(nc, sh, dram):
    GJ = GROUP_BATCHES
    UNITS = 2 * FC
    AHEAD = 3
    chunks = [("qkv", 0), ("qkv", 1), ("qkv", 2), ("proj", 0), ("qc", 0)]
    with ExitStack() as ctx:
        def sb(name, shape, dt=F32):
            return ctx.enter_context(nc.sbuf_tensor(name, shape, dt))

        def sem(name):
            return ctx.enter_context(nc.semaphore(name))

        bank = ctx.enter_context(nc.psum_tensor("bank1", [P, 8, 512], F32))
        w_hi = {"qkv": sb("wqkv_hi", [P, FC, 3 * D], F32R), "proj": sb("wproj_hi", [P, FC, D], F32R),
                "qc": sb("wqc_hi", [P, FC, D], F32R)}
        columns = {"qkv": 3 * D, "proj": D, "qc": D}
        with ExitStack() as place:
            w_raw = {kind: place.enter_context(nc.sbuf_tensor(f"w{kind}_raw", [P, FC, n], F32)) for kind, n in columns.items()}
        w_lo = {kind: sb(f"w{kind}_lo", [P, FC, n], F32R) for kind, n in columns.items()}
        x_tok = sb("x_tok", [N, GJ, D])
        stats_a, stats_b = sb("stats_a", [N, GJ, 6]), sb("stats_b", [N, GJ, 6])
        mean_var_a, mean_var_b = sb("mean_var_a", [N, GJ, 2]), sb("mean_var_b", [N, GJ, 2])
        var_eps_a, var_eps_b = sb("var_eps_a", [N, GJ]), sb("var_eps_b", [N, GJ])
        half_bits = sb("half_bits", [N, GJ], I32)
        rstd_a, rstd_b = sb("rstd_a", [N, GJ]), sb("rstd_b", [N, GJ])
        newton_work = sb("newton_work", [N, GJ])
        gp = sb("gp", [P, 8, GJ])
        gate = sb("gate", [P, 8, GJ])
        xm = sb("xm", [P, FC, GT])
        x_hi = sb("x_hi", [P, FC, GT], F32R)
        x_lo = sb("x_lo", [P, FC, GT], F32R)
        qk = sb("qk", [P, 2 * FC, GT])
        q_hi, q_lo = (qk[:, i * FC:(i + 1) * FC, :].bitcast(F32R) for i in range(2))
        v = sb("v", [N, GJ, NH, HD + 1])
        prob = [sb(f"prob{i}", [N, 8, N]) for i in range(2)]
        prob_t = [sb(f"prob_t{i}", [N, 2, 4 * N]) for i in range(2)]
        top = sb("top", [N, 2, 8])
        recip = sb("recip", [N, 2, 8])
        att = sb("att", [N, GJ, D])
        att_t = sb("att_t", [P, GT])
        a_hi = sb("a_hi", [P, FC, GT], F32R)
        a_lo = sb("a_lo", [P, FC, GT], F32R)
        xt = sb("xt", [P, FC, GT])
        gated = [sb(f"gated{i}", [P, GT]) for i in range(2)]
        xn = [sb(f"xn{i}", [N, D]) for i in range(2)]
        q32 = [sb(f"q32_{i}", [P, GT]) for i in range(2)]

        mod_landed = [sem(f"mod_landed1_{i}") for i in range(2)]
        w_landed = [sem(f"w_landed{k}") for k in range(len(chunks))]
        w_hi_done, w_lo_done = sem("w_hi_done"), sem("w_lo_done")
        silu_done, mod_mm, mod_added, mod_one, gate_bias = (
            sem(n) for n in ("silu_done", "mod_mm", "mod_added", "mod_one", "gate_bias"))
        x_landed, xt_landed, x1_stored, q_stored = (sem(n) for n in ("x_landed", "xt_landed", "x1_stored", "q_stored"))
        ones_set, gp_ready, gate_ready = sem("ones_set"), sem("gp_ready"), sem("gate_ready")
        st_a, mv_a, rstd_done_a, ln_a = (sem(n) for n in ("st_a", "mv_a", "rstd_done_a", "ln_a"))
        st_b, mv_b, rstd_done_b, ln_b = (sem(n) for n in ("st_b", "mv_b", "rstd_done_b", "ln_b"))
        x_turned, xm_ready, x_split = sem("x_turned"), sem("xm_ready"), sem("x_split")
        v_mm, v_copied, qk_mm, qk_copied = (sem(n) for n in ("v_mm", "v_copied", "qk_mm", "qk_copied"))
        s_mm, top_done, sub_done, exp_done = (sem(n) for n in ("s_mm", "top_done", "sub_done", "exp_done"))
        p_turned, p_copied, pv_mm, recip_done, att_ready = (
            sem(n) for n in ("p_turned", "p_copied", "pv_mm", "recip_done", "att_ready"))
        att_turned, att_added, att_split = sem("att_turned"), sem("att_added"), sem("att_split")
        proj_mm, gated_done, x1_ready = sem("proj_mm"), sem("gated_done"), sem("x1_ready")
        x1_turned, xn_back, xn_hi, xn_lo = (sem(n) for n in ("x1_turned", "xn_back", "xn_hi", "xn_lo"))
        q_mm, q32_done, q_split = sem("q_mm"), sem("q32_done"), sem("q_split")

        def weight(k):
            kind, q = chunks[k]
            return (w[kind][:, :, q * 512:(q + 1) * 512] for w in (w_raw, w_hi, w_lo))

        def unit_bank(u):
            return 2 * (u % 2)

        def qk_tile(n):
            return n // 2 + FC * (n % 2)

        def qk_bank(n):
            return 6 if n == 1 else 7

        def groups(eng, front, body):
            front(0)
            with eng.Fori(0, GROUPS - 1) as g:
                body(g)
            body(GROUPS - 1, last=True)

        block = ctx.enter_context(nc.Block())

        @block.sync
        def _(sp):
            sp.dma_start(sh.bias, dram["bias_cols"]).then_inc(sh.consts, 16)
            sp.dma_start(sh.ident, dram["ident"]).then_inc(sh.consts, 16)
            sp.dma_start(sh.cond, dram["cond_t"]).then_inc(sh.consts, 16)
            def load_mod(m):
                if m >= 2:
                    sp.wait_ge(mod_mm, m - 1)
                sp.dma_start(sh.raw[:, m % 2], dram["w_mod"][:, :, m * 512:(m + 1) * 512]).then_inc(mod_landed[m % 2], 16)

            def load_weight(k):
                kind, q = chunks[k]
                raw, _, _ = weight(k)
                sp.dma_start(raw, dram["w_" + kind][:, :, q * 512:(q + 1) * 512]).then_inc(w_landed[k], 16)

            load_mod(0)
            load_mod(1)
            for k in range(3):
                load_weight(k)
            load_mod(2)
            load_weight(3)
            load_weight(4)
            for q in (1, 0):
                sp.wait_ge(mod_mm, 3 - q)
                sp.dma_start(sh.raw[:, q], dram["w_mod"][:, :, (3 + q) * 512:(4 + q) * 512]).then_inc(sh.mod_landed[q], 16)
            with sp.Fori(0, GROUPS) as g:
                wait_apart(sp, sh.consts, x1_stored, 16 * g)
                sp.wait_ge(x1_turned, GJ * g)
                sp.dma_start(xt[:], dram["x_t"][:, :, bass.ds(g * GT, GT)]).then_inc(xt_landed, 16)
                sp.wait_ge(x1_ready, FC * g + FC)
                sp.dma_start(dram["x1"][:, :, bass.ds(g * GT, GT)], xt[:]).then_inc(x1_stored, 16)
                sp.wait_ge(q_split, 2 * FC * g + 2 * FC)
                sp.dma_start(dram["q_hi"].rearrange("(f p) t -> p f t", p=P)[:, :, bass.ds(g * GT, GT)],
                             q_hi.bitcast(F32)).then_inc(q_stored, 16)
                sp.dma_start(dram["q_lo"].rearrange("(f p) t -> p f t", p=P)[:, :, bass.ds(g * GT, GT)],
                             q_lo.bitcast(F32)).then_inc(q_stored, 16)
            sp.wait_ge(x1_stored, 16 * GROUPS)
            sp.wait_ge(q_stored, 32 * GROUPS)

        @block.tensor
        def _(pe):
            def modulation(m):
                pe.wait_ge(mod_landed[m % 2], 16 * (m // 2 + 1))
                if m >= 2:
                    pe.wait_ge(mod_added, m - 1)
                for f in range(4):
                    for c in range(FC):
                        mm = pe.matmul(bank[:, m % 2, f * B:(f + 1) * B], sh.raw[:, m % 2, c, f * P:(f + 1) * P],
                                       sh.silu[:, c, :], start=(c == 0), stop=(c == FC - 1))
                mm.then_inc(mod_mm, 1)

            def turn_x(g, js, first=False):
                for j in js:
                    pe.wait_ge(ln_a, GJ * g + j + 1)
                    if j == 0 and not first:
                        pe.wait_ge(att_ready, UNITS * g)
                        pe.wait_ge(att_added, FC * g)
                    if j >= 2:
                        pe.wait_ge(xm_ready, GJ * g + j - 1)
                    for f in range(FC):
                        mm = pe.transpose(bank[:, 6 + j % 2, f * N:(f + 1) * N], x_tok[:, j, f * P:(f + 1) * P],
                                          sh.ident[0:N, 0:N])
                    mm.then_inc(x_turned, 1)

            def front(g):
                pe.wait_ge(silu_done, 1)
                modulation(0)
                modulation(1)
                turn_x(g, range(GJ), first=True)
                modulation(2)
                pe.wait_ge(w_lo_done, 3)
                pe.wait_ge(mod_added, 3)

            def body(g, last=False):
                def product_v(j):
                    product3(pe, bank[0:N, j, :],
                             lambda c: x_hi[:, c, j * N:(j + 1) * N], lambda c: x_lo[:, c, j * N:(j + 1) * N],
                             lambda c: w_hi["qkv"][:, c, 2 * D:3 * D], lambda c: w_lo["qkv"][:, c, 2 * D:3 * D],
                             FC).then_inc(v_mm, 1)

                def product_qk(n):
                    if n >= 2:
                        pe.wait_ge(qk_copied, 2 * FC * g + (1 if n == 2 else n))
                    if n == AHEAD + 4:
                        pe.wait_ge(att_added, FC * g + 1)
                    fs = slice(qk_tile(n) * P, (qk_tile(n) + 1) * P)
                    product3(pe, bank[:, qk_bank(n), 0:GT],
                             lambda c: w_hi["qkv"][:, c, fs], lambda c: w_lo["qkv"][:, c, fs],
                             lambda c: x_hi[:, c, :], lambda c: x_lo[:, c, :], FC).then_inc(qk_mm, 1)

                def scores(u):
                    if u % 2 == 0:
                        pe.wait_ge(qk_copied, 2 * FC * g + u + 2)
                    if u < 2:
                        pe.wait_ge(v_copied, GJ * g + GJ)
                    else:
                        pe.wait_ge(sub_done, UNITS * g + u - 1)
                    f = u // 2
                    for h in range(8):
                        j, r = h % 4, 32 * (unit_bank(u) + h // 4)
                        mm = pe.matmul(bank[0:N, unit_bank(u) + h // 4, j * N:(j + 1) * N],
                                       qk[r:r + 32, f, j * N:(j + 1) * N], qk[r:r + 32, FC + f, j * N:(j + 1) * N],
                                       start=True, stop=True)
                    mm.then_inc(s_mm, 1)

                def turn_probs(u):
                    pe.wait_ge(exp_done, UNITS * g + u + 1)
                    if u == 0:
                        pe.wait_ge(xn_lo, GJ * g)
                    else:
                        pe.wait_ge(p_copied, UNITS * g + u)
                    for h in range(8):
                        mm = pe.transpose(bank[0:N, 4 + h // 4, (h % 4) * N:(h % 4 + 1) * N], prob[u % 2][:, h, :],
                                          sh.ident[0:N, 0:N])
                    mm.then_inc(p_turned, 1)

                def weigh(u):
                    pe.wait_ge(p_copied, UNITS * g + u + 1)
                    if u == 0:
                        pe.wait_ge(qk_copied, 2 * FC * g + 2)
                    pe.wait_ge(att_ready, UNITS * g + u)
                    for h in range(8):
                        mm = pe.matmul(bank[0:N, 6, h * (HD + 1):(h + 1) * (HD + 1)],
                                       prob_t[u % 2][:, h // 4, (h % 4) * N:(h % 4 + 1) * N],
                                       v[:, h % 4, 4 * (u // 2) + unit_bank(u) + h // 4, :], start=True, stop=True)
                    mm.then_inc(pv_mm, 1)

                def turn_att(f):
                    pe.wait_ge(att_ready, UNITS * g + 2 * f + 2)
                    pe.wait_ge(qk_copied, 2 * FC * g + (AHEAD + 4 if f == 0 else 2 * FC))
                    if f >= 1:
                        pe.wait_ge(att_added, FC * g + f)
                    for j in range(GJ):
                        mm = pe.transpose(bank[:, 7, j * N:(j + 1) * N], att[:, j, f * P:(f + 1) * P], sh.ident[0:N, 0:N])
                    mm.then_inc(att_turned, 1)

                def project(c):
                    pe.wait_ge(att_split, 2 * FC * g + 2 * c + 2)
                    if c == 0:
                        pe.wait_ge(w_lo_done, 5)
                        pe.wait_ge(sub_done, UNITS * g + UNITS)
                    for f in range(FC):
                        out, fs = bank[:, f, 0:GT], slice(f * P, (f + 1) * P)
                        pe.matmul(out, w_hi["proj"][:, c, fs], a_hi[:, c, :], start=(c == 0), stop=False)
                        pe.matmul(out, w_hi["proj"][:, c, fs], a_lo[:, c, :], start=False, stop=False)
                        mm = pe.matmul(out, w_lo["proj"][:, c, fs], a_hi[:, c, :], start=False, stop=(c == FC - 1))
                        if c == FC - 1:
                            mm.then_inc(proj_mm, 1)

                pe.wait_ge(x_split, 2 * GJ * g + 2 * GJ)
                pe.wait_ge(xm_ready, GJ * g + GJ)
                product_qk(0)
                product_qk(1)
                for j in range(GJ):
                    if j == 0:
                        pe.wait_ge(q32_done, FC * g)
                    product_v(j)
                product_qk(2)
                scores(0)
                pe.wait_ge(ones_set, 1)
                for u in range(UNITS):
                    if u + 1 < UNITS:
                        scores(u + 1)
                    if AHEAD + u < 2 * FC:
                        product_qk(AHEAD + u)
                    if u >= 1:
                        weigh(u - 1)
                    turn_probs(u)
                    if u >= 3 and u % 2:
                        turn_att((u - 3) // 2)
                project(0)
                weigh(UNITS - 1)
                project(1)
                turn_att(FC - 1)
                project(2)
                project(3)
                if not last:
                    turn_x(g + 1, (0, 1))
                for j in range(GJ):
                    if j == 0:
                        pe.wait_ge(x1_ready, FC * g + FC)
                        pe.wait_ge(gated_done, FC * g + FC)
                    for f in range(FC):
                        mm = pe.transpose(bank[0:N, j, f * P:(f + 1) * P], xt[:, f, j * N:(j + 1) * N], sh.ident)
                    mm.then_inc(x1_turned, 1)
                if not last:
                    turn_x(g + 1, (2, 3))
                for j in range(GJ):
                    pe.wait_ge(ln_b, GJ * g + j + 1)
                    if j < 2:
                        pe.wait_ge(p_copied, UNITS * g + UNITS)
                    else:
                        pe.wait_ge(xn_lo, GJ * g + j - 1)
                    for f in range(FC):
                        mm = pe.transpose(bank[:, 4 + j % 2, f * N:(f + 1) * N], xn[j % 2][:, f * P:(f + 1) * P],
                                          sh.ident[0:N, 0:N])
                    mm.then_inc(xn_back, 1)
                for f in range(FC):
                    if f == 0:
                        pe.wait_ge(xn_lo, GJ * g + GJ)
                    product3(pe, bank[:, f, 0:GT],
                             lambda c: w_hi["qc"][:, c, f * P:(f + 1) * P], lambda c: w_lo["qc"][:, c, f * P:(f + 1) * P],
                             lambda c: a_hi[:, c, :], lambda c: a_lo[:, c, :], FC).then_inc(q_mm, 1)

            groups(pe, front, body)

        @block.scalar
        def _(act):
            act.wait_ge(sh.consts, 48)
            act.activation(sh.silu, sh.cond, ACT.Silu).then_inc(silu_done, 1)

            def round_weights(ks):
                for k in ks:
                    raw, hi, _ = weight(k)
                    act.wait_ge(w_landed[k], 16)
                    act.activation(hi, raw, ACT.Copy).then_inc(w_hi_done, 1)

            def front(g):
                round_weights((0, 1, 2))
                modulate(g)
                round_weights((3, 4))
                act.wait_ge(gate_bias, 2)

            def modulate(g):
                for j in range(GJ):
                    act.wait_ge(x_turned, GJ * g + j + 1)
                    if j == 0:
                        act.wait_ge(gp_ready, g + 1)
                        act.wait_ge(x_split, 2 * GJ * g)
                    for f in range(FC):
                        last = act.activation(xm[:, f, j * N:(j + 1) * N], bank[:, 6 + j % 2, f * N:(f + 1) * N],
                                              ACT.Identity, bias=gp[:, f, j:j + 1], scale=gp[:, 4 + f, j:j + 1])
                    last.then_inc(xm_ready, 1)

            def body(g, last=False):
                def copy_qk(n):
                    act.wait_ge(qk_mm, 2 * FC * g + n + 1)
                    if n == 0:
                        act.wait_ge(s_mm, UNITS * g)
                        act.wait_ge(q_stored, 32 * g)
                    act.activation(qk[:, qk_tile(n), :], bank[:, qk_bank(n), 0:GT], ACT.Identity,
                                   bias=sh.b("qk", qk_tile(n))).then_inc(qk_copied, 1)

                def exponentiate(u):
                    act.wait_ge(sub_done, UNITS * g + u + 1)
                    act.activation(prob[u % 2][:], prob[u % 2][:], ACT.Exp, scale=SCALE).then_inc(exp_done, 1)

                def copy_probs(u):
                    act.wait_ge(p_turned, UNITS * g + u + 1)
                    act.wait_ge(pv_mm, UNITS * g + (u - 1 if u >= 2 else 0))
                    act.activation(prob_t[u % 2][:], bank[0:N, 4:6, 0:4 * N], ACT.Copy).then_inc(p_copied, 1)

                def add_bias(f):
                    act.wait_ge(att_turned, FC * g + f + 1)
                    act.wait_ge(att_split, 2 * FC * g + 2 * f)
                    act.activation(att_t[:], bank[:, 7, 0:GT], ACT.Identity, bias=sh.b("v", f)).then_inc(att_added, 1)

                for n in range(AHEAD):
                    copy_qk(n)
                exponentiate(0)
                for u in range(UNITS):
                    if AHEAD + u < 2 * FC:
                        copy_qk(AHEAD + u)
                    if u + 1 < UNITS:
                        exponentiate(u + 1)
                    copy_probs(u)
                    if u >= 3 and u % 2:
                        add_bias((u - 3) // 2)
                add_bias(FC - 1)
                act.wait_ge(gate_ready, 2 * g + 2)
                for f in range(FC):
                    act.wait_ge(proj_mm, FC * g + f + 1)
                    act.wait_ge(x1_ready, FC * g + (f - 1 if f >= 2 else 0))
                    for j in range(GJ):
                        mm = act.activation(gated[f % 2][:, j * N:(j + 1) * N], bank[:, f, j * N:(j + 1) * N],
                                            ACT.Identity, bias=gate[:, 4 + f, j:j + 1], scale=gate[:, f, j:j + 1])
                    mm.then_inc(gated_done, 1)
                if not last:
                    modulate(g + 1)
                for j in range(GJ):
                    act.wait_ge(xn_back, GJ * g + j + 1)
                    act.activation(a_hi[:, :, j * N:(j + 1) * N],
                                   bank[:, 4 + j % 2, 0:GT].rearrange("p (f t) -> p f t", f=FC), ACT.Copy).then_inc(xn_hi, 1)
                for f in range(FC):
                    act.wait_ge(q_mm, FC * g + f + 1)
                    act.wait_ge(q_split, 2 * FC * g + (2 * f - 2 if f >= 2 else 0))
                    act.activation(q32[f % 2][:], bank[:, f, 0:GT], ACT.Identity, bias=sh.b_qc_scaled[:, f:f + 1],
                                   scale=SCALE).then_inc(q32_done, 1)

            groups(act, front, body)

        @block.vector
        def _(dve):
            dve.wait_ge(sh.consts, 48)
            dve.tensor_scalar(sh.b_qc_scaled, sh.bias[:, BIAS_OF["qc"]], SCALE, None, ALU.mult).then_inc(gate_bias, 1)
            def add_mod_bias(m):
                dve.wait_ge(mod_mm, m + 1)
                dve.tensor_tensor(sh.mod[:, 4 * m:4 * m + 4, :], bank[:, m % 2, 0:4 * B].rearrange("p (f b) -> p f b", f=4),
                                  sh.bias[:, 4 * m:4 * m + 4].unsqueeze(2).to_broadcast([P, 4, B]),
                                  ALU.add).then_inc(mod_added, 1)

            def split_weights(ks):
                for k in ks:
                    raw, hi, lo = weight(k)
                    dve.wait_ge(w_hi_done, k + 1)
                    dve.tensor_tensor(lo, raw, hi.bitcast(F32), ALU.subtract).then_inc(w_lo_done, 1)

            def stats_of_x(g, j):
                dve.wait_ge(x_landed, 16 * g + 16)
                dve.bn_stats(stats_a[:, j, :], x_tok[:, j, :]).then_inc(st_a, 1)

            def rstd_of_x(g):
                wait_apart(dve, sh.consts, st_a, GJ * g + GJ)
                for j in range(GJ):
                    dve.bn_aggr(mean_var_a[:, j, :], stats_a[:, j, :]).then_inc(mv_a, 1)
                dve.wait_ge(mv_a, GJ * g + GJ)
                rsqrt(dve, rstd_done_a, RSQRT_STEPS * g, mean_var_a[:], var_eps_a[:], half_bits[:], rstd_a[:], newton_work[:])

            def normalise_x(g, js):
                dve.wait_ge(rstd_done_a, RSQRT_STEPS * g + RSQRT_STEPS)
                for j in js:
                    dve.tensor_scalar(x_tok[:, j, :], x_tok[:, j, :], mean_var_a[:, j, 0:1], rstd_a[:, j:j + 1],
                                      ALU.subtract, ALU.mult).then_inc(ln_a, 1)

            def split_x(g):
                for j in range(GJ):
                    sl = slice(j * N, (j + 1) * N)
                    dve.wait_ge(xm_ready, GJ * g + j + 1)
                    if j == 0:
                        dve.wait_ge(qk_mm, 2 * FC * g)
                    dve.tensor_copy(x_hi[:, :, sl], xm[:, :, sl]).then_inc(x_split, 1)
                    dve.wait_ge(x_split, 2 * GJ * g + 2 * j + 1)
                    dve.tensor_tensor(x_lo[:, :, sl], xm[:, :, sl], x_hi[:, :, sl].bitcast(F32),
                                      ALU.subtract).then_inc(x_split, 1)

            def front(g):
                for j in range(GJ):
                    stats_of_x(g, j)
                rstd_of_x(g)
                normalise_x(g, range(GJ))
                add_mod_bias(0)
                add_mod_bias(1)
                dve.wait_ge(mod_added, 2)
                dve.tensor_scalar(sh.mod[:, 4:8, :], sh.mod[:, 4:8, :], 1.0, None, ALU.add).then_inc(mod_one, 1)
                split_weights((0, 1, 2))
                split_x(g)
                add_mod_bias(2)
                dve.wait_ge(mod_added, 3)
                dve.tensor_tensor(sh.gate_bias[:, 0:4, :], sh.mod[:, 8:12, :],
                                  sh.bias[:, BIAS_OF["proj"]].unsqueeze(2).to_broadcast([P, 4, B]),
                                  ALU.mult).then_inc(gate_bias, 1)
                split_weights((3, 4))

            def body(g, last=False):
                for j in range(GJ):
                    dve.wait_ge(v_mm, GJ * g + j + 1)
                    dve.tensor_copy(v[:, j, :, 0:HD], bank[0:N, j, :].rearrange("p (h d) -> p h d", h=NH)).then_inc(v_copied, 1)

                def soften(u):
                    s = bank[0:N, unit_bank(u):unit_bank(u) + 2, 0:4 * N].rearrange("p b (h k) -> p b h k", h=4)
                    dve.wait_ge(s_mm, UNITS * g + u + 1)
                    dve.tensor_reduce(top[:, u % 2, :].rearrange("p (b h) -> p b h", b=2), s, AX.X, ALU.max).then_inc(top_done, 1)
                    dve.wait_ge(top_done, UNITS * g + u + 1)
                    dve.wait_ge(p_turned, UNITS * g + (u - 1 if u >= 2 else 0))
                    dve.tensor_tensor(prob[u % 2][:].rearrange("p (b h) k -> p b h k", b=2), s,
                                      top[:, u % 2, :].rearrange("p (b h) -> p b h", b=2).unsqueeze(3).to_broadcast([N, 2, 4, N]),
                                      ALU.subtract).then_inc(sub_done, 1)

                def normalise(u):
                    o = bank[0:N, 6, 0:8 * (HD + 1)].rearrange("p (h d) -> p h d", h=8)
                    head = 4 * (u // 2) + unit_bank(u)
                    dve.wait_ge(pv_mm, UNITS * g + u + 1)
                    dve.reciprocal(recip[:, u % 2, :], o[:, :, HD]).then_inc(recip_done, 1)
                    dve.wait_ge(recip_done, UNITS * g + u + 1)
                    dve.wait_ge(att_turned, FC * g)
                    dve.tensor_tensor(att[:].rearrange("p j (h d) -> p h j d", h=NH)[:, head:head + 2],
                                      o[:, :, 0:HD].rearrange("p (r j) d -> p r j d", r=2),
                                      recip[:, u % 2, :].rearrange("p (r j) -> p r j", r=2).unsqueeze(3).to_broadcast([N, 2, 4, HD]),
                                      ALU.mult).then_inc(att_ready, 1)

                def split_att(f):
                    dve.wait_ge(att_added, FC * g + f + 1)
                    if f == 0:
                        dve.wait_ge(q_mm, FC * g)
                    dve.tensor_copy(a_hi[:, f, :], att_t[:]).then_inc(att_split, 1)
                    dve.wait_ge(att_split, 2 * FC * g + 2 * f + 1)
                    dve.tensor_tensor(a_lo[:, f, :], att_t[:], a_hi[:, f, :].bitcast(F32), ALU.subtract).then_inc(att_split, 1)

                for u in range(UNITS):
                    soften(u)
                    if u >= 2:
                        normalise(u - 2)
                    if u >= 5 and u % 2:
                        split_att((u - 5) // 2)
                    if not last:
                        if 1 <= u <= GJ:
                            stats_of_x(g + 1, u - 1)
                        if u == GJ + 1:
                            rstd_of_x(g + 1)
                        if u >= GJ + 2:
                            normalise_x(g + 1, (0, 1) if u == GJ + 2 else (2, 3))
                normalise(UNITS - 2)
                split_att(FC - 2)
                normalise(UNITS - 1)
                split_att(FC - 1)
                for f in range(FC):
                    dve.wait_ge(gated_done, FC * g + f + 1)
                    if f == 0:
                        dve.wait_ge(xt_landed, 16 * g + 16)
                    dve.tensor_tensor(xt[:, f, :], xt[:, f, :], gated[f % 2][:], ALU.add).then_inc(x1_ready, 1)
                for j in range(GJ):
                    dve.wait_ge(x1_turned, GJ * g + j + 1)
                    dve.bn_stats(stats_b[:, j, :], bank[0:N, j, :]).then_inc(st_b, 1)
                wait_apart(dve, sh.consts, st_b, GJ * g + GJ)
                for j in range(GJ):
                    dve.bn_aggr(mean_var_b[:, j, :], stats_b[:, j, :]).then_inc(mv_b, 1)
                dve.wait_ge(mv_b, GJ * g + GJ)
                rsqrt(dve, rstd_done_b, RSQRT_STEPS * g, mean_var_b[:], var_eps_b[:], half_bits[:], rstd_b[:], newton_work[:])
                dve.wait_ge(rstd_done_b, RSQRT_STEPS * g + RSQRT_STEPS)

                def lo_back(j):
                    sl = slice(j * N, (j + 1) * N)
                    dve.wait_ge(xn_hi, GJ * g + j + 1)
                    dve.tensor_tensor(a_lo[:, :, sl], bank[:, 4 + j % 2, 0:GT].rearrange("p (f t) -> p f t", f=FC),
                                      a_hi[:, :, sl].bitcast(F32), ALU.subtract).then_inc(xn_lo, 1)

                for j in range(GJ):
                    if j >= 2:
                        dve.wait_ge(xn_back, GJ * g + j - 1)
                    dve.tensor_scalar(xn[j % 2][:], bank[0:N, j, :], mean_var_b[:, j, 0:1], rstd_b[:, j:j + 1],
                                      ALU.subtract, ALU.mult).then_inc(ln_b, 1)
                    if j >= 1:
                        lo_back(j - 1)
                lo_back(GJ - 1)
                if not last:
                    split_x(g + 1)
                for f in range(FC):
                    dve.wait_ge(q32_done, FC * g + f + 1)
                    dve.tensor_copy(q_hi[:, f, :], q32[f % 2][:]).then_inc(q_split, 1)
                    dve.wait_ge(q_split, 2 * FC * g + 2 * f + 1)
                    dve.tensor_tensor(q_lo[:, f, :], q32[f % 2][:], q_hi[:, f, :].bitcast(F32), ALU.subtract).then_inc(q_split, 1)

            groups(dve, front, body)

        @block.gpsimd
        def _(pool):
            pool.memset(v[:, :, :, HD:HD + 1], 1.0).then_inc(ones_set, 1)
            def load_x(g):
                pool.dma_start(x_tok[:], dram["x_tok"][:, bass.ds(g * GJ, GJ), :]).then_inc(x_landed, 16)

            def copy_modulation(g):
                pool.tensor_copy(gp[:], sh.mod[:, 0:8, bass.ds(g * GJ, GJ)]).then_inc(gp_ready, 1)

            def front(g):
                load_x(g)
                pool.wait_ge(mod_one, 1)
                copy_modulation(g)
                pool.wait_ge(gate_bias, 2)

            def body(g, last=False):
                wait_apart(pool, sh.consts, gated_done, FC * g)
                pool.tensor_copy(gate[:, 0:4, :], sh.mod[:, 8:12, bass.ds(g * GJ, GJ)]).then_inc(gate_ready, 1)
                pool.tensor_copy(gate[:, 4:8, :], sh.gate_bias[:, 0:4, bass.ds(g * GJ, GJ)]).then_inc(gate_ready, 1)
                if not last:
                    wait_apart(pool, sh.consts, x_turned, GJ * g + GJ)
                    load_x(g + 1)
                    wait_apart(pool, sh.consts, xm_ready, GJ * g + GJ)
                    copy_modulation(g + 1)

            groups(pool, front, body)


def cross_attention_stage(nc, sh, dram):
    TILES = [(t * P, min(P, S - t * P)) for t in range((S + P - 1) // P)]
    CT = len(TILES)
    HALF = S // 2
    LN_SLOT = 7
    WIDE = HALF + 1
    V_UNITS = [(t, c) for t in range(CT) for c in range(FC)]
    V_SLOTS = [4, 5, 6, 7, 12, 13, 14, 15]
    V_SHARE = len(V_UNITS) // len(V_SLOTS)
    SLOTS = {0: ["K2a"], 1: ["K2b"], 2: ["K3a"], 3: ["T0", "K3b"], 8: ["T5", "K0a"], 9: ["K0b"], 10: ["K1a"], 11: ["K1b"]}
    for _i, _s in enumerate(V_SLOTS):
        SLOTS[_s] = [f"T{_s - 3}"] if _s < 8 else []
        SLOTS[_s] += [f"V{t}{c}" for t, c in V_UNITS[_i * V_SHARE:(_i + 1) * V_SHARE]]
    ENDS = {s: [x[:2] if x[0] == "V" else x for x in work if x[0] != "V" or int(x[2]) == FC - 1]
            for s, work in SLOTS.items()}
    ORDER = [x for s in range(NH) for x in ENDS[s]]
    OWN = ["K2a", "K2b", "K3a", "K3b"]
    SPLIT = [x for x in ORDER if x[0] != "V"]
    VS = [x for x in ORDER if x[0] == "V"]
    BIG = [x for x in ORDER if x[0] != "T"]

    def done(seq, b, x):
        at = seq.index(x)
        if isinstance(b, int) and b < 0:
            return len([y for y in seq[:at + 1] if y not in OWN])
        if isinstance(b, int) and b == B - 1:
            return len(seq) * B - len(OWN) + len([y for y in seq[:at + 1] if y in OWN])
        return len(seq) * (b + 1) - len(OWN) + at + 1

    def pieces_done(b, x):
        return done(ORDER, b, x)

    def splits_done(b, x):
        return done(SPLIT, b, x)

    def vs_done(b, x):
        return len(VS) * (b + 1) + VS.index(x) + 1

    with ExitStack() as ctx:
        def sb(name, shape, dt=F32):
            return ctx.enter_context(nc.sbuf_tensor(name, shape, dt))

        def sem(name):
            return ctx.enter_context(nc.semaphore(name))

        bank = ctx.enter_context(nc.psum_tensor("bank2", [P, 8, 512], F32))
        PROBS_T, PIECES, OUT, TURNED = 2, 4, 6, 7
        MOD_BANKS = (0, 1, OUT)
        wkv_hi = sb("wkv_hi", [P, FC, 2 * D], F32R)
        with ExitStack() as place:
            wkv_raw = place.enter_context(nc.sbuf_tensor("wkv_raw", [P, FC, 2 * D], F32))
        wkv_lo = sb("wkv_lo", [P, FC, 2 * D], F32R)
        W_HALF = {"k": slice(0, D), "v": slice(D, 2 * D)}
        c_raw = sb("c_raw", [P, CT, D])
        c_norm = sb("c_norm", [P, CT, D])
        c_hi = sb("c_hi", [P, FC, S], F32R)
        c_lo = sb("c_lo", [P, FC, S], F32R)
        stats = sb("stats2", [P, CT, 6])
        mean_var = sb("mean_var2", [P, CT, 2])
        var_eps = sb("var_eps2", [P, CT])
        half_bits = sb("half_bits2", [P, CT], I32)
        rstd = sb("rstd2", [P, CT])
        newton_work = sb("newton_work2", [P, CT])
        neg_mean = sb("neg_mean2", [P, CT])
        k_hi = sb("k_hi", [P, 2, S], F32R)
        k_lo = sb("k_lo", [P, 2, S], F32R)
        k_stack = sb("k_stack", [3 * HD, NH, S + 1], F32R)
        q_stack = sb("q_stack", [3 * HD, NH, N], F32R)
        v_next = sb("v_next", [P, CT, D])
        v_now = sb("v_now", [P, CT, D])
        neg_top = sb("neg_top", [N, NH])
        total = sb("total", [N, NH])
        recip = sb("recip2", [N, NH])
        prob = [sb(f"prob2_{i}", [N, S]) for i in range(2)]
        prob_t = [sb(f"prob_t2_{i}", [P, CT, N]) for i in range(4)]
        out_t = sb("out_t", [P, FC, N])
        att = sb("att2", [N, D])

        w_hi_done, cleared = sem("w_hi_done2"), sem("cleared")
        w_landed, w_split = ({half: sem(f"w{half}_{n}") for half in "kv"} for n in ("landed", "split"))
        ctx_landed = [sem(f"ctx_landed{t}") for t in range(CT)]
        k_landed = [sem(f"k_landed{f}") for f in range(FC)]
        q_landed = [sem(f"q_landed{i}") for i in range(2)]
        att_stored = sem("att_stored")
        st_done, mv_done, seed_done, newton_done, ctx_normed = (
            sem(n) for n in ("st_done", "mv_done", "seed_done", "newton_done", "ctx_normed"))
        piece_mm, hi_done, lo_done, v_copied = (sem(n) for n in ("piece_mm", "hi_done", "lo_done", "v_copied2"))
        v_moved = [sem(f"v_moved{i}") for i in range(2)]
        s_mm, top_done, exp_done, p_turned, p_copied_dve, p_copied_act, pv_mm = (
            sem(n) for n in ("s_mm2", "top_done2", "exp_done2", "p_turned2", "p_copied_dve", "p_copied_act", "pv_mm2"))
        recip_done, out_taken, out_turned, att_ready = (
            sem(n) for n in ("recip_done2", "out_taken", "out_turned", "att_ready2"))
        mod5_landed, cproj_landed, rstd_done = sem("mod5_landed"), sem("cproj_landed"), sem("rstd_done2")
        mod_mm, mod_added = sem("mod_mm2"), sem("mod_added2")

        def steps(eng, step, between=None):
            step(-1)
            if between:
                between()
            step(0)
            with eng.Fori(1, B - 2) as b:
                step(b)
            step(B - 2, last_ln=True)
            step(B - 1, last_ln=True, last=True)

        def own(b, last, x):
            if x in OWN:
                return not is_first(b)
            return not last

        def big_before(b, s, last):
            if s > 0:
                return [(b, x) for x in ENDS[s - 1] if x[0] != "T" and own(b, last, x)]
            return [] if is_first(b) else [(b - 1, x) for x in ENDS[NH - 1]]

        def turned_now(b, s, last):
            return [x for x in ENDS[s] if x[0] == "T" and own(b, last, x)]

        def is_first(b):
            return isinstance(b, int) and b < 0

        def is_int(b, n):
            return isinstance(b, int) and b == n

        def piece_bank(x):
            return TURNED if x[0] == "T" else PIECES + BIG.index(x) % 2

        block = ctx.enter_context(nc.Block())

        @block.sync
        def _(sp):
            def load_ctx(m, t):
                at, n = TILES[t]
                sp.dma_start(c_raw[0:n, t, :], dram["ctx"][bass.ds(m, 1), at:at + n, :].rearrange("b s d -> (b s) d")
                             ).then_inc(ctx_landed[t], 16)

            def load_q(b, half):
                hs = slice(8 * half, 8 * half + 8)
                for i, name in enumerate(("q_hi", "q_hi", "q_lo")):
                    sp.dma_start(q_stack[i * HD:(i + 1) * HD, hs, :].bitcast(F32),
                                 dram[name].rearrange("(h d) t -> d h t", d=HD)[:, hs, bass.ds(b * N, N)]
                                 ).then_inc(q_landed[half], 16)

            def stack_k(f):
                for r in range(4):
                    rows = slice(r * HD, (r + 1) * HD)
                    for i, part in enumerate((k_hi, k_lo, k_hi)):
                        sp.dma_start(k_stack[i * HD:(i + 1) * HD, 4 * f + r, 1:S + 1].bitcast(F32),
                                     part[rows, f % 2, :].bitcast(F32)).then_inc(k_landed[f], 16)

            def step(b, last_ln=False, last=False):
                first = is_first(b)
                if not first:
                    sp.wait_ge(s_mm, NH * b)
                    load_q(b, 1)
                if not last_ln:
                    for t in range(CT):
                        sp.wait_ge(ctx_normed, CT * (b + 2))
                        load_ctx(b + 2, t)
                if not first:
                    wait_apart(sp, sh.consts, lo_done, splits_done(b, "K2b"))
                    if not is_int(b, 0):
                        sp.wait_ge(s_mm, NH * b - 4)
                    stack_k(2)
                    sp.wait_ge(lo_done, splits_done(b, "K3b"))
                    stack_k(3)
                    if not is_int(b, 0):
                        sp.wait_ge(att_ready, b)
                        sp.dma_start(dram["att"][:, bass.ds(b - 1, 1), :].rearrange("p b d -> p (b d)"), att[:]
                                     ).then_inc(att_stored, 16)
                if not last:
                    if not first:
                        sp.wait_ge(s_mm, NH * b + 8)
                    load_q(b + 1, 0)
                    for f in range(2):
                        sp.wait_ge(lo_done, splits_done(b, f"K{f}b"))
                        stack_k(f)

            for t in range(CT):
                load_ctx(0, t)
            for half in "vk":
                sp.dma_start(wkv_raw[:, :, W_HALF[half]], dram["w_kvc"][:, :, W_HALF[half]]).then_inc(w_landed[half], 16)
            sp.wait_ge(mod_mm, 1)
            sp.dma_start(sh.raw[:, 0], dram["w_mod"][:, :, 5 * 512:6 * 512]).then_inc(mod5_landed, 16)
            sp.wait_ge(mod_mm, 2)
            sp.dma_start(sh.raw[:, 1], dram["w_cproj"]).then_inc(cproj_landed, 16)
            steps(sp, step)
            sp.wait_ge(att_ready, B)
            sp.dma_start(dram["att"][:, B - 1, :], att[:]).then_inc(att_stored, 16)
            sp.wait_ge(att_stored, 16 * B)
            sp.wait_ge(cproj_landed, 16)

        @block.tensor
        def _(pe):

            def bank_freed(b, x):
                if x[0] == "T":
                    if x != "T0":
                        pe.wait_ge(lo_done, splits_done(b, f"T{int(x[1]) - 1}"))
                    elif not is_first(b) and not is_int(b, 0):
                        pe.wait_ge(att_ready, b)
                    return
                at = BIG.index(x)
                if is_first(b) and at < len(OWN) + 2:
                    return
                before, its_step = BIG[at - 2], (b if at >= 2 else b - 1)
                if before[0] == "V":
                    pe.wait_ge(v_copied, vs_done(its_step, before))
                else:
                    pe.wait_ge(lo_done, splits_done(its_step, before))

            def piece(b, x):
                if x[0] == "T":
                    t = int(x[1])
                    n = TILES[t][1]
                    bank_freed(b, x)
                    pe.wait_ge(ctx_normed, CT * (b + 1) + t + 1)
                    for c in range(FC):
                        mm = pe.transpose(bank[:, TURNED, c * P:c * P + n], c_norm[0:n, t, c * P:(c + 1) * P], sh.ident[0:n, 0:n])
                elif x[0] == "V":
                    t, c = int(x[1]), int(x[2])
                    at_t, n = TILES[t]
                    out = bank[0:n, piece_bank(x[:2]), :]
                    if is_first(b) and x == "V00":
                        pe.wait_ge(w_split["v"], 1)
                    if c == 0:
                        bank_freed(b, x[:2])
                        pe.wait_ge(lo_done, splits_done(b, f"T{t}"))
                    pe.matmul(out, c_hi[:, c, at_t:at_t + n], wkv_hi[:, c, D:], start=(c == 0), stop=False)
                    pe.matmul(out, c_hi[:, c, at_t:at_t + n], wkv_lo[:, c, D:], start=False, stop=False)
                    mm = pe.matmul(out, c_lo[:, c, at_t:at_t + n], wkv_hi[:, c, D:], start=False, stop=(c == FC - 1))
                    if c < FC - 1:
                        return
                else:
                    f, half = int(x[1]), "ab".index(x[2])
                    at_k = half * (S - WIDE)
                    bank_freed(b, x)
                    if is_first(b) and x == "K0a":
                        pe.wait_ge(w_split["k"], 1)
                    if x[1] == "0":
                        pe.wait_ge(lo_done, splits_done(b, f"T{(at_k + WIDE - 1) // P}"))
                    mm = product3(pe, bank[:, piece_bank(x), 0:WIDE],
                                  lambda c: wkv_hi[:, c, f * P:(f + 1) * P], lambda c: wkv_lo[:, c, f * P:(f + 1) * P],
                                  lambda c: c_hi[:, c, at_k:at_k + WIDE], lambda c: c_lo[:, c, at_k:at_k + WIDE], FC)
                mm.then_inc(piece_mm, 1)

            def scores(b, h):
                if is_int(b, 0) and h == 0:
                    pe.wait_ge(mod_added, 3)
                    pe.wait_ge(cleared, 3)
                if h % 8 == 0:
                    pe.wait_ge(q_landed[h // 8], 48 * (b + 1))
                if h % 4 == 0:
                    pe.wait_ge(k_landed[h // 4], 192 * (b + 1))
                if not (is_int(b, 0) and h == 0):
                    pe.wait_ge(exp_done, NH * b + h)
                for half in range(2):
                    mm = pe.matmul(bank[0:N, half, 0:WIDE], q_stack[:, h, :], k_stack[:, h, half * HALF:half * HALF + WIDE],
                                   start=True, stop=True)
                mm.then_inc(s_mm, 1)

            def turn_probs(n, h):
                pe.wait_ge(exp_done, n + 1)
                if not is_int(n, 0):
                    pe.wait_ge(p_copied_dve, n)
                    pe.wait_ge(p_copied_act, n)
                for t, (at, rows) in enumerate(TILES):
                    mm = pe.transpose(bank[0:rows, PROBS_T + t // 3, (t % 3) * N:(t % 3 + 1) * N],
                                      prob[h % 2][:, at:at + rows], sh.ident[0:N, 0:N])
                mm.then_inc(p_turned, 1)

            def weigh(b, g):
                pe.wait_ge(p_copied_dve, NH * b + 4 * g + 4)
                pe.wait_ge(p_copied_act, NH * b + 4 * g + 4)
                if g % 2 == 0:
                    pe.wait_ge(v_moved[g // 2], b + 1)
                if g == 0 and not is_int(b, 0):
                    pe.wait_ge(out_taken, b)
                for t, (at, rows) in enumerate(TILES):
                    for j in range(4):
                        h = 4 * g + j
                        mm = pe.matmul(bank[j * HD:(j + 1) * HD, OUT, g * N:(g + 1) * N], v_now[0:rows, t, h * HD:(h + 1) * HD],
                                       prob_t[j][0:rows, t, :], start=(t == 0), stop=(t == CT - 1), tile_position=(0, j * HD))
                mm.then_inc(pv_mm, 1)

            def turn_out(b, t5_step):
                pe.wait_ge(out_taken, b + 1)
                pe.wait_ge(lo_done, splits_done(t5_step, "T5"))
                for f in range(FC):
                    mm = pe.transpose(bank[0:N, TURNED, f * P:(f + 1) * P], out_t[:, f, :], sh.ident)
                mm.then_inc(out_turned, 1)

            def step(b, last_ln=False, last=False):
                for s in range(NH):
                    if not is_first(b):
                        scores(b, s)
                        if s >= 1:
                            turn_probs(NH * b + s - 1, s - 1)
                        elif not is_int(b, 0):
                            turn_probs(NH * b - 1, NH - 1)
                        if s == 2 and not is_int(b, 0):
                            turn_out(b - 1, b - 1)
                    for x in SLOTS[s]:
                        if own(b, last, x):
                            piece(b, x)
                    if is_first(b):
                        continue
                    if s % 4 == 0 and s > 0:
                        weigh(b, s // 4 - 1)
                    elif s == 0 and not is_int(b, 0):
                        weigh(b - 1, 3)

            def modulation(m):
                pe.wait_ge(mod5_landed if m == 2 else sh.mod_landed[m], 16)
                for f in range(4):
                    for c in range(FC):
                        mm = pe.matmul(bank[:, MOD_BANKS[m], f * B:(f + 1) * B], sh.raw[:, m % 2, c, f * P:(f + 1) * P],
                                       sh.silu[:, c, :], start=(c == 0), stop=(c == FC - 1))
                mm.then_inc(mod_mm, 1)

            modulation(0)
            modulation(1)
            steps(pe, step, lambda: modulation(2))
            turn_probs(NH * B - 1, NH - 1)
            weigh(B - 1, 3)
            turn_out(B - 1, B - 2)

        @block.scalar
        def _(act):
            for half in "vk":
                act.wait_ge(w_landed[half], 16)
                act.activation(wkv_hi[:, :, W_HALF[half]], wkv_raw[:, :, W_HALF[half]], ACT.Copy).then_inc(w_hi_done, 1)

            def take(b, x):
                src = bank[:, piece_bank(x), :]
                act.wait_ge(piece_mm, pieces_done(b, x))
                if x[0] == "T":
                    at, n = TILES[int(x[1])]
                    act.activation(c_hi[:, :, at:at + n], src.rearrange("p (c s) -> p c s", c=FC)[:, :, 0:n],
                                   ACT.Copy).then_inc(hi_done, 1)
                elif x[0] == "V":
                    n = TILES[int(x[1])][1]
                    if x == "V0":
                        act.wait_ge(v_moved[1], b + 1)
                        act.wait_ge(v_moved[0], b + 1)
                    act.activation(v_next[0:n, int(x[1]), :], src[0:n, :], ACT.Copy).then_inc(v_copied, 1)
                else:
                    f, half = int(x[1]), "ab".index(x[2])
                    if half == 0 and not (is_first(b)) and f < 2:
                        act.wait_ge(k_landed[f + 2], 192 * (b + 1))
                    if half == 0 and f >= 2:
                        act.wait_ge(k_landed[f - 2], 192 * (b + 1))
                    act.activation(k_hi[:, f % 2, half * HALF:(half + 1) * HALF], src[:, half:half + HALF],
                                   ACT.Identity, bias=sh.b("kc", f)).then_inc(hi_done, 1)

            def soften(b, h):
                act.wait_ge(top_done, NH * b + h + 1)
                if not (is_int(b, 0) and h < 2):
                    act.wait_ge(p_turned, NH * b + h - 1)
                if h % 8 == 0 and not is_int(b, 0):
                    act.wait_ge(recip_done, 2 * b - 1 + h // 8)
                act.activation(prob[h % 2][:].rearrange("p (a k) -> p a k", a=2), bank[0:N, 0:2, 1:1 + HALF], ACT.Exp,
                               bias=neg_top[:, h:h + 1], accum_out=total[:, h:h + 1]).then_inc(exp_done, 1)

            def copy_probs(b, h):
                act.wait_ge(p_turned, NH * b + h + 1)
                if not (is_int(b, 0) and h < 4):
                    act.wait_ge(pv_mm, 4 * b + h // 4)
                act.activation(prob_t[h % 4][:, 3:6, :], bank[:, PROBS_T + 1, 0:3 * N].rearrange("p (t q) -> p t q", t=3),
                               ACT.Copy).then_inc(p_copied_act, 1)

            def step(b, last_ln=False, last=False):
                for s in range(NH):
                    for its_step, x in big_before(b, s, last):
                        take(its_step, x)
                    if not is_first(b):
                        if s >= 1:
                            copy_probs(b, s - 1)
                        elif not is_int(b, 0):
                            copy_probs(b - 1, NH - 1)
                    for x in turned_now(b, s, last):
                        take(b, x)
                    if not is_first(b):
                        soften(b, s)

            act.wait_ge(cleared, 3)
            steps(act, step)
            copy_probs(B - 1, NH - 1)

        @block.vector
        def _(dve):
            dve.memset(bank[:, PROBS_T + 1, :], 0.0).then_inc(cleared, 1)

            def ln_stats(m, t):
                n = TILES[t][1]
                dve.wait_ge(ctx_landed[t], 16 * (m + 1))
                dve.bn_stats(stats[0:n, t, :], c_raw[0:n, t, :]).then_inc(st_done, 1)

            def ln_seed(m):
                dve.wait_ge(st_done, CT * (m + 1))
                if not is_int(m, 0):
                    wait_apart(dve, sh.consts, ctx_normed, CT * m)
                for t in range(CT):
                    n = TILES[t][1]
                    dve.bn_aggr(mean_var[0:n, t, :], stats[0:n, t, :]).then_inc(mv_done, 1)
                dve.wait_ge(mv_done, CT * (m + 1))
                if is_int(m, 0):
                    rsqrt(dve, rstd_done, 0, mean_var[:], var_eps[:], half_bits[:], rstd[:], newton_work[:])
                else:
                    seed_rsqrt(dve, seed_done, SEED_STEPS * (m - 1), mean_var[:], var_eps[:], half_bits[:], rstd[:])

            def take(b, x):
                if x[0] == "V":
                    return
                src = bank[:, piece_bank(x), :]
                dve.wait_ge(hi_done, splits_done(b, x))
                if x[0] == "T":
                    at, n = TILES[int(x[1])]
                    dve.tensor_tensor(c_lo[:, :, at:at + n], src.rearrange("p (c s) -> p c s", c=FC)[:, :, 0:n],
                                      c_hi[:, :, at:at + n].bitcast(F32), ALU.subtract).then_inc(lo_done, 1)
                else:
                    f, half = int(x[1]), "ab".index(x[2])
                    sl = slice(half * HALF, (half + 1) * HALF)
                    dve.scalar_tensor_tensor(out=k_lo[:, f % 2, sl], in0=src[:, half:half + HALF], scalar=sh.b("kc", f),
                                             in1=k_hi[:, f % 2, sl].bitcast(F32), op0=ALU.add, op1=ALU.subtract
                                             ).then_inc(lo_done, 1)

            def top(b, h):
                dve.wait_ge(s_mm, NH * b + h + 1)
                dve.tensor_reduce(neg_top[:, h:h + 1], bank[0:N, 0:2, 1:1 + HALF], AX.XY, ALU.max, negate=True).then_inc(top_done, 1)

            def copy_probs(b, h):
                dve.wait_ge(p_turned, NH * b + h + 1)
                if not (is_int(b, 0) and h < 4):
                    dve.wait_ge(pv_mm, 4 * b + h // 4)
                dve.tensor_copy(prob_t[h % 4][:, 0:3, :], bank[:, PROBS_T, 0:3 * N].rearrange("p (t q) -> p t q", t=3)
                                ).then_inc(p_copied_dve, 1)

            def invert_totals(b, half):
                hs = slice(8 * half, 8 * half + 8)
                dve.wait_ge(exp_done, NH * b + 8 * half + 8)
                dve.reciprocal(recip[:, hs], total[:, hs]).then_inc(recip_done, 1)

            def take_out(b):
                dve.wait_ge(pv_mm, 4 * b + 4)
                dve.tensor_copy(out_t[:], bank[:, OUT, 0:FC * N].rearrange("p (f t) -> p f t", f=FC)).then_inc(out_taken, 1)

            def normalise(b):
                dve.wait_ge(out_turned, b + 1)
                dve.wait_ge(recip_done, 2 * b + 2)
                if not is_int(b, 0):
                    dve.wait_ge(att_stored, 16 * b)
                dve.tensor_tensor(att[:].rearrange("p (h d) -> p h d", h=NH),
                                  bank[0:N, TURNED, :].rearrange("p (h d) -> p h d", h=NH),
                                  recip[:].unsqueeze(2).to_broadcast([N, NH, HD]), ALU.mult).then_inc(att_ready, 1)

            def step(b, last_ln=False, last=False):
                for s in range(NH):
                    again = not is_first(b) and not is_int(b, 0)
                    if not is_first(b):
                        top(b, s)
                    if s == 1 and again:
                        take_out(b - 1)
                    for its_step, x in big_before(b, s, last):
                        take(its_step, x)
                    if not is_first(b):
                        if s >= 1:
                            copy_probs(b, s - 1)
                        elif again:
                            copy_probs(b - 1, NH - 1)
                    if s == 1 and again:
                        invert_totals(b - 1, 1)
                    if s == 2 and again:
                        normalise(b - 1)
                    for x in turned_now(b, s, last):
                        take(b, x)
                    if s == 9 and not is_first(b):
                        invert_totals(b, 0)
                    if not last_ln:
                        if LN_SLOT <= s < LN_SLOT + CT:
                            ln_stats(b + 2, s - LN_SLOT)
                        if s == LN_SLOT + CT:
                            ln_seed(b + 2)

            dve.wait_ge(cleared, 3)
            for t in range(CT):
                ln_stats(0, t)
            ln_seed(0)
            dve.wait_ge(rstd_done, RSQRT_STEPS)
            for t, (at, n) in enumerate(TILES):
                dve.tensor_scalar(c_norm[0:n, t, :], c_raw[0:n, t, :], mean_var[0:n, t, 0:1], rstd[0:n, t:t + 1],
                                  ALU.subtract, ALU.mult).then_inc(ctx_normed, 1)
            dve.wait_ge(w_hi_done, 1)
            dve.tensor_tensor(wkv_lo[:, :, W_HALF["v"]], wkv_raw[:, :, W_HALF["v"]], wkv_hi[:, :, W_HALF["v"]].bitcast(F32),
                              ALU.subtract).then_inc(w_split["v"], 1)

            def add_mod_bias():
                for m in range(3):
                    dve.wait_ge(mod_mm, m + 1)
                    dve.tensor_tensor(sh.mod[:, 12 + 4 * m:16 + 4 * m, :],
                                      bank[:, MOD_BANKS[m], 0:4 * B].rearrange("p (f b) -> p f b", f=4),
                                      sh.bias[:, 12 + 4 * m:16 + 4 * m].unsqueeze(2).to_broadcast([P, 4, B]),
                                      ALU.add).then_inc(mod_added, 1)
                dve.wait_ge(mod_added, 3)
                dve.tensor_scalar(sh.mod[:, 16:20, :], sh.mod[:, 16:20, :], 1.0, None, ALU.add)
                dve.tensor_tensor(sh.gate_bias[:, 4:8, :], sh.mod[:, 20:24, :],
                                  sh.bias[:, BIAS_OF["mlp2"]].unsqueeze(2).to_broadcast([P, 4, B]), ALU.mult)

            steps(dve, step, add_mod_bias)
            copy_probs(B - 1, NH - 1)
            invert_totals(B - 1, 1)
            take_out(B - 1)
            normalise(B - 1)

        @block.gpsimd
        def _(pool):
            pool.memset(k_stack[:, :, 0:1].bitcast(F32), 0.0)
            pool.memset(mean_var[:, CT - 1, :], 1.0).then_inc(cleared, 1)
            pool.memset(v_next[:, CT - 1, :], 0.0).then_inc(cleared, 1)

            def normalise_ctx(m):
                wait_apart(pool, sh.consts, seed_done, SEED_STEPS * m)
                newton_rsqrt(pool, sh.consts, newton_done, NEWTON_STEPS * (m - 1), mean_var[:], var_eps[:], rstd[:],
                             newton_work[:], neg_mean[:])
                pool.wait_ge(newton_done, NEWTON_STEPS * m)
                for t, (at, n) in enumerate(TILES):
                    if not is_int(m, 0):
                        wait_apart(pool, sh.consts, piece_mm, pieces_done(m - 2, f"T{t}"))
                    pool.tensor_scalar(c_norm[0:n, t, :], c_raw[0:n, t, :], neg_mean[0:n, t:t + 1], rstd[0:n, t:t + 1],
                                       ALU.add, ALU.mult).then_inc(ctx_normed, 1)

            def move_v(b, half):
                pool.wait_ge(v_copied, CT * (b + 1))
                if not is_int(b, 0):
                    wait_apart(pool, sh.consts, pv_mm, 4 * (b - 1) + 2 * half + 2)
                pool.tensor_copy(v_now[:, :, 256 * half:256 * half + 256], v_next[:, :, 256 * half:256 * half + 256]
                                 ).then_inc(v_moved[half], 1)

            def step(b, last_ln=False, last=False):
                if not is_first(b):
                    move_v(b, 1)
                if not last_ln:
                    normalise_ctx(b + 2)
                if not last:
                    move_v(b + 1, 0)

            pool.wait_ge(w_hi_done, 2)
            pool.tensor_tensor(wkv_lo[:, :, W_HALF["k"]], wkv_raw[:, :, W_HALF["k"]], wkv_hi[:, :, W_HALF["k"]].bitcast(F32),
                               ALU.subtract).then_inc(w_split["k"], 1)
            steps(pool, step)


def mlp_stage(nc, sh, dram):
    GJ = GROUP_BATCHES
    PAIRS = GROUPS // 2
    HB = 2
    AHEAD = 4
    quarters = [("w_mlp1", q) for q in range(4)] + [("w_mlp2", q) for q in (3, 2, 1, 0)]
    with ExitStack() as ctx:
        def sb(name, shape, dt=F32):
            return ctx.enter_context(nc.sbuf_tensor(name, shape, dt))

        def sem(name):
            return ctx.enter_context(nc.semaphore(name))

        bank = ctx.enter_context(nc.psum_tensor("bank3", [P, 8, 512], F32))
        wc_hi, wc_lo = sb("wc_hi", [P, FC, D], F32R), sb("wc_lo", [P, FC, D], F32R)
        w1_hi = sb("w1_hi", [P, FC, MLP], F32R)
        with ExitStack() as place:
            w1_raw = place.enter_context(nc.sbuf_tensor("w1_raw", [P, FC, MLP], F32))
        w1_lo = sb("w1_lo", [P, FC, MLP], F32R)
        a_tok = [sb("a_tok", [N, GJ, D])[:]]
        a_hi, a_lo = [sb("a_hi3", [P, FC, GT], F32R)[:]], [sb("a_lo3", [P, FC, GT], F32R)[:]]
        xt, xm = [sb("xt3", [P, FC, GT])[:]], [sb("xm3", [P, FC, GT])[:]]
        with ExitStack() as place:
            def early(name, shape, dt=F32):
                return place.enter_context(nc.sbuf_tensor(name, shape, dt))[:]

            xm.append(early("xm3_1", [P, FC, GT]))
            a_tok.append(early("a_tok_1", [N, GJ, D]))
            xt.append(early("xt3_1", [P, FC, GT]))
            early("gap", [P, MC * D - GJ * D - 2 * FC * GT])
            a_hi.append(early("a_hi3_1", [P, FC, GT], F32R))
            a_lo.append(early("a_lo3_1", [P, FC, GT], F32R))
        w2_hi = sb("w2_hi", [P, MC, D], F32R)
        with ExitStack() as place:
            w2_raw = place.enter_context(nc.sbuf_tensor("w2_raw", [P, MC, D], F32))
        w2_lo = sb("w2_lo", [P, MC, D], F32R)
        m_raw = [sh.raw[:, i, :, 0:GT] for i in range(2)]
        m_hi, m_lo = [wc_hi[:, :, 0:GT], a_hi[0]], [wc_lo[:, :, 0:GT], a_lo[0]]
        hidden_raw, gated = xm[0][:, 0:HB, :], xm[0][:, HB:FC, :]
        h_hi = [sb(f"h_hi{i}", [P, GT], F32R) for i in range(HB)]
        h_lo = [sb(f"h_lo{i}", [P, GT], F32R) for i in range(HB)]
        gp = sb("gp3", [P, 2, 8, GJ])
        gp2 = sb("gp3_gate", [P, 8, GJ])
        stats, mean_var = sb("stats3", [N, 2, GJ, 6]), sb("mean_var3", [N, 2, GJ, 2])
        var_eps, half_bits = sb("var_eps3", [N, 2, GJ]), sb("half_bits3", [N, 2, GJ], I32)
        rstd, newton_work = sb("rstd3", [N, 2, GJ]), sb("newton_work3", [N, GJ])

        w1_landed = [sem(f"w1_landed{i}") for i in range(2)]
        w2_landed = [sem(f"w2_landed{i}") for i in range(4)]
        w_hi_done, w_lo_done, c_hi_done, c_split, gp_ready = (
            sem(n) for n in ("w_hi_done3", "w_lo_done3", "c_hi_done3", "c_split", "gp_ready3"))
        a_landed, x1_landed = ([sem(f"{n}{i}") for i in range(2)] for n in ("a_landed", "x1_landed"))
        x2_stored, xm_stored = ([sem(f"{n}{i}") for i in range(2)] for n in ("x2_stored", "xm_stored"))
        a_added = sem("a_added")
        a_turned, a_split, c_mm, x2_ready, x2_turned = (sem(n) for n in ("a_turned", "a_split", "c_mm", "x2_ready", "x2_turned"))
        st_done, mv_done, rstd_done, normed = (sem(n) for n in ("st_done3", "mv_done3", "rstd_done3", "normed3"))
        xn_back, xm_ready, m_split = sem("xn_back3"), sem("xm_ready3"), sem("m_split")
        m_landed, x2_landed, out_stored = [sem(f"m_landed{i}") for i in range(2)], sem("x2_landed"), sem("out_stored")
        h_mm, gelu_done, h_split, y_mm, gated_done, y_ready = (
            sem(n) for n in ("h_mm", "gelu_done", "h_split", "y_mm", "gated_done3", "y_ready"))
        gp2_ready = sem("gp2_ready")

        def quarter(k):
            name, q = quarters[k]
            if name == "w_mlp1":
                return (w[:, :, q * 512:(q + 1) * 512] for w in (w1_raw, w1_hi, w1_lo))
            return (w[:, 4 * q:4 * q + 4, :] for w in (w2_raw, w2_hi, w2_lo))

        block = ctx.enter_context(nc.Block())

        @block.sync
        def _(sp):
            def load_quarter(k):
                name, q = quarters[k]
                raw, _, _ = quarter(k)
                if name == "w_mlp1":
                    if k >= 2:
                        sp.wait_ge(w_hi_done, k - 1)
                    sp.dma_start(raw, dram[name][:, :, q * 512:(q + 1) * 512]
                                 ).then_inc(w1_landed[k % 2], 16)
                else:
                    sp.dma_start(raw, dram[name][:, 4 * q:4 * q + 4, :]).then_inc(w2_landed[k - 4], 16)

            def load_mlp_input(g):
                if g >= 2:
                    sp.wait_ge(m_split, 2 * FC * (g - 1))
                else:
                    sp.wait_ge(xm_stored[g], 16)
                    sp.wait_ge(c_split, 1)
                if g == 3:
                    sp.wait_ge(xm_stored[1], 32)
                elif g == 2:
                    sp.wait_ge(xm_stored[0], 32)
                sp.dma_start(m_raw[g % 2], dram["xm"][:, :, g * GT:(g + 1) * GT]).then_inc(m_landed[g % 2], 16)

            def load_attention(g):
                sp.dma_start(a_tok[g % 2], dram["att"][:, g * GJ:(g + 1) * GJ, :]).then_inc(a_landed[g % 2], 16)

            def load_residual(g):
                sp.dma_start(xt[g % 2], dram["x1"][:, :, g * GT:(g + 1) * GT]).then_inc(x1_landed[g % 2], 16)

            def store_mlp_input(g):
                sp.wait_ge(xm_ready, GJ * g + GJ)
                sp.dma_start(dram["xm"][:, :, g * GT:(g + 1) * GT], xm[g % 2]).then_inc(xm_stored[g % 2], 16)

            load_attention(0)
            load_attention(1)
            load_residual(0)
            load_residual(1)
            for k in range(4):
                load_quarter(k)
            for g in range(2, GROUPS):
                sp.wait_ge(xn_back, GJ * (g - 1))
                load_attention(g)
                store_mlp_input(g - 2)
                sp.wait_ge(x2_stored[g % 2], 16 * (g // 2))
                load_residual(g)
            load_quarter(4)
            load_quarter(5)
            sp.wait_ge(c_mm, FC * GROUPS)
            load_quarter(6)
            load_quarter(7)
            load_mlp_input(0)
            load_mlp_input(1)
            for g in range(GROUPS - 2, GROUPS):
                store_mlp_input(g)
            for i in range(2):
                sp.wait_ge(x2_stored[i], 16 * PAIRS)
            sp.wait_ge(x2_turned, GJ * GROUPS)
            for g in range(GROUPS):
                if 2 <= g + 1 < GROUPS:
                    load_mlp_input(g + 1)
                if g >= 1:
                    sp.wait_ge(out_stored, 16 * g)
                sp.dma_start(xt[0], dram["x2"][:, :, g * GT:(g + 1) * GT]).then_inc(x2_landed, 16)
                sp.wait_ge(y_ready, FC * g + FC)
                sp.dma_start(dram["out"][:, :, g * GT:(g + 1) * GT], xt[0]).then_inc(out_stored, 16)
            sp.wait_ge(out_stored, 16 * GROUPS)

        @block.tensor
        def _(pe):
            pe.wait_ge(c_split, 1)
            with pe.Fori(0, PAIRS) as p:
                def turn_attention(i):
                    g = 2 * p + i
                    for j in range(GJ):
                        if j == 0:
                            pe.wait_ge(a_landed[i], 16 * p + 16)
                            pe.wait_ge(normed, 2 * GJ * p)
                            pe.wait_ge(xm_ready, 2 * GJ * p)
                        if j >= 2:
                            pe.wait_ge(a_added, GJ * g + j - 1)
                        for f in range(FC):
                            mm = pe.transpose(bank[:, 4 * i + j % 2, f * N:(f + 1) * N], a_tok[i][:, j, f * P:(f + 1) * P],
                                              sh.ident[0:N, 0:N])
                        mm.then_inc(a_turned, 1)

                def project(i, fs):
                    g = 2 * p + i
                    for f in fs:
                        if f == 0:
                            pe.wait_ge(a_split, 2 * GJ * g + 2 * GJ)
                            pe.wait_ge(a_added, GJ * g + GJ)
                        product3(pe, bank[:, 4 * i + f, 0:GT],
                                 lambda c: wc_hi[:, c, f * P:(f + 1) * P], lambda c: wc_lo[:, c, f * P:(f + 1) * P],
                                 lambda c: a_hi[i][:, c, :], lambda c: a_lo[i][:, c, :], FC).then_inc(c_mm, 1)

                def turn_x2(i):
                    g = 2 * p + i
                    for j in range(GJ):
                        if j == 0:
                            pe.wait_ge(x2_ready, FC * g + FC)
                        for f in range(FC):
                            mm = pe.transpose(bank[0:N, 4 * i + j, f * P:(f + 1) * P], xt[i][:, f, j * N:(j + 1) * N], sh.ident)
                        mm.then_inc(x2_turned, 1)

                def turn_back(i):
                    g = 2 * p + i
                    for j in range(GJ):
                        if j == 0:
                            pe.wait_ge(normed, GJ * g + GJ)
                        if j >= 2:
                            pe.wait_ge(xm_ready, GJ * g + j - 1)
                        for f in range(FC):
                            mm = pe.transpose(bank[:, 4 * i + 2 + j % 2, f * N:(f + 1) * N], a_tok[i][:, j, f * P:(f + 1) * P],
                                              sh.ident[0:N, 0:N])
                        mm.then_inc(xn_back, 1)

                turn_attention(0)
                turn_attention(1)
                project(0, range(FC))
                project(1, (0, 1))
                turn_x2(0)
                project(1, (2, 3))
                turn_x2(1)
                turn_back(0)
                turn_back(1)
            pe.wait_ge(w_lo_done, 4)
            pe.wait_ge(normed, GJ * GROUPS)
            pe.wait_ge(xm_ready, GJ * GROUPS)
            with pe.Fori(0, PAIRS) as p:
                for i in range(2):
                    g = 2 * p + i

                    def hidden(c):
                        if c == 0:
                            pe.wait_ge(m_split, 2 * FC * (g + 1))
                            pe.wait_ge(gelu_done, MC * g)
                        if c >= 4:
                            pe.wait_ge(gelu_done, MC * g + c - 3)
                        product3(pe, bank[:, 4 + c % 4, 0:GT],
                                 lambda k: w1_hi[:, k, c * P:(c + 1) * P], lambda k: w1_lo[:, k, c * P:(c + 1) * P],
                                 lambda k: m_hi[i][:, k, :], lambda k: m_lo[i][:, k, :], FC).then_inc(h_mm, 1)

                    def output(c):
                        pe.wait_ge(h_split, 2 * MC * g + 2 * c + 2)
                        if c == 0:
                            pe.wait_ge(w_lo_done, len(quarters))
                            pe.wait_ge(gated_done, FC * g)
                        for f in range(FC):
                            out = bank[:, f, 0:GT]
                            fs = slice(f * P, (f + 1) * P)
                            pe.matmul(out, w2_hi[:, c, fs], h_hi[c % HB][:], start=(c == 0), stop=False)
                            pe.matmul(out, w2_lo[:, c, fs], h_hi[c % HB][:], start=False, stop=False)
                            mm = pe.matmul(out, w2_hi[:, c, fs], h_lo[c % HB][:], start=False, stop=(c == MC - 1))
                        mm.then_inc(y_mm, 1)

                    for c in range(AHEAD):
                        hidden(c)
                    for c in range(MC):
                        output(c)
                        if c + AHEAD < MC:
                            hidden(c + AHEAD)

        @block.scalar
        def _(act):
            act.activation(wc_hi[:], sh.raw[:, 1], ACT.Copy).then_inc(c_hi_done, 1)
            with act.Fori(0, PAIRS) as p:
                for i in range(2):
                    g = 2 * p + i
                    for j in range(GJ):
                        act.wait_ge(a_turned, GJ * g + j + 1)
                        if j == 0:
                            act.wait_ge(xm_stored[i], 16 * p)
                        for f in range(FC):
                            last = act.activation(xm[i][:, f, j * N:(j + 1) * N], bank[:, 4 * i + j % 2, f * N:(f + 1) * N],
                                                  ACT.Identity, bias=sh.b("vc", f))
                        last.then_inc(a_added, 1)
                for q in range(2):
                    qs = bass.ds((2 * p + q) * 512, 512)
                    act.wait_ge(w1_landed[q], 16 * p + 16)
                    act.activation(w1_hi[:, :, qs], w1_raw[:, :, qs], ACT.Copy).then_inc(w_hi_done, 1)
                for i in range(2):
                    g = 2 * p + i
                    for j in range(GJ):
                        act.wait_ge(xn_back, GJ * g + j + 1)
                        if j == 0:
                            act.wait_ge(gp_ready, 2 * p + 2)
                            act.wait_ge(a_split, 2 * GJ * (g + 1))
                        for f in range(FC):
                            last = act.activation(xm[i][:, f, j * N:(j + 1) * N], bank[:, 4 * i + 2 + j % 2, f * N:(f + 1) * N],
                                                  ACT.Identity, bias=gp[:, i, f, j:j + 1], scale=gp[:, i, 4 + f, j:j + 1])
                        last.then_inc(xm_ready, 1)
            for k in range(4, 8):
                act.wait_ge(w2_landed[k - 4], 16)
                if k == 5:
                    act.wait_ge(x2_stored[1], 16 * PAIRS)
                if k == 7:
                    act.wait_ge(xm_stored[1], 16 * PAIRS)
                raw, hi, _ = quarter(k)
                act.activation(hi, raw, ACT.Copy).then_inc(w_hi_done, 1)
            act.wait_ge(xm_stored[0], 16 * PAIRS)
            with act.Fori(0, PAIRS) as p:
                for i in range(2):
                    g = 2 * p + i
                    for c in range(MC):
                        act.wait_ge(h_mm, MC * g + c + 1)
                        if c >= HB:
                            act.wait_ge(h_split, 2 * MC * g + 2 * (c - HB) + 2)
                        elif c == 0:
                            act.wait_ge(h_split, 2 * MC * g)
                        act.activation(hidden_raw[:, c % HB, :], bank[:, 4 + c % 4, 0:GT], ACT.Gelu_apprx_tanh,
                                       bias=sh.b("mlp1", c)).then_inc(gelu_done, 1)
                    act.wait_ge(y_mm, MC * g + MC)
                    act.wait_ge(gp2_ready, 2 * g + 2)
                    for f in range(FC):
                        act.wait_ge(y_ready, FC * g + (f - 1 if f >= 2 else 0))
                        for j in range(GJ):
                            last = act.activation(gated[:, f % 2, j * N:(j + 1) * N], bank[:, f, j * N:(j + 1) * N],
                                                  ACT.Identity, bias=gp2[:, 4 + f, j:j + 1], scale=gp2[:, f, j:j + 1])
                        last.then_inc(gated_done, 1)

        @block.vector
        def _(dve):
            dve.wait_ge(c_hi_done, 1)
            dve.tensor_tensor(wc_lo[:], sh.raw[:, 1], wc_hi[:].bitcast(F32), ALU.subtract).then_inc(c_split, 1)
            with dve.Fori(0, PAIRS) as p:
                for i in range(2):
                    g = 2 * p + i
                    for j in range(GJ):
                        sl = slice(j * N, (j + 1) * N)
                        dve.wait_ge(a_added, GJ * g + j + 1)
                        if j == 0:
                            dve.wait_ge(c_mm, 2 * FC * p)
                        dve.tensor_copy(a_hi[i][:, :, sl], xm[i][:, :, sl]).then_inc(a_split, 1)
                        dve.wait_ge(a_split, 2 * GJ * g + 2 * j + 1)
                        dve.tensor_tensor(a_lo[i][:, :, sl], xm[i][:, :, sl], a_hi[i][:, :, sl].bitcast(F32),
                                          ALU.subtract).then_inc(a_split, 1)

                def add_x1(i):
                    g = 2 * p + i
                    for f in range(FC):
                        dve.wait_ge(c_mm, FC * g + f + 1)
                        if f == 0:
                            dve.wait_ge(x1_landed[i], 16 * p + 16)
                        dve.scalar_tensor_tensor(out=xt[i][:, f, :], in0=bank[:, 4 * i + f, 0:GT], scalar=sh.b("cproj", f),
                                                 in1=xt[i][:, f, :], op0=ALU.add, op1=ALU.add).then_inc(x2_ready, 1)

                def rstd_of_x2(i):
                    g = 2 * p + i
                    for j in range(GJ):
                        dve.wait_ge(x2_turned, GJ * g + j + 1)
                        dve.bn_stats(stats[:, i, j, :], bank[0:N, 4 * i + j, :]).then_inc(st_done, 1)
                    wait_apart(dve, sh.consts, st_done, GJ * g + GJ)
                    for j in range(GJ):
                        dve.bn_aggr(mean_var[:, i, j, :], stats[:, i, j, :]).then_inc(mv_done, 1)
                    dve.wait_ge(mv_done, GJ * g + GJ)
                    rsqrt(dve, rstd_done, RSQRT_STEPS * g, mean_var[:, i], var_eps[:, i], half_bits[:, i], rstd[:, i],
                          newton_work[:])

                def normalise_x2(i):
                    g = 2 * p + i
                    dve.wait_ge(rstd_done, RSQRT_STEPS * g + RSQRT_STEPS)
                    for j in range(GJ):
                        dve.wait_ge(a_turned, GJ * g + GJ)
                        dve.tensor_scalar(a_tok[i][:, j, :], bank[0:N, 4 * i + j, :], mean_var[:, i, j, 0:1], rstd[:, i, j:j + 1],
                                          ALU.subtract, ALU.mult).then_inc(normed, 1)

                add_x1(0)
                rstd_of_x2(0)
                add_x1(1)
                normalise_x2(0)
                rstd_of_x2(1)
                normalise_x2(1)
                for q in range(2):
                    qs = bass.ds((2 * p + q) * 512, 512)
                    dve.wait_ge(w_hi_done, 2 * p + q + 1)
                    dve.tensor_tensor(w1_lo[:, :, qs], w1_raw[:, :, qs], w1_hi[:, :, qs].bitcast(F32),
                                      ALU.subtract).then_inc(w_lo_done, 1)

            def split_input(g, i, loads):
                for f in range(FC):
                    if f == 0:
                        dve.wait_ge(m_landed[i], 16 * loads)
                        if not (isinstance(g, int) and g == 0):
                            dve.wait_ge(h_mm, MC * (g - 1))
                    dve.tensor_copy(m_hi[i][:, f, :], m_raw[i][:, f, :]).then_inc(m_split, 1)
                    dve.wait_ge(m_split, 2 * FC * g + 2 * f + 1)
                    dve.tensor_tensor(m_lo[i][:, f, :], m_raw[i][:, f, :], m_hi[i][:, f, :].bitcast(F32),
                                      ALU.subtract).then_inc(m_split, 1)

            dve.wait_ge(c_mm, FC * GROUPS)
            split_input(0, 0, 1)
            for k in range(4, 8):
                raw, hi, lo = quarter(k)
                dve.wait_ge(w_hi_done, k + 1)
                dve.tensor_tensor(lo, raw, hi.bitcast(F32), ALU.subtract).then_inc(w_lo_done, 1)

            def mlp_pair(p, last=False):
                for i in range(2):
                    g = 2 * p + i
                    for c in range(MC):
                        dve.wait_ge(gelu_done, MC * g + c + 1)
                        if c >= HB:
                            dve.wait_ge(y_mm, MC * g + c - HB + 1)
                        elif c == 0:
                            dve.wait_ge(y_mm, MC * g)
                        dve.tensor_copy(h_hi[c % HB][:], hidden_raw[:, c % HB, :]).then_inc(h_split, 1)
                        dve.wait_ge(h_split, 2 * MC * g + 2 * c + 1)
                        dve.tensor_tensor(h_lo[c % HB][:], hidden_raw[:, c % HB, :], h_hi[c % HB][:].bitcast(F32),
                                          ALU.subtract).then_inc(h_split, 1)
                        if c == MC // 2 and not (last and i == 1):
                            split_input(g + 1, (i + 1) % 2, p + 1 + i)
                    for f in range(FC):
                        if f == 0:
                            dve.wait_ge(x2_landed, 16 * g + 16)
                        dve.wait_ge(gated_done, FC * g + f + 1)
                        dve.tensor_tensor(xt[0][:, f, :], xt[0][:, f, :], gated[:, f % 2, :], ALU.add).then_inc(y_ready, 1)

            with dve.Fori(0, PAIRS - 1) as p:
                mlp_pair(p)
            mlp_pair(PAIRS - 1, last=True)

        @block.gpsimd
        def _(pool):
            with pool.Fori(0, PAIRS) as p:
                wait_apart(pool, sh.consts, xm_ready, 2 * GJ * p)
                for i in range(2):
                    pool.tensor_copy(gp[:, i], sh.mod[:, 12:20, bass.ds((2 * p + i) * GJ, GJ)]).then_inc(gp_ready, 1)
                for i in range(2):
                    g = 2 * p + i
                    wait_apart(pool, sh.consts, x2_ready, FC * g + FC)
                    pool.dma_start(dram["x2"][:, :, bass.ds(g * GT, GT)], xt[i]).then_inc(x2_stored[i], 16)
            with pool.Fori(0, GROUPS) as g:
                wait_apart(pool, sh.consts, gated_done, FC * g)
                pool.tensor_copy(gp2[:, 0:4, :], sh.mod[:, 20:24, bass.ds(g * GJ, GJ)]).then_inc(gp2_ready, 1)
                pool.tensor_copy(gp2[:, 4:8, :], sh.gate_bias[:, 4:8, bass.ds(g * GJ, GJ)]).then_inc(gp2_ready, 1)


def build(nc, x_tok, x_t, ctx_tok, cond_t, bias_cols, ident, w_mod, w_qkv, w_proj, w_qc, w_kvc, w_cproj, w_mlp1, w_mlp2, out):
    dram = {"x_tok": x_tok, "x_t": x_t, "ctx": ctx_tok, "cond_t": cond_t, "bias_cols": bias_cols, "ident": ident,
            "w_mod": w_mod, "w_qkv": w_qkv, "w_proj": w_proj, "w_qc": w_qc, "w_kvc": w_kvc, "w_cproj": w_cproj,
            "w_mlp1": w_mlp1, "w_mlp2": w_mlp2, "out": out}
    dram["x1"] = nc.dram_tensor("scratch_x1", (P, FC, B * N), F32, kind="Internal").ap()
    dram["q_hi"] = nc.dram_tensor("scratch_q_hi", (D, B * N), F32, kind="Internal").ap()
    dram["q_lo"] = nc.dram_tensor("scratch_q_lo", (D, B * N), F32, kind="Internal").ap()
    dram["att"] = nc.dram_tensor("scratch_att", (N, B, D), F32, kind="Internal").ap()
    for name in ("x2", "xm"):
        dram[name] = nc.dram_tensor("scratch_" + name, (P, FC, B * N), F32, kind="Internal").ap()
    with ExitStack() as ctx:
        sh = Shared(nc, ctx)
        self_attention_stage(nc, sh, dram)
        cross_attention_stage(nc, sh, dram)
        mlp_stage(nc, sh, dram)


_INS = ["x_tok", "x_t", "ctx_tok", "cond_t", "bias_cols", "ident", "w_mod", "w_qkv", "w_proj", "w_qc", "w_kvc",
        "w_cproj", "w_mlp1", "w_mlp2"]


def kernel(x, cond_1024, ctx_1024, L0_xcond_W_mod, L0_xcond_b_mod, L0_xcond_W_qkv, L0_xcond_b_qkv,
           L0_xcond_W_proj, L0_xcond_b_proj, L0_xcond_W_qc, L0_xcond_b_qc, L0_xcond_W_kvc, L0_xcond_b_kvc,
           L0_xcond_W_cproj, L0_xcond_b_cproj, L0_xcond_W_mlp1, L0_xcond_b_mlp1, L0_xcond_W_mlp2,
           L0_xcond_b_mlp2):
    import numpy as _np
    import concourse.bacc as _bacc
    from concourse import mybir as _mybir
    from concourse.bass_utils import run_bass_kernel_spmd as _run

    def chunked(w):
        return _np.ascontiguousarray(_np.asarray(w).reshape(-1, 128, w.shape[1]).transpose(1, 0, 2))

    x = _np.asarray(x)
    biases = [L0_xcond_b_mod, L0_xcond_b_qkv, L0_xcond_b_proj, L0_xcond_b_qc, L0_xcond_b_kvc,
              L0_xcond_b_cproj, L0_xcond_b_mlp1, L0_xcond_b_mlp2]
    laid = {
        "x_tok": _np.ascontiguousarray(x.transpose(1, 0, 2)),
        "x_t": chunked(x.reshape(-1, x.shape[2]).T),
        "ctx_tok": _np.ascontiguousarray(ctx_1024),
        "cond_t": chunked(_np.asarray(cond_1024).T),
        "bias_cols": _np.ascontiguousarray(_np.concatenate([_np.asarray(b) for b in biases]).reshape(-1, 128).T),
        "ident": _np.eye(128, dtype=_np.float32),
        "w_mod": chunked(L0_xcond_W_mod), "w_qkv": chunked(L0_xcond_W_qkv), "w_proj": chunked(L0_xcond_W_proj),
        "w_qc": chunked(L0_xcond_W_qc), "w_kvc": chunked(L0_xcond_W_kvc), "w_cproj": chunked(L0_xcond_W_cproj),
        "w_mlp1": chunked(L0_xcond_W_mlp1), "w_mlp2": chunked(L0_xcond_W_mlp2),
    }
    nc = _bacc.Bacc("TRN2", target_bir_lowering=False, num_devices=1)
    arrays, args = {}, []
    for name in _INS:
        a = laid[name]
        arrays[f"in_{name}_dram"] = a
        args.append(nc.dram_tensor(f"in_{name}_dram", a.shape, _mybir.dt.from_np(a.dtype), kind="ExternalInput").ap())
    args.append(nc.dram_tensor("out_0_dram", (P, FC, B * N), _mybir.dt.float32, kind="ExternalOutput").ap())
    build(nc, *args)
    r = _run(nc, [arrays], core_ids=[0])
    got = _np.asarray(r.results[0]["out_0_dram"])
    return _np.ascontiguousarray(got.transpose(2, 1, 0).reshape(B, N, D))
```
